# Optimizing a Trainium2 kernel written in Bass

```python
import numpy as np
import jax
import jax.numpy as jnp

def _softmax(x, axis=-1):
    return jax.nn.softmax(x, axis=axis)

def _gelu(x):
    return jax.nn.gelu(x, approximate=True)

def _silu(x):
    return jax.nn.silu(x)

def _sigmoid(x):
    return jax.nn.sigmoid(x)

def _layernorm(x, axis=-1, eps=1e-05):
    m = jnp.mean(x, axis=axis, keepdims=True)
    v = jnp.var(x, axis=axis, keepdims=True)
    return (x - m) / jnp.sqrt(v + eps)

def _scatter_add(tgt, idx, src, axis=0):
    return tgt.at[idx].add(src)

def _segment_sum(src, seg, n):
    return jax.ops.segment_sum(src, seg, n)
kernel_name = 'mk_xattn_ffn_d2_seqx_r8_25041c'

def setup_inputs(seed: int=0):
    np.random.seed(seed)
    _w = jnp.asarray

    def _rec_inputs():
        import jax
        import jax.numpy as jnp
        _rk = jax.random.key(seed)
        x = -0.0002928 + 1 * jax.random.normal(jax.random.fold_in(_rk, 1), (2, 512, 128), jnp.float32)
        _lenS = 512 - jax.random.randint(jax.random.fold_in(_rk, 7), (2,), 0, max(1, 512 // 4) + 1, jnp.int32)
        _lenS2 = 154 - jax.random.randint(jax.random.fold_in(_rk, 8), (2,), 0, max(1, 154 // 4) + 1, jnp.int32)
        _ctx_1024P = jax.random.normal(jax.random.fold_in(_rk, 11), (2, 16, 128), jnp.float32)
        _ctx_1024c = jax.random.dirichlet(jax.random.fold_in(_rk, 511), 0.3 * jnp.ones((16,), jnp.float32), (2, 154))
        _ctx_1024t = jnp.einsum('bsk,bkd->bsd', _ctx_1024c, _ctx_1024P)
        _ctx_1024t = _ctx_1024t * jax.lax.rsqrt(jnp.mean(jnp.square(_ctx_1024t)) + 1e-12) * 0.953939
        ctx_1024 = -1.39393e-06 + 0.999914 * (_ctx_1024t + 0.3 * jax.random.normal(jax.random.fold_in(_rk, 611), (2, 154, 128), jnp.float32))
        _validS = jnp.arange(512)[None, :] < _lenS[:, None]
        _validS2 = jnp.arange(154)[None, :] < _lenS2[:, None]
        _causal = jnp.tril(jnp.ones((512, 512), dtype=bool))
        mask_BxSxS2_bk0 = jnp.logical_not(jnp.broadcast_to(_validS2[:, None, :], (2, 512, 154)))
        return (x, ctx_1024, mask_BxSxS2_bk0)
    x, ctx_1024, mask_BxSxS2_bk0 = _rec_inputs()

    def _L0_xattn_setup():
        import jax, jax.numpy as jnp
        import numpy as np
        EMBED_DIM = 128
        NUM_HEADS = 16
        HEAD_DIM = EMBED_DIM // NUM_HEADS
        B, T_Q, T_K = (2, 256, 256)
        key = jax.random.key(seed)
        ks = jax.random.split(key, 11)
        s = 1.0 / np.sqrt(EMBED_DIM)
        return {'query': jax.random.normal(ks[0], (B, T_Q, EMBED_DIM), jnp.float32), 'key': jax.random.normal(ks[1], (B, T_K, EMBED_DIM), jnp.float32), 'value': jax.random.normal(ks[2], (B, T_K, EMBED_DIM), jnp.float32), 'Wq': jax.random.normal(ks[3], (EMBED_DIM, EMBED_DIM), jnp.float32) * s, 'bq': jnp.zeros((EMBED_DIM,), jnp.float32), 'Wk': jax.random.normal(ks[4], (EMBED_DIM, EMBED_DIM), jnp.float32) * s, 'bk': jnp.zeros((EMBED_DIM,), jnp.float32), 'Wv': jax.random.normal(ks[5], (EMBED_DIM, EMBED_DIM), jnp.float32) * s, 'bv': jnp.zeros((EMBED_DIM,), jnp.float32), 'Wo': jax.random.normal(ks[6], (EMBED_DIM, EMBED_DIM), jnp.float32) * s, 'bo': jnp.zeros((EMBED_DIM,), jnp.float32)}
    _L0_xattn_all = _L0_xattn_setup()
    _L0_xattn_in = {k: v for k, v in _L0_xattn_all.items() if k in ('Wq', 'bq', 'Wk', 'bk', 'Wv', 'bv', 'Wo', 'bo')}
    del _L0_xattn_all

    def _L0_ffn_setup():
        import jax, jax.numpy as jnp
        import numpy as np
        B, S, D = (4, 512, 128)
        DD = 4 * D
        N_EXPERTS = 8
        CAPACITY = 1.0
        LN_EPS = 1e-05
        key = jax.random.key(seed)
        ks = jax.random.split(key, 8)
        s1 = 1.0 / np.sqrt(D)
        s2 = 1.0 / np.sqrt(DD)
        return {'x': jax.random.normal(ks[0], (B, S, D), jnp.float32), 'gate_w': jax.random.normal(ks[1], (N_EXPERTS, D), jnp.float32) * 0.02, 'ln_w': jnp.ones((D,), jnp.float32), 'ln_b': jnp.zeros((D,), jnp.float32), 'fc1s': jax.random.normal(ks[2], (N_EXPERTS, DD, D), jnp.float32) * s1, 'b1s': jax.random.normal(ks[3], (N_EXPERTS, DD), jnp.float32) * s1, 'fc2s': jax.random.normal(ks[4], (N_EXPERTS, D, DD), jnp.float32) * s2, 'b2s': jax.random.normal(ks[5], (N_EXPERTS, D), jnp.float32) * s2}
    _L0_ffn_all = _L0_ffn_setup()
    _L0_ffn_in = {k: v for k, v in _L0_ffn_all.items() if k in ('gate_w', 'ln_w', 'ln_b', 'fc1s', 'b1s', 'fc2s', 'b2s')}
    del _L0_ffn_all

    def _L1_xattn_setup():
        import jax, jax.numpy as jnp
        import numpy as np
        B, TQ, TK, D, ATTN = (16, 64, 256, 128, 128)
        key = jax.random.key(seed)
        k1, k2, k3, k4 = jax.random.split(key, 4)
        dec_out = jax.random.normal(k1, (B, TQ, D), dtype=jnp.float32)
        enc_out = jax.random.normal(k2, (B, TK, D), dtype=jnp.float32)
        enc_mask = jax.random.randint(k3, (B, TQ, TK), 0, 2) == 1
        W_attn = jax.random.normal(k4, (ATTN, 2 * D), dtype=jnp.float32) * (np.sqrt(6.0) * np.sqrt(6.0 / (2 * D + ATTN)))
        return {'dec_out': dec_out, 'enc_out': enc_out, 'enc_mask': enc_mask, 'W_attn': W_attn}
    _L1_xattn_all = _L1_xattn_setup()
    _L1_xattn_in = {k: v for k, v in _L1_xattn_all.items() if k in ('W_attn',)}
    del _L1_xattn_all

    def _L1_ffn_setup():
        import jax, jax.numpy as jnp
        import numpy as np
        H, I, E, K = (128, 64, 32, 8)
        B, S = (4, 128)

        def silu(x):
            return x * jax.nn.sigmoid(x)
        key = jax.random.key(seed)
        ks = jax.random.split(key, 14)

        def w(k, shape, fan_in):
            return jax.random.normal(k, shape, jnp.float32) / np.float32(np.sqrt(fan_in))
        return {'hidden_states': jax.random.normal(ks[0], (B, S, H), jnp.float32), 'Wr': w(ks[1], (H, E), H), 'br': jnp.zeros((E,), jnp.float32), 'Wg_s': w(ks[2], (H, I), H), 'bg_s': jnp.zeros((I,), jnp.float32), 'Wu_s': w(ks[3], (H, I), H), 'bu_s': jnp.zeros((I,), jnp.float32), 'Wd_s': w(ks[4], (I, H), I), 'bd_s': jnp.zeros((H,), jnp.float32), 'Wg': w(ks[5], (E, H, I), H), 'bg': jnp.zeros((E, I), jnp.float32), 'Wu': w(ks[6], (E, H, I), H), 'bu': jnp.zeros((E, I), jnp.float32), 'Wd': w(ks[7], (E, I, H), I), 'bd': jnp.zeros((E, H), jnp.float32)}
    _L1_ffn_all = _L1_ffn_setup()
    _L1_ffn_in = {k: v for k, v in _L1_ffn_all.items() if k in ('Wr', 'br', 'Wg_s', 'bg_s', 'Wu_s', 'bu_s', 'Wd_s', 'bd_s', 'Wg', 'bg', 'Wu', 'bu', 'Wd', 'bd')}
    del _L1_ffn_all
    return {'x': x, 'ctx_1024': ctx_1024, 'mask_BxSxS2_bk0': mask_BxSxS2_bk0, 'L0_xattn_Wq': _L0_xattn_in['Wq'], 'L0_xattn_bq': _L0_xattn_in['bq'], 'L0_xattn_Wk': _L0_xattn_in['Wk'], 'L0_xattn_bk': _L0_xattn_in['bk'], 'L0_xattn_Wv': _L0_xattn_in['Wv'], 'L0_xattn_bv': _L0_xattn_in['bv'], 'L0_xattn_Wo': _L0_xattn_in['Wo'], 'L0_xattn_bo': _L0_xattn_in['bo'], 'L0_ffn_gate_w': _L0_ffn_in['gate_w'], 'L0_ffn_ln_w': _L0_ffn_in['ln_w'], 'L0_ffn_ln_b': _L0_ffn_in['ln_b'], 'L0_ffn_fc1s': _L0_ffn_in['fc1s'], 'L0_ffn_b1s': _L0_ffn_in['b1s'], 'L0_ffn_fc2s': _L0_ffn_in['fc2s'], 'L0_ffn_b2s': _L0_ffn_in['b2s'], 'L1_xattn_W_attn': _L1_xattn_in['W_attn'], 'L1_ffn_Wr': _L1_ffn_in['Wr'], 'L1_ffn_br': _L1_ffn_in['br'], 'L1_ffn_Wg_s': _L1_ffn_in['Wg_s'], 'L1_ffn_bg_s': _L1_ffn_in['bg_s'], 'L1_ffn_Wu_s': _L1_ffn_in['Wu_s'], 'L1_ffn_bu_s': _L1_ffn_in['bu_s'], 'L1_ffn_Wd_s': _L1_ffn_in['Wd_s'], 'L1_ffn_bd_s': _L1_ffn_in['bd_s'], 'L1_ffn_Wg': _L1_ffn_in['Wg'], 'L1_ffn_bg': _L1_ffn_in['bg'], 'L1_ffn_Wu': _L1_ffn_in['Wu'], 'L1_ffn_bu': _L1_ffn_in['bu'], 'L1_ffn_Wd': _L1_ffn_in['Wd'], 'L1_ffn_bd': _L1_ffn_in['bd']}

def reference(x, ctx_1024, mask_BxSxS2_bk0, L0_xattn_Wq, L0_xattn_bq, L0_xattn_Wk, L0_xattn_bk, L0_xattn_Wv, L0_xattn_bv, L0_xattn_Wo, L0_xattn_bo, L0_ffn_gate_w, L0_ffn_ln_w, L0_ffn_ln_b, L0_ffn_fc1s, L0_ffn_b1s, L0_ffn_fc2s, L0_ffn_b2s, L1_xattn_W_attn, L1_ffn_Wr, L1_ffn_br, L1_ffn_Wg_s, L1_ffn_bg_s, L1_ffn_Wu_s, L1_ffn_bu_s, L1_ffn_Wd_s, L1_ffn_bd_s, L1_ffn_Wg, L1_ffn_bg, L1_ffn_Wu, L1_ffn_bu, L1_ffn_Wd, L1_ffn_bd):
    import jax
    import jax.numpy as jnp

    def _L0_xattn_ref(query, key, value, Wq, bq, Wk, bk, Wv, bv, Wo, bo):
        import jax, jax.numpy as jnp
        import numpy as np
        EMBED_DIM = 128
        NUM_HEADS = 16
        HEAD_DIM = EMBED_DIM // NUM_HEADS
        B, T_Q, T_K = (2, 256, 256)
        b, tq, _ = query.shape
        tk = key.shape[1]
        q = (query @ Wq.T + bq).reshape(b, tq, NUM_HEADS, HEAD_DIM).transpose(0, 2, 1, 3)
        k = (key @ Wk.T + bk).reshape(b, tk, NUM_HEADS, HEAD_DIM).transpose(0, 2, 1, 3)
        v = (value @ Wv.T + bv).reshape(b, tk, NUM_HEADS, HEAD_DIM).transpose(0, 2, 1, 3)
        scores = jnp.einsum('bhqd,bhkd->bhqk', q, k) / np.sqrt(HEAD_DIM)
        attn = jax.nn.softmax(scores, axis=-1)
        attn = jnp.nan_to_num(attn, nan=0.0)
        out = jnp.einsum('bhqk,bhkd->bhqd', attn, v)
        out = out.transpose(0, 2, 1, 3).reshape(b, tq, EMBED_DIM)
        return out @ Wo.T + bo

    def _L0_ffn_ref(x, gate_w, ln_w, ln_b, fc1s, b1s, fc2s, b2s):
        import jax, jax.numpy as jnp
        import numpy as np
        B, S, D = (4, 512, 128)
        DD = 4 * D
        N_EXPERTS = 8
        CAPACITY = 1.0
        LN_EPS = 1e-05
        og_shape = x.shape
        d = og_shape[-1]
        xf = x.reshape(-1, d)
        bs = xf.shape[0]
        n = gate_w.shape[0]
        k = int(bs * CAPACITY) // n
        scores = jax.nn.softmax(xf @ gate_w.T, axis=-1)
        vals, idx = jax.lax.top_k(scores.T, k)
        kept_w = vals.T
        kept_idx = idx.T
        flat_idx = kept_idx.reshape(-1)
        y = xf[flat_idx].reshape(k, n, d)
        mu = y.mean(-1, keepdims=True)
        var = ((y - mu) ** 2).mean(-1, keepdims=True)
        y = (y - mu) * jax.lax.rsqrt(var + LN_EPS) * ln_w + ln_b
        h = jnp.einsum('knd,nfd->knf', y, fc1s) + b1s
        h = jax.nn.gelu(h, approximate=True)
        out = jnp.einsum('knf,ndf->knd', h, fc2s) + b2s
        out = out * kept_w[..., None]
        xf = xf.at[flat_idx].add(out.reshape(k * n, d))
        return xf.reshape(og_shape)

    def _L1_xattn_ref(dec_out, enc_out, enc_mask, W_attn):
        import jax, jax.numpy as jnp
        import numpy as np
        B, TQ, TK, D, ATTN = (16, 64, 256, 128, 128)
        attn = jnp.einsum('bqd,bkd->bqk', dec_out, enc_out)
        attn = jnp.where(enc_mask, -jnp.inf, attn)
        attn = jax.nn.softmax(attn, axis=2)
        context = jnp.einsum('bqk,bkd->bqd', attn, enc_out)
        cat = jnp.concatenate([context, dec_out], axis=2)
        output = jnp.einsum('bqf,af->bqa', cat, W_attn)
        return output

    def _L1_ffn_ref(hidden_states, Wr, br, Wg_s, bg_s, Wu_s, bu_s, Wd_s, bd_s, Wg, bg, Wu, bu, Wd, bd):
        import jax, jax.numpy as jnp
        import numpy as np
        H, I, E, K = (128, 64, 32, 8)
        B, S = (4, 128)

        def silu(x):
            return x * jax.nn.sigmoid(x)
        b, s, h = hidden_states.shape
        T = b * s
        x = hidden_states.reshape(T, h)
        logits = jnp.dot(x.astype(jnp.float32), Wr) + br
        aff = jax.nn.sigmoid(logits)
        top_v, top_i = jax.lax.top_k(aff, K)
        top_w = top_v / (jnp.sum(top_v, axis=-1, keepdims=True) + 1e-09)
        top_w = top_w.astype(hidden_states.dtype)
        e_total = Wr.shape[1]
        w_full = jnp.zeros((T, e_total), hidden_states.dtype)
        w_full = w_full.at[jnp.arange(T)[:, None], top_i].set(top_w)
        shared = jnp.dot(silu(jnp.dot(x, Wg_s) + bg_s) * (jnp.dot(x, Wu_s) + bu_s), Wd_s) + bd_s
        gate = silu(jnp.einsum('th,ehi->eti', x, Wg) + bg[:, None, :])
        up = jnp.einsum('th,ehi->eti', x, Wu) + bu[:, None, :]
        down = jnp.einsum('eti,eih->eth', gate * up, Wd) + bd[:, None, :]
        routed = jnp.einsum('te,eth->th', w_full, down)
        return (shared + routed).reshape(b, s, h)
    x = x + _L0_xattn_ref(_layernorm(x, axis=-1), ctx_1024, ctx_1024, L0_xattn_Wq, L0_xattn_bq, L0_xattn_Wk, L0_xattn_bk, L0_xattn_Wv, L0_xattn_bv, L0_xattn_Wo, L0_xattn_bo)
    x = x + _L0_ffn_ref(_layernorm(x, axis=-1), L0_ffn_gate_w, L0_ffn_ln_w, L0_ffn_ln_b, L0_ffn_fc1s, L0_ffn_b1s, L0_ffn_fc2s, L0_ffn_b2s)
    x = x + _L1_xattn_ref(_layernorm(x, axis=-1), ctx_1024, mask_BxSxS2_bk0, L1_xattn_W_attn)
    x = x + _L1_ffn_ref(_layernorm(x, axis=-1), L1_ffn_Wr, L1_ffn_br, L1_ffn_Wg_s, L1_ffn_bg_s, L1_ffn_Wu_s, L1_ffn_bu_s, L1_ffn_Wd_s, L1_ffn_bd_s, L1_ffn_Wg, L1_ffn_bg, L1_ffn_Wu, L1_ffn_bu, L1_ffn_Wd, L1_ffn_bd)
    return x

_drawn_inputs = setup_inputs


def setup_inputs(seed=0):
    import zlib

    import numpy as np

    out = dict(_drawn_inputs(seed))
    spreads = {'L0_xattn_bq': (0.0, 0.1),
     'L0_xattn_bk': (0.0, 0.8),
     'L0_xattn_bv': (0.0, 0.1),
     'L0_xattn_bo': (0.0, 0.1),
     'L0_ffn_ln_w': (1.0, 0.6),
     'L0_ffn_ln_b': (0.0, 0.8),
     'L1_ffn_br': (0.0, 0.77),
     'L1_ffn_bg_s': (0.0, 0.611),
     'L1_ffn_bu_s': (0.0, 0.786),
     'L1_ffn_bd_s': (0.0, 0.454),
     'L1_ffn_bg': (0.0, 0.8),
     'L1_ffn_bu': (0.0, 0.8),
     'L1_ffn_bd': (0.0, 0.8)}
    factors = {'L0_ffn_b1s': 6.777, 'L0_ffn_b2s': 8.0}
    for name, (base, spread) in spreads.items():
        noise = np.random.default_rng([zlib.crc32(name.encode()), seed]).standard_normal(out[name].shape)
        drawn = base * np.exp(spread * noise) if base else spread * noise
        out[name] = jnp.asarray(drawn.astype(out[name].dtype))
    for name, factor in factors.items():
        out[name] = (out[name] * factor).astype(out[name].dtype)
    return out
```

```python
from contextlib import ExitStack

import numpy as np
import concourse.bass as bass
from concourse import mybir

P = 128
D = 128
B, S = 2, 512
T = B * S // P
TB = T // B
SK = 154
HEADS, DH = 16, 8
HH = HEADS // 2
FLAT = HH * SK
NBLK = -(-FLAT // P)
VW = DH + 1
E0, F0 = 8, 512
FT = F0 // P
CAP = B * S // E0
E1, I1, TOP = 32, 64, 8
PAIRS = E1 // 2 + 1
GW = 3 * P + P
REC = GW + 2
EPS = 1e-5
SHIFTS = [28, 24, 20, 16, 12, 8, 4, 0]
MASKED = -3.0e38
NOSLOT = 200.0

F32 = mybir.dt.float32
F32R = mybir.dt.float32r
BF16 = mybir.dt.bfloat16
I32 = mybir.dt.int32
U8 = mybir.dt.uint8
ALU = mybir.AluOpType
ACT = mybir.ActivationFunctionType
AX = mybir.AxisListType

PACK = {}
_at = 0
for _name, _width in (("ident", P), ("headmask", HH), ("vmask", NBLK * HH), ("tri", P), ("group", P),
                      ("iota", P), ("jf", len(SHIFTS)), ("cand0", 1), ("bq", 1), ("bk", 1), ("bv", 1),
                      ("ln_w", 1), ("ln_b", 1), ("bd_s", 1), ("b1", E0 * FT)):
    PACK[_name] = (_at, _at + _width)
    _at += _width
NPACK = _at


def build(nc, x_d, ctx2_d, ctxk_d, mask_d, watt_d, pack_d, rows_d, gate_d, fc1_d, fc2_d, wout_d, wr_d, rec_d,
          bd_d, out_d):
    with ExitStack() as ctx:
        def sb(name, shape, dt=F32):
            return ctx.enter_context(nc.sbuf_tensor(name, shape, dt))

        def sem(name):
            return ctx.enter_context(nc.semaphore(name))

        def lay(base, names, parts=P):
            out, at = [], 0
            for shape in names:
                n = int(np.prod(shape[1:]))
                v = base[0:shape[0], at:at + n]
                ax = "abcd"[:len(shape) - 1]
                if len(shape) > 2:
                    v = v.rearrange(f"p ({' '.join(ax)}) -> p {' '.join(ax)}",
                                    **{a: m for a, m in zip(ax, shape[1:])})
                out.append(v)
                at += n
            assert at <= base.shape[1], (at, base.shape)
            return out

        bank = ctx.enter_context(nc.psum_tensor("bank", [P, 8, 512], F32))
        flat = bank[:, :, :].rearrange("p b c -> p (b c)")

        x = sb("x", [P, T, D])
        ctx2 = sb("ctx2", [P, B, 2 * SK])
        ctxa = sb("ctxa", [P, B, D])
        ctxb = sb("ctxb", [SK - P, B, D])
        mask = sb("mask", [P, T, SK], U8)
        keep = sb("keep", [P, T, SK], U8)
        watt = sb("watt", [P, 4, D])
        pack = sb("pack", [P, NPACK])
        rows = sb("rows", [1, D + E0 * D + E1])
        gate = sb("gate", [P, E0])
        fc2 = sb("fc2", [P, E0, FT, D])
        wout = sb("wout", [P, 2, D])
        wr = sb("wr", [P, E1])
        bd = sb("bd", [E1, D])

        def const(name):
            return pack[:, PACK[name][0]:PACK[name][1]]

        ident = const("ident")
        bo_row = rows[0:1, 0:D]
        br_row = rows[0:1, D + E0 * D:]
        b1 = const("b1").rearrange("p (e f) -> p e f", e=E0)

        arena_a = sb("arena_a", [P, E0 * T * P], F32R)
        qhi, qlo, kbdhi, kbdlo = lay(arena_a, ([P, T * P], [P, T * P], [P, B, HH, SK], [P, B, HH, SK]))
        pickT, = lay(arena_a, ([P, E0, T * P],))
        arena_b = sb("arena_b", [P, T * E0 * P], F32R)
        pick, = lay(arena_b, ([P, T, E0, P],))
        y3hi, y3lo, w3, whi, wlo, hhi, hlo = lay(arena_b, (
            [P, T * P], [P, T * P], [3 * E1, T * P], [P, 2, GW], [P, 2, 3 * P], [P, 2, 512], [P, 2, 512]))
        arena_c = sb("arena_c", [P, 8192])
        vraw, vblk, prob, probT = lay(arena_c, ([P, NBLK, D], [P, B, 2, NBLK, HH * VW], [P, 2, NBLK * P],
                                                [P, NBLK, P]))
        yg, ygT, hid, aff, ex, left, wsel, pTa, pTb, coT, wT, sm = lay(arena_c, (
            [P, E0, D + E0], [P, 2, P], [P, 2, FT, P], [P, T, E1], [P, T, E1], [P, T, E1], [P, T, E1],
            [P, TB * P], [SK - P, TB * P], [P, TB * P], [E1, T * P],
            [P, T, SK]))
        screp, = lay(arena_c, ([P, T, E0, P // E0],))
        arena_d = sb("arena_d", [P, E0 * F0])
        fc1, = lay(arena_d, ([P, E0, F0],))
        sil, gu, hh, yT = lay(arena_d, ([P, 2, 512], [P, 2, 512], [P, 2, 512], [P, T * P]))

        stats = sb("stats", [P, TB, 6])
        mv = sb("mv", [P, TB, 2])
        vareps = sb("vareps", [P, TB])
        rstd = sb("rstd", [P, TB])
        neghalf = sb("neghalf", [P, TB])
        onesrow = sb("onesrow", [1, P])
        onesb = sb("onesb", [P, P], BF16)
        trib = sb("trib", [P, P], BF16)
        groupb = sb("groupb", [P, P], BF16)

        xn = sb("xn", [P, T, D])
        xnT = sb("xnT", [P, T * P])
        kT = sb("kT", [P, B, SK])
        khi = sb("khi", [P, B, SK], F32R)
        klo = sb("klo", [P, B, SK], F32R)
        smax = sb("smax", [P, 2 * T, HH])
        rsum = sb("rsum", [P, HH])
        att = sb("att", [P, D])
        attT = sb("attT", [P, D])
        x1 = sb("x1", [P, T, D])
        y0 = sb("y0", [P, T, D])
        res = sb("res", [P, T, D])
        x2, x3, out = x1, res, x

        lg = sb("lg", [P, T, E0])
        sc = sb("sc", [P, T, E0])
        small = sb("small", [P, 4, T])
        srep = sb("srep", [P, T * P])
        junk = sb("junk", [P, T * P], BF16)
        count = sb("count", [P, 1])
        okb = sb("okb", [P, 1], BF16)
        prefix = sb("prefix", [P, 1], I32)
        delta = sb("delta", [P, 2], I32)
        cand = sb("cand", [P, 1], I32)
        thr = sb("thr", [P, E0])
        gteq = sb("gteq", [P, 2, T, E0], BF16)
        room = sb("room", [P, E0])
        pre = sb("pre", [P, 2, T, E0])
        work = sb("work", [P, 3, T, E0])
        slot = sb("slot", [P, T, E0])
        GC = D + E0
        yhi = sb("yhi", [P, T, GC], F32R)
        ylo = sb("ylo", [P, T, GC], F32R)
        ohi = sb("ohi", [P, E0, D], F32R)
        olo = sb("olo", [P, E0, D], F32R)

        negmax = sb("negmax", [P, T])
        ssum = sb("ssum", [P, T])
        srec = sb("srec", [P, T])

        top8 = sb("top8", [P, T, TOP])
        wsum = sb("wsum", [P, 2, T])
        rec = sb("rec", [P, 2, REC])
        bias = sb("bias", [P, 2, 2])

        def f32(ap):
            return ap.bitcast(F32)

        L = {n: sem("ld_" + n) for n in ("x0", "x1", "ctx2", "watt", "pack", "rows", "gate", "fc1", "fc2", "ctxa",
                                          "ctxb", "mask", "wout", "wr", "bd")}
        names = """var_ready rstd_ready consts_ready xn_ready xnT_psum xnT_ready q_psum qhi_ready qlo_ready k_psum
        kT_ready khi_ready klo_ready kbd_dve kbd_pool v_psum vraw_ready vblk_ready pad_zero scores_done
        max_done sub_done exp_done pT_psum pT_ready pv_done rsum_done att_ready attT_psum attT_ready proj_done x1_ready
        y0_ready y0T_psum y0T_ready logit_psum lgsub_ready lgexp_ready sc_ready screp_ready srep_psum srep_ready
        count_ready ok_ready nok_psum delta_ready prefix_ready cand_ready thr_psum gteq_ready pre_psum slot_ready
        pick_ready yh_ready yhi_ready ylo_ready res_ready gath_psum yg_ready ygT_psum ygT_ready fc1_psum hid_ready
        fc2_psum ohi_ready olo_ready pickT_psum pickT_ready scat_psum x2_ready
        y2_ready y2T_psum y2T_ready s1_psum keep_ready sm_ready negmax_ready p1_ready p1n_ready p1T_psum p1T_ready
        co_psum co_ready o1_psum x3_ready y3_ready y3T_psum y3T_ready y3hi_ready y3lo_ready
        lr_psum aff0_ready ex_ready wsel_ready wT_psum wT_ready w3_ready w3ones_ready rec_ready0 rec_ready1 split_ready
        bias_ready rec_asked split_begun gate_psum upw_psum sil_ready gu_ready hh_ready hhi_ready hlo_ready down_done y_psum yT_ready
        outT_psum out_ready stored dve_chain""".split()
        Z = {n: sem(n) for n in names}

        block = ctx.enter_context(nc.Block())

        @block.sync
        def _(sp):
            sp.dma_start(x[:, 0:TB], x_d[:, 0:TB]).then_inc(L["x0"], 16)
            sp.dma_start(watt[:, :, :], watt_d).then_inc(L["watt"], 16)
            sp.dma_start(x[:, TB:], x_d[:, TB:]).then_inc(L["x1"], 16)
            sp.dma_start(rows[:, :], rows_d).then_inc(L["rows"], 16)
            sp.dma_start(gate[:, :], gate_d).then_inc(L["gate"], 16)
            sp.dma_start(fc1[:, :, :], fc1_d).then_inc(L["fc1"], 16)
            sp.dma_start(fc2[:, :, :, :], fc2_d).then_inc(L["fc2"], 16)
            sp.dma_start(mask[:, :, :], mask_d).then_inc(L["mask"], 16)
            sp.dma_start(ctxa[:, :, :], ctxk_d[0:P]).then_inc(L["ctxa"], 16)
            sp.dma_start(ctxb[:, :, :], ctxk_d[P:SK]).then_inc(L["ctxb"], 16)
            sp.dma_start(wout[:, :, :], wout_d).then_inc(L["wout"], 16)
            sp.dma_start(wr[:, :], wr_d).then_inc(L["wr"], 16)
            sp.dma_start(bd[:, :], bd_d).then_inc(L["bd"], 16)
            for n in range(2):
                sp.dma_start(rec[:, n, :], rec_d[n]).then_inc(Z["rec_ready%d" % n], 16)
            with sp.Fori(1, PAIRS // 2) as m:
                for u in range(2):
                    sp.wait_ge(Z["split_ready"], m * 2 + (u - 1))
                    sp.sem_inc(Z["rec_asked"], 1)
                    sp.dma_start(rec[:, u, :], rec_d[bass.ds(m * 2 + u, 1)].rearrange("o p c -> (o p) c"))\
                        .then_inc(Z["rec_ready%d" % u], 16)
            sp.wait_ge(Z["split_ready"], PAIRS - 2)
            sp.dma_start(rec[:, 0, :], rec_d[PAIRS - 1]).then_inc(Z["rec_ready0"], 16)
            for b in range(B):
                sp.wait_ge(Z["out_ready"], b + 1)
                sp.dma_start(out_d[:, b * TB:(b + 1) * TB], out[:, b * TB:(b + 1) * TB]).then_inc(Z["stored"], 16)
            sp.wait_ge(Z["stored"], 16 * B)

        @block.gpsimd
        def _(pool):
            rstds = [0]

            def rsqrt():
                rstds[0] += 1
                pool.wait_ge(Z["var_ready"], rstds[0])
                pool.tensor_tensor(rstd[:, :], vareps[:, :], neghalf[:, :], ALU.pow).then_inc(Z["rstd_ready"], 1)

            pool.memset(neghalf[:, :], -0.5).then_inc(Z["consts_ready"], 1)
            pool.memset(onesrow[:, :], 1.0).then_inc(Z["consts_ready"], 1)
            pool.memset(onesb[:, :], 1.0).then_inc(Z["consts_ready"], 1)
            pool.memset(prob[:, :, FLAT:], 0.0).then_inc(Z["pad_zero"], 1)
            pool.wait_ge(Z["consts_ready"], 3)
            rsqrt()
            rsqrt()
            def expand(dst, src, b):
                pool.tensor_tensor(dst[:, b], src[:, b, None, :].bitcast(F32).broadcast_to([P, HH, SK]),
                                   const("headmask")[:, :, None].broadcast_to([P, HH, SK]),
                                   ALU.mult).then_inc(Z["kbd_pool"], 1)
            pool.wait_ge(Z["klo_ready"], 1)
            expand(kbdlo, klo, 0)
            vm = const("vmask").rearrange("p (i h) -> p i h", i=NBLK)
            for b in range(B):
                pool.wait_ge(Z["vraw_ready"], b + 1)
                for g in range(2):
                    v = vblk[:, b, g].rearrange("p i (h w) -> p i h w", h=HH)
                    pool.tensor_tensor(v[:, :, :, 0:DH],
                                       vraw[:, :, g * HH * DH:(g + 1) * HH * DH].rearrange("p i (h d) -> p i h d", h=HH),
                                       vm[:, :, :, None].broadcast_to([P, NBLK, HH, DH]), ALU.mult)\
                        .then_inc(Z["vblk_ready"], 1)
                    pool.tensor_copy(v[:, :, :, DH:VW], vm[:, :, :, None]).then_inc(Z["vblk_ready"], 1)
                if b == 0:
                    expand(kbdhi, khi, 1)
                    expand(kbdlo, klo, 1)
            pool.wait_ge(L["mask"], 16)
            rsqrt()
            rsqrt()
            rsqrt()
            rsqrt()
            pool.wait_ge(Z["y0_ready"], 2 * TB)
            pool.tensor_tensor(res[:, :, :], x1[:, :, :], y0[:, :, :], ALU.add).then_inc(Z["res_ready"], 1)
            pool.memset(sm[:, :, :], MASKED).then_inc(Z["pad_zero"], 1)
            for b in range(B):
                rsqrt()
                rsqrt()
            pool.wait_ge(Z["rstd_ready"], rstds[0])
            pool.memset(w3[2 * E1:3 * E1, :].bitcast(F32), 1.0).then_inc(Z["w3ones_ready"], 1)
            pool.wait_ge(Z["w3ones_ready"], 1)
            def split(u):
                pool.tensor_copy(whi[:, u, :], rec[:, u, 0:GW])\
                    .then_inc(Z["bias_ready"], 1)
                pool.tensor_copy(bias[:, u, :], rec[:, u, GW:REC]).then_inc(Z["bias_ready"], 1)
            def split_lo(u):
                pool.tensor_tensor(wlo[:, u, :], rec[:, u, 0:3 * P], f32(whi[:, u, 0:3 * P]), ALU.subtract)\
                    .then_inc(Z["split_ready"], 1)
            for u in range(2):
                pool.wait_ge(Z["rec_ready%d" % u], 16)
                split(u)
                pool.wait_ge(Z["bias_ready"], 2 * (u + 1))
                split_lo(u)
            with pool.Fori(1, PAIRS // 2) as m:
                for u in range(2):
                    pool.wait_ge(Z["rec_ready%d" % u], m * 16 + 16)
                    pool.wait_ge(Z["down_done"], m * 4 + (2 * u - 2))
                    pool.sem_inc(Z["split_begun"], 1)
                    split(u)
                    pool.wait_ge(Z["bias_ready"], m * 4 + (2 * u + 2))
                    split_lo(u)
            pool.wait_ge(Z["rec_ready0"], 16 * (PAIRS // 2 + 1))
            pool.wait_ge(Z["down_done"], 2 * (PAIRS - 2))
            split(0)
            pool.wait_ge(Z["bias_ready"], 2 * PAIRS)
            split_lo(0)

        @block.vector
        def _(dve):
            chain = [0]

            def link(ins):
                chain[0] += 1
                ins.then_inc(Z["dve_chain"], 1)
                dve.wait_ge(Z["dve_chain"], chain[0])

            norms = [0]

            def norm(src, dst, t0, done):
                norms[0] += 1
                for i in range(TB):
                    ins = dve.bn_stats(stats[:, i, :], src[:, t0 + i, :])
                link(ins)
                for i in range(TB):
                    ins = dve.bn_aggr(mv[:, i, :], stats[:, i, :])
                link(ins)
                dve.tensor_scalar_add(vareps[:, :], mv[:, :, 1], EPS).then_inc(Z["var_ready"], 1)
                dve.wait_ge(Z["rstd_ready"], norms[0])
                for i in range(TB):
                    dve.tensor_scalar(dst[:, t0 + i, 0:D], src[:, t0 + i, :], mv[:, i, 0:1], rstd[:, i:i + 1],
                                      ALU.subtract, ALU.mult).then_inc(Z[done], 1)

            dve.wait_ge(L["x0"], 16)
            norm(x, xn, 0, "xn_ready")
            dve.wait_ge(L["pack"], 16)
            dve.wait_ge(Z["kT_ready"], 1)
            dve.tensor_copy(khi[:, :, :], kT[:, :, :]).then_inc(Z["khi_ready"], 1)
            dve.wait_ge(Z["khi_ready"], 1)
            dve.tensor_tensor(klo[:, :, :], kT[:, :, :], f32(khi[:, :, :]), ALU.subtract).then_inc(Z["klo_ready"], 1)
            dve.tensor_tensor(kbdhi[:, 0], khi[:, 0, None, :].bitcast(F32).broadcast_to([P, HH, SK]),
                              const("headmask")[:, :, None].broadcast_to([P, HH, SK]), ALU.mult)\
                .then_inc(Z["kbd_dve"], 1)

            def q_lo(b):
                dve.wait_ge(Z["qhi_ready"], b + 1)
                dve.scalar_tensor_tensor(qlo[:, b * S:(b + 1) * S], bank[:, 7, :], const("bq"),
                                         f32(qhi[:, b * S:(b + 1) * S]), ALU.add, ALU.subtract)\
                    .then_inc(Z["qlo_ready"], 1)
            q_lo(0)
            dve.wait_ge(L["x1"], 16)
            norm(x, xn, TB, "xn_ready")
            dve.tensor_copy(trib[:, :], const("tri")).then_inc(Z["consts_ready"], 1)
            dve.tensor_copy(groupb[:, :], const("group")).then_inc(Z["consts_ready"], 1)
            q_lo(1)

            def normalise(s):
                t, g = s // 2, s % 2
                dve.wait_ge(Z["pv_done"], s + 1)
                o = bank[:, 7, 0:HH * VW].rearrange("p (h w) -> p h w", h=HH)
                dve.reciprocal(rsum[:, :], o[:, :, DH]).then_inc(Z["rsum_done"], 1)
                dve.wait_ge(Z["rsum_done"], s + 1)
                if g == 0 and t:
                    dve.wait_ge(Z["attT_psum"], t)
                dve.tensor_tensor(att[:, g * HH * DH:(g + 1) * HH * DH].rearrange("p (h d) -> p h d", h=HH),
                                  o[:, :, 0:DH], rsum[:, :, None].broadcast_to([P, HH, DH]), ALU.mult)\
                    .then_inc(Z["att_ready"], 1)

            def residual(t):
                dve.wait_ge(Z["proj_done"], t + 1)
                dve.tensor_tensor(x1[:, t, :], bank[:, 7, 0:D], x[:, t, :], ALU.add).then_inc(Z["x1_ready"], 1)

            for s in range(2 * T):
                dve.wait_ge(Z["scores_done"], s + 1)
                b0 = 3 * (s % 2) * 512
                score = flat[:, b0:b0 + FLAT].rearrange("p (h k) -> p h k", h=HH)
                dve.tensor_reduce(smax[:, s, :], score, AX.X, ALU.max).then_inc(Z["max_done"], 1)
                dve.wait_ge(Z["max_done"], s + 1)
                if s >= 2:
                    dve.wait_ge(Z["pT_psum"], 3 * (s - 1))
                dve.tensor_tensor(prob[:, s % 2, 0:FLAT].rearrange("p (h k) -> p h k", h=HH), score,
                                  smax[:, s, :, None].broadcast_to([P, HH, SK]), ALU.subtract)\
                    .then_inc(Z["sub_done"], 1)
                if s:
                    normalise(s - 1)
                if s and s % 2 == 0:
                    residual(s // 2 - 1)
                if s == 9:
                    dve.wait_ge(Z["x1_ready"], TB)
                    norm(x1, y0, 0, "y0_ready")
                    dve.wait_ge(Z["y0_ready"], TB)
                    norm(y0, xn, 0, "yh_ready")
                    dve.wait_ge(L["mask"], 16)
                    dve.tensor_scalar(keep[:, :, :], mask[:, :, :], 0.0, None, ALU.is_equal)\
                        .then_inc(Z["keep_ready"], 1)
            normalise(2 * T - 1)
            residual(T - 1)
            dve.wait_ge(Z["x1_ready"], T)
            norm(x1, y0, TB, "y0_ready")
            dve.wait_ge(Z["y0_ready"], T)
            dve.wait_ge(Z["logit_psum"], 1)
            gl = bank[:, 6, 0:T * E0].rearrange("p (t e) -> p t e", t=T)
            link(dve.tensor_reduce(small[:, 0, :], gl, AX.X, ALU.max))
            dve.tensor_tensor(lg[:, :, :], gl, small[:, 0, :, None].broadcast_to([P, T, E0]), ALU.subtract)\
                .then_inc(Z["lgsub_ready"], 1)
            norm(y0, xn, TB, "yh_ready")
            dve.wait_ge(Z["lgexp_ready"], 1)
            link(dve.tensor_reduce(small[:, 1, :], lg[:, :, :], AX.X, ALU.add))
            link(dve.reciprocal(small[:, 2, :], small[:, 1, :]))
            dve.tensor_tensor(sc[:, :, :], lg[:, :, :], small[:, 2, :, None].broadcast_to([P, T, E0]), ALU.mult)\
                .then_inc(Z["sc_ready"], 1)
            dve.wait_ge(Z["sc_ready"], 1)
            dve.tensor_copy(screp[:, :, :, :], sc[:, :, :, None].broadcast_to([P, T, E0, P // E0]))\
                .then_inc(Z["screp_ready"], 1)
            dve.memset(prefix[:, :], 0).then_inc(Z["prefix_ready"], 1)
            dve.wait_ge(Z["prefix_ready"], 1)
            dve.wait_ge(Z["srep_ready"], 1)
            for k, shift in enumerate(SHIFTS):
                c = const("cand0") if k == 0 else cand[:, :].bitcast(F32)
                if k:
                    dve.wait_ge(Z["cand_ready"], k)
                dve.tensor_scalar(junk[:, :], srep[:, :], c, 0.0, ALU.is_ge, ALU.add, accum_out=count[:, :])\
                    .then_inc(Z["count_ready"], 1)
                dve.wait_ge(Z["count_ready"], k + 1)
                dve.tensor_scalar(okb[:, :], count[:, :], CAP - 0.5, None, ALU.is_ge).then_inc(Z["ok_ready"], 1)
                dve.wait_ge(Z["nok_psum"], k + 1)
                nok = bank[:, 7, 0:1]
                if k + 1 < len(SHIFTS):
                    dve.tensor_scalar(delta[:, 0:1], nok, float(1 << shift), const("jf")[:, k:k + 1], ALU.mult, ALU.add)\
                        .then_inc(Z["delta_ready"], 1)
                else:
                    dve.tensor_scalar(delta[:, 0:1], nok, -1.0, None, ALU.add).then_inc(Z["delta_ready"], 1)
                dve.tensor_scalar(delta[:, 1:2], nok, -1.0, float(1 << shift), ALU.add, ALU.mult)\
                    .then_inc(Z["delta_ready"], 1)
                dve.wait_ge(Z["delta_ready"], 2 * k + 2)
                if k + 1 < len(SHIFTS):
                    dve.tensor_tensor(cand[:, :], prefix[:, :], delta[:, 0:1], ALU.bitwise_or)\
                        .then_inc(Z["cand_ready"], 1)
                dve.tensor_tensor(prefix[:, :], prefix[:, :], delta[:, 1:2], ALU.bitwise_or)\
                    .then_inc(Z["prefix_ready"], 1)
                dve.wait_ge(Z["prefix_ready"], k + 2)
            dve.wait_ge(Z["thr_psum"], 1)
            link(dve.tensor_copy(thr[:, :], bank[:, 6, 0:P].rearrange("p (e j) -> p e j", e=E0)[:, :, 0]))
            tb = thr[:, None, :].broadcast_to([P, T, E0])
            dve.tensor_tensor(gteq[:, 0], sc[:, :, :], tb, ALU.is_gt).then_inc(Z["gteq_ready"], 1)
            dve.tensor_tensor(gteq[:, 1], sc[:, :, :], tb, ALU.is_equal).then_inc(Z["gteq_ready"], 1)
            dve.wait_ge(Z["pre_psum"], 1)
            dve.tensor_copy(pre[:, :, :, :].rearrange("p k t e -> p (k t e)"), bank[:, 6, 0:2 * T * E0])
            link(dve.tensor_scalar(room[:, :], bank[:, 7, 0:E0], -1.0, float(CAP), ALU.mult, ALU.add))
            rb = room[:, None, :].broadcast_to([P, T, E0])
            link(dve.tensor_tensor(work[:, 0], pre[:, 1], rb, ALU.is_lt))
            link(dve.tensor_tensor(work[:, 1], work[:, 0], gteq[:, 1], ALU.mult))
            link(dve.tensor_tensor(work[:, 0], work[:, 1], gteq[:, 0], ALU.add))
            link(dve.tensor_tensor(work[:, 2], pre[:, 1], rb, ALU.min))
            link(dve.tensor_tensor(work[:, 1], work[:, 2], pre[:, 0], ALU.add))
            link(dve.scalar_tensor_tensor(work[:, 2], work[:, 1], -NOSLOT, work[:, 0], ALU.add, ALU.mult))
            dve.tensor_scalar_add(slot[:, :, :], work[:, 2], NOSLOT).then_inc(Z["slot_ready"], 1)
            dve.wait_ge(Z["slot_ready"], 1)
            dve.wait_ge(Z["yhi_ready"], 2)
            dve.tensor_tensor(ylo[:, :, 0:D], xn[:, :, :], f32(yhi[:, :, 0:D]), ALU.subtract)\
                .then_inc(Z["ylo_ready"], 1)
            dve.tensor_tensor(ylo[:, :, D:GC], sc[:, :, :], f32(yhi[:, :, D:GC]), ALU.subtract)\
                .then_inc(Z["ylo_ready"], 1)
            def picks(e):
                for t in range(T):
                    dve.tensor_scalar(pick[:, t, e, :], const("iota"), slot[:, t, e:e + 1], None, ALU.is_equal)\
                        .then_inc(Z["pick_ready"], 1)

            def low_out(e):
                dve.wait_ge(Z["ohi_ready"], e + 1)
                dve.scalar_tensor_tensor(olo[:, e, :], bank[:, 5, 0:D], yg[:, e, D + e:D + e + 1], f32(ohi[:, e, :]),
                                         ALU.mult, ALU.subtract).then_inc(Z["olo_ready"], 1)

            def keep_picks(e):
                dve.wait_ge(Z["pickT_psum"], 2 * e + 2)
                dve.tensor_copy(pickT[:, e, S:], bank[:, 7, :]).then_inc(Z["pickT_ready"], 1)

            picks(0)
            picks(1)
            keep_picks(0)
            for e in range(E0):
                if e + 2 < E0:
                    picks(e + 2)
                if e + 1 < E0:
                    keep_picks(e + 1)
                if e:
                    low_out(e - 1)
            low_out(E0 - 1)
            for b in range(B):
                dve.wait_ge(Z["res_ready"], 1)
                dve.wait_ge(Z["scat_psum"], b + 1)
                t0 = b * TB
                dve.tensor_tensor(x2[:, t0:t0 + TB, :].rearrange("p t d -> p (t d)"), bank[:, b, :],
                                  res[:, t0:t0 + TB, :].rearrange("p t d -> p (t d)"), ALU.add)\
                    .then_inc(Z["x2_ready"], 1)
                dve.wait_ge(Z["x2_ready"], b + 1)
                norm(x2, xn, t0, "y2_ready")
                dve.wait_ge(Z["s1_psum"], b + 1)
                dve.wait_ge(Z["keep_ready"], 1)
                dve.wait_ge(Z["pad_zero"], 2)
                dve.copy_predicated(sm[:, t0:t0 + 3, :], keep[:, t0:t0 + 3, :],
                                    bank[:, 3, 0:3 * SK].rearrange("p (t k) -> p t k", t=3))
                link(dve.copy_predicated(sm[:, t0 + 3, :], keep[:, t0 + 3, :], bank[:, 4, 0:SK]))
                dve.tensor_reduce(negmax[:, t0:t0 + TB], sm[:, t0:t0 + TB, :], AX.X, ALU.max, negate=True)\
                    .then_inc(Z["negmax_ready"], 1)
                dve.wait_ge(Z["p1_ready"], TB * (b + 1))
                link(dve.scalar_tensor_tensor(srec[:, t0:t0 + TB], negmax[:, t0:t0 + TB], -MASKED,
                                              ssum[:, t0:t0 + TB], ALU.is_lt, ALU.mult))
                link(dve.reciprocal(srec[:, t0:t0 + TB], srec[:, t0:t0 + TB]))
                for t in range(t0, t0 + TB):
                    dve.tensor_scalar(sm[:, t, :], sm[:, t, :], srec[:, t:t + 1], None, ALU.mult)\
                        .then_inc(Z["p1n_ready"], 1)
                dve.wait_ge(Z["o1_psum"], b + 1)
                dve.tensor_tensor(x3[:, t0:t0 + TB, :].rearrange("p t d -> p (t d)"), bank[:, 3, :],
                                  x2[:, t0:t0 + TB, :].rearrange("p t d -> p (t d)"), ALU.add)\
                    .then_inc(Z["x3_ready"], 1)
                dve.wait_ge(Z["x3_ready"], b + 1)
                norm(x3, y0, t0, "y3_ready")
                dve.wait_ge(Z["y3T_ready"], b + 1)
                cs = slice(b * S, (b + 1) * S)
                dve.tensor_copy(y3hi[:, cs], xnT[:, cs]).then_inc(Z["y3hi_ready"], 1)
                dve.wait_ge(Z["y3hi_ready"], b + 1)
                dve.tensor_tensor(y3lo[:, cs], xnT[:, cs], f32(y3hi[:, cs]), ALU.subtract).then_inc(Z["y3lo_ready"], 1)
            dve.wait_ge(Z["ex_ready"], 1)
            link(dve.tensor_scalar_add(ex[:, :, :], ex[:, :, :], 1.0))
            link(dve.reciprocal(aff[:, :, :], ex[:, :, :]))
            for t in range(T):
                ins = dve.max(top8[:, t, :], aff[:, t, :])
            link(ins)
            for t in range(T):
                ins = dve.match_replace(left[:, t, :], top8[:, t, :], aff[:, t, :], -1.0)
            link(ins)
            link(dve.scalar_tensor_tensor(wsel[:, :, :], left[:, :, :], 0.0, aff[:, :, :], ALU.is_lt, ALU.mult))
            link(dve.tensor_reduce(wsum[:, 0, :], wsel[:, :, :], AX.X, ALU.add))
            link(dve.tensor_scalar_add(wsum[:, 0, :], wsum[:, 0, :], 1e-9))
            link(dve.reciprocal(wsum[:, 1, :], wsum[:, 0, :]))
            dve.tensor_tensor(wsel[:, :, :], wsel[:, :, :], wsum[:, 1, :, None].broadcast_to([P, T, E1]), ALU.mult)\
                .then_inc(Z["wsel_ready"], 1)
            dve.wait_ge(Z["wT_ready"], 2)
            dve.tensor_copy(w3[0:E1, :], wT[:, :]).then_inc(Z["w3_ready"], 1)
            dve.wait_ge(Z["w3_ready"], 1)
            dve.tensor_tensor(w3[E1:2 * E1, :], wT[:, :], f32(w3[0:E1, :]), ALU.subtract).then_inc(Z["w3_ready"], 1)
            def hidden(k, c, u, first=False):
                dve.wait_ge(Z["sil_ready"], k + 1)
                dve.wait_ge(Z["upw_psum"], k + 1)
                dve.scalar_tensor_tensor(gu[:, c, :], bank[:, 2 + c, :], bias[:, u, 1:2], sil[:, c, :],
                                         ALU.add, ALU.mult).then_inc(Z["gu_ready"], 1)
                if not first:
                    low_hidden(k - 1, 1 - c)
                dve.wait_ge(Z["gu_ready"], k + 1)
                dve.tensor_tensor(hh[:, c, :], gu[:, c, :], bank[:, 4 + c, :], ALU.mult).then_inc(Z["hh_ready"], 1)

            def low_hidden(k, c):
                dve.wait_ge(Z["hhi_ready"], k + 1)
                dve.tensor_tensor(hlo[:, c, :], hh[:, c, :], f32(hhi[:, c, :]), ALU.subtract)\
                    .then_inc(Z["hlo_ready"], 1)

            hidden(0, 0, 0, first=True)
            hidden(1, 1, 0)
            with dve.Fori(1, PAIRS, 2) as q:
                for u in range(2):
                    for c in range(2):
                        hidden(q * 2 + (2 * u + c), c, (u + 1) % 2)
            low_hidden(2 * PAIRS - 1, 1)
            for b in range(B):
                dve.wait_ge(Z["outT_psum"], b + 1)
                dve.tensor_tensor(out[:, b * TB:(b + 1) * TB, :].rearrange("p t d -> p (t d)"), bank[:, b, :],
                                  x3[:, b * TB:(b + 1) * TB, :].rearrange("p t d -> p (t d)"), ALU.add)\
                    .then_inc(Z["out_ready"], 1)

        @block.scalar
        def _(act):
            act.dma_start(pack[:, :], pack_d).then_inc(L["pack"], 16)
            act.dma_start(ctx2[:, :, :], ctx2_d).then_inc(L["ctx2"], 16)
            act.wait_ge(L["pack"], 16)
            act.wait_ge(Z["k_psum"], 1)
            act.activation(kT[:, :, :].rearrange("p b k -> p (b k)"), bank[:, 5, 0:B * SK], ACT.Identity,
                           bias=const("bk")).then_inc(Z["kT_ready"], 1)

            def queries(b):
                cs = slice(b * S, (b + 1) * S)
                act.wait_ge(Z["xnT_psum"], b + 1)
                act.copy(xnT[:, cs], bank[:, 6, :]).then_inc(Z["xnT_ready"], 1)
                act.wait_ge(Z["q_psum"], b + 1)
                act.activation(qhi[:, cs], bank[:, 7, :], ACT.Identity, bias=const("bq")).then_inc(Z["qhi_ready"], 1)

            def values(b):
                if b:
                    act.wait_ge(Z["vblk_ready"], 4 * b)
                act.wait_ge(Z["v_psum"], b + 1)
                act.copy(vraw[:, :, :].rearrange("p i d -> p (i d)"), flat[:, 0:NBLK * D]).then_inc(Z["vraw_ready"], 1)

            queries(0)
            values(0)
            queries(1)
            values(1)

            for s in range(2 * T):
                act.wait_ge(Z["sub_done"], s + 1)
                act.activation(prob[:, s % 2, 0:FLAT], prob[:, s % 2, 0:FLAT], ACT.Exp, scale=float(DH) ** -0.5)\
                    .then_inc(Z["exp_done"], 1)
                for r, (i0, i1) in enumerate(((0, 4), (4, 8), (8, NBLK))):
                    act.wait_ge(Z["pT_psum"], 3 * s + r + 1)
                    if r == 0 and s:
                        act.wait_ge(Z["pv_done"], s)
                    act.copy(probT[:, i0:i1, :].rearrange("p i q -> p (i q)"), bank[:, 6, 0:(i1 - i0) * P])\
                        .then_inc(Z["pT_ready"], 1)
                    if r == 0 and s and s % 2 == 0:
                        turn_out = s // 2
                        act.wait_ge(Z["attT_psum"], turn_out)
                        act.activation(attT[:, :], bank[:, 7, 0:D], ACT.Identity, bias=const("bv"))\
                            .then_inc(Z["attT_ready"], 1)
            act.wait_ge(Z["attT_psum"], T)
            act.activation(attT[:, :], bank[:, 7, 0:D], ACT.Identity, bias=const("bv")).then_inc(Z["attT_ready"], 1)

            for b in range(B):
                act.wait_ge(Z["y0T_psum"], b + 1)
                act.copy(xnT[:, b * S:(b + 1) * S], bank[:, b, :]).then_inc(Z["y0T_ready"], 1)
            act.wait_ge(Z["lgsub_ready"], 1)
            act.activation(lg[:, :, :], lg[:, :, :], ACT.Exp).then_inc(Z["lgexp_ready"], 1)
            act.wait_ge(Z["srep_psum"], 1)
            act.copy(srep[:, :], flat[:, 2 * 512:4 * 512]).then_inc(Z["srep_ready"], 1)
            act.wait_ge(Z["yh_ready"], T)
            act.copy(yhi[:, :, 0:D], xn[:, :, :]).then_inc(Z["yhi_ready"], 1)
            act.wait_ge(Z["sc_ready"], 1)
            act.copy(yhi[:, :, D:GC], sc[:, :, :]).then_inc(Z["yhi_ready"], 1)

            def gathered(e):
                act.wait_ge(Z["gath_psum"], e + 1)
                act.copy(yg[:, e, :], bank[:, e % 2, 0:GC]).then_inc(Z["yg_ready"], 1)
                act.wait_ge(Z["pickT_psum"], 2 * e + 1)
                act.copy(pickT[:, e, 0:S], bank[:, 6, :]).then_inc(Z["pickT_ready"], 1)

            def high_out(e):
                act.wait_ge(Z["fc2_psum"], e + 1)
                act.activation(ohi[:, e, :], bank[:, 5, 0:D], ACT.Copy, scale=yg[:, e, D + e:D + e + 1])\
                    .then_inc(Z["ohi_ready"], 1)

            gathered(0)
            for e in range(E0):
                if e + 1 < E0:
                    gathered(e + 1)
                act.wait_ge(Z["ygT_psum"], e + 1)
                act.activation(ygT[:, e % 2, :], bank[:, 2, 0:P], ACT.Identity, bias=const("ln_b"),
                               scale=const("ln_w")).then_inc(Z["ygT_ready"], 1)
                act.wait_ge(Z["fc1_psum"], e + 1)
                for f in range(FT):
                    act.activation(hid[:, e % 2, f, :], bank[:, 3 + e % 2, f * P:(f + 1) * P], ACT.Gelu_apprx_tanh,
                                   bias=b1[:, e, f:f + 1]).then_inc(Z["hid_ready"], 1)
                if e:
                    high_out(e - 1)
            high_out(E0 - 1)

            for b in range(B):
                t0, cs = b * TB, slice(b * S, (b + 1) * S)
                act.wait_ge(Z["y2T_psum"], b + 1)
                act.copy(xnT[:, cs], bank[:, 2, :]).then_inc(Z["y2T_ready"], 1)
                act.wait_ge(Z["negmax_ready"], b + 1)
                for t in range(t0, t0 + TB):
                    act.activation(sm[:, t, :], sm[:, t, :], ACT.Exp, bias=negmax[:, t:t + 1],
                                   accum_out=ssum[:, t:t + 1]).then_inc(Z["p1_ready"], 1)
                act.wait_ge(Z["p1T_psum"], b + 1)
                act.copy(pTa[:, :], bank[:, 5, :]).then_inc(Z["p1T_ready"], 1)
                act.copy(pTb[:, :], bank[0:SK - P, 6, :]).then_inc(Z["p1T_ready"], 1)
                act.wait_ge(Z["co_psum"], b + 1)
                act.copy(coT[:, :], bank[:, 7, :]).then_inc(Z["co_ready"], 1)
                act.wait_ge(Z["y3T_psum"], b + 1)
                act.copy(xnT[:, cs], bank[:, 2, :]).then_inc(Z["y3T_ready"], 1)
            act.wait_ge(Z["lr_psum"], 1)
            act.activation(ex[:, :, :].rearrange("p t e -> p (t e)"), bank[:, 4, 0:T * E1], ACT.Exp, scale=-1.0)\
                .then_inc(Z["ex_ready"], 1)
            for b in range(B):
                act.wait_ge(Z["wT_psum"], b + 1)
                act.copy(wT[:, b * S:(b + 1) * S], bank[0:E1, 5 + b, :]).then_inc(Z["wT_ready"], 1)

            def silu(k, c, u):
                act.wait_ge(Z["gate_psum"], k + 1)
                act.activation(sil[:, c, :], bank[:, c, :], ACT.Silu, bias=bias[:, u, 0:1]).then_inc(Z["sil_ready"], 1)

            def high_hidden(k, c, free=True):
                act.wait_ge(Z["hh_ready"], k + 1)
                if free:
                    act.wait_ge(Z["down_done"], k - 1)
                act.copy(hhi[:, c, :], hh[:, c, :]).then_inc(Z["hhi_ready"], 1)

            silu(0, 0, 0)
            silu(1, 1, 0)
            high_hidden(0, 0, free=False)
            with act.Fori(1, PAIRS, 2) as q:
                for u in range(2):
                    for c in range(2):
                        k = q * 2 + (2 * u + c)
                        act.wait_ge(Z["hh_ready"], k - 1)
                        silu(k, c, (u + 1) % 2)
                        high_hidden(k - 1, 1 - c, free=False)
            high_hidden(2 * PAIRS - 1, 1, free=False)
            for b in range(B):
                if b == 0:
                    act.wait_ge(Z["down_done"], 2 * PAIRS - 1)
                else:
                    act.wait_ge(Z["y_psum"], 1)
                act.activation(yT[:, b * S:(b + 1) * S], bank[:, 6 + b, :], ACT.Identity, bias=const("bd_s"))\
                    .then_inc(Z["yT_ready"], 1)

        @block.tensor
        def _(pe):
            def turn(dst, src, n=P):
                return pe.transpose(dst, src, ident[0:n, 0:n])

            pe.wait_ge(L["ctx2"], 16)
            pe.wait_ge(L["watt"], 16)
            pe.matmul(bank[:, 5, 0:B * SK], watt[:, 1, :], ctx2[:, :, 0:SK], start=True, stop=True)\
                .then_inc(Z["k_psum"], 1)
            pe.wait_ge(L["pack"], 16)

            def queries(b):
                pe.wait_ge(Z["xn_ready"], TB * (b + 1))
                for i in range(TB):
                    ins = turn(bank[:, 6, i * P:(i + 1) * P], xn[:, b * TB + i, :])
                ins.then_inc(Z["xnT_psum"], 1)
                pe.wait_ge(Z["xnT_ready"], b + 1)
                if b:
                    pe.wait_ge(Z["qlo_ready"], b)
                pe.matmul(bank[:, 7, :], watt[:, 0, :], xnT[:, b * S:(b + 1) * S], start=True, stop=True)\
                    .then_inc(Z["q_psum"], 1)

            def values(b):
                if b:
                    pe.wait_ge(Z["vraw_ready"], b)
                for i in range(NBLK):
                    o = (P * i) % SK
                    ins = pe.matmul(flat[:, i * D:(i + 1) * D], ctx2[:, b, o:o + P], watt[:, 2, :], start=True, stop=True)
                ins.then_inc(Z["v_psum"], 1)

            queries(0)
            values(0)
            queries(1)
            values(1)

            chunks = ((0, 512), (512, 1024), (1024, FLAT))

            def scores(s):
                t, g, b = s // 2, s % 2, s // 2 // TB
                if s == 0:
                    pe.wait_ge(Z["vraw_ready"], 2)
                    pe.wait_ge(Z["qlo_ready"], 2)
                    pe.wait_ge(Z["kbd_dve"], 1)
                    pe.wait_ge(Z["kbd_pool"], 1)
                if s == 2 * TB:
                    pe.wait_ge(Z["kbd_pool"], 3)
                if s >= 2:
                    pe.wait_ge(Z["sub_done"], s - 1)
                b0 = 3 * (s % 2) * 512
                r = slice(64 * g, 64 * g + 64)
                q = slice(t * P, (t + 1) * P)
                for n, (qq, kk) in enumerate(((qhi, kbdhi), (qhi, kbdlo), (qlo, kbdhi))):
                    for c0, c1 in chunks:
                        ins = pe.matmul(flat[:, b0 + c0:b0 + c1], qq[r, q],
                                        kk[r, b].rearrange("p h k -> p (h k)")[:, c0:c1],
                                        start=(n == 0), stop=(n == 2))
                ins.then_inc(Z["scores_done"], 1)

            def project(t):
                pe.wait_ge(Z["attT_ready"], t + 1)
                pe.matmul(bank[:, 7, 0:D], onesrow[:, :], bo_row, start=True, stop=False)
                pe.matmul(bank[:, 7, 0:D], attT[:, :], watt[:, 3, :], start=False, stop=True).then_inc(Z["proj_done"], 1)

            pe.wait_ge(L["rows"], 16)
            pe.wait_ge(Z["consts_ready"], 3)
            scores(0)
            for s in range(2 * T):
                b = s // 2 // TB
                if s + 1 < 2 * T:
                    scores(s + 1)
                for r, (i0, i1) in enumerate(((0, 4), (4, 8), (8, NBLK))):
                    pe.wait_ge(Z["exp_done"], s + 1)
                    if s == 0 and r == 0:
                        pe.wait_ge(Z["pad_zero"], 1)
                    if 3 * s + r:
                        pe.wait_ge(Z["pT_ready"], 3 * s + r)
                    for i in range(i0, i1):
                        ins = turn(bank[:, 6, (i - i0) * P:(i - i0 + 1) * P], prob[:, s % 2, i * P:(i + 1) * P])
                    ins.then_inc(Z["pT_psum"], 1)
                    if s and s % 2 == 0 and r == 0:
                        pe.wait_ge(Z["att_ready"], s)
                        turn(bank[:, 7, 0:D], att[:, :]).then_inc(Z["attT_psum"], 1)
                    if s and s % 2 == 0 and r == 1:
                        project(s // 2 - 1)
                if s % 2:
                    pe.wait_ge(Z["att_ready"], s)
                elif s:
                    pe.wait_ge(Z["x1_ready"], s // 2)
                pe.wait_ge(Z["pT_ready"], 3 * s + 3)
                pe.wait_ge(Z["vblk_ready"], 4 * (b + 1))
                for i in range(NBLK):
                    ins = pe.matmul(bank[:, 7, 0:HH * VW], probT[:, i, :], vblk[:, b, s % 2, i, :],
                                    start=(i == 0), stop=(i == NBLK - 1))
                ins.then_inc(Z["pv_done"], 1)
            pe.wait_ge(Z["att_ready"], 2 * T)
            turn(bank[:, 7, 0:D], att[:, :]).then_inc(Z["attT_psum"], 1)
            project(T - 1)

            for b in range(B):
                pe.wait_ge(Z["y0_ready"], TB * (b + 1))
                for i in range(TB):
                    ins = turn(bank[:, b, i * P:(i + 1) * P], y0[:, b * TB + i, :])
                ins.then_inc(Z["y0T_psum"], 1)
            pe.wait_ge(L["gate"], 16)
            pe.wait_ge(Z["y0T_ready"], 2)
            for t in range(T):
                ins = pe.matmul(bank[:, 6, t * E0:(t + 1) * E0], xnT[:, t * P:(t + 1) * P], gate[:, :],
                                start=True, stop=True)
            ins.then_inc(Z["logit_psum"], 1)
            pe.wait_ge(Z["screp_ready"], 1)
            for t in range(T):
                ins = turn(flat[:, 2 * 512 + t * P:2 * 512 + (t + 1) * P],
                           screp[:, t].rearrange("p e j -> p (e j)"))
            ins.then_inc(Z["srep_psum"], 1)
            pe.wait_ge(Z["consts_ready"], 5)
            pe.wait_ge(Z["x1_ready"], T)
            for k in range(len(SHIFTS)):
                pe.wait_ge(Z["ok_ready"], k + 1)
                if k:
                    pe.wait_ge(Z["delta_ready"], 2 * k)
                pe.matmul(bank[:, 7, 0:1], groupb[:, :], okb[:, :], start=True, stop=True).then_inc(Z["nok_psum"], 1)
            pe.wait_ge(Z["prefix_ready"], len(SHIFTS) + 1)
            turn(bank[:, 6, 0:P], prefix[:, :].bitcast(F32).broadcast_to([P, P])).then_inc(Z["thr_psum"], 1)
            pe.wait_ge(Z["gteq_ready"], 2)
            pv = bank[:, 6, 0:2 * T * E0].rearrange("p (k t e) -> p k t e", k=2, t=T)
            pe.matmul(bank[:, 6, 0:2 * T * E0], trib[:, :], gteq[:, :, :, :].rearrange("p k t e -> p (k t e)"),
                      start=True, stop=False)
            for t in range(T - 1):
                n = T - 1 - t
                for k in range(2):
                    pe.matmul(pv[:, k, t + 1:, :], onesb[:, :], gteq[:, k, t, None, :].broadcast_to([P, n, E0]),
                              start=False, stop=(t == T - 2 and k == 1))
            for t in range(T):
                ins = pe.matmul(bank[:, 7, 0:E0], onesb[:, :], gteq[:, 0, t, :], start=(t == 0), stop=(t == T - 1))
            ins.then_inc(Z["pre_psum"], 1)

            pe.wait_ge(L["fc1"], 16)
            pe.wait_ge(L["fc2"], 16)
            pe.wait_ge(Z["slot_ready"], 1)
            pe.wait_ge(Z["ylo_ready"], 2)

            def gather(e):
                pe.wait_ge(Z["pick_ready"], T * (e + 1))
                if e >= 2:
                    pe.wait_ge(Z["yg_ready"], e - 1)
                for t in range(T):
                    pe.matmul(bank[:, e % 2, 0:GC], pick[:, t, e, :], yhi[:, t, :], start=(t == 0), stop=False)
                    ins = pe.matmul(bank[:, e % 2, 0:GC], pick[:, t, e, :], ylo[:, t, :], start=False,
                                    stop=(t == T - 1))
                ins.then_inc(Z["gath_psum"], 1)
                for b in range(B):
                    if e:
                        pe.wait_ge(Z["pickT_ready"], 2 * e)
                    for i in range(TB):
                        ins = turn(bank[:, 6 + b, i * P:(i + 1) * P], f32(pick[:, b * TB + i, e, :]))
                    ins.then_inc(Z["pickT_psum"], 1)

            def first_layer(e):
                pe.wait_ge(Z["yg_ready"], e + 1)
                if e:
                    pe.wait_ge(Z["ygT_ready"], e)
                turn(bank[:, 2, 0:P], yg[:, e, 0:D]).then_inc(Z["ygT_psum"], 1)
                pe.wait_ge(Z["ygT_ready"], e + 1)
                if e >= 2:
                    pe.wait_ge(Z["hid_ready"], FT * (e - 1))
                for f in range(FT):
                    ins = pe.matmul(bank[:, 3 + e % 2, f * P:(f + 1) * P], fc1[:, e, f * P:(f + 1) * P],
                                    ygT[:, e % 2, :], start=True, stop=True)
                ins.then_inc(Z["fc1_psum"], 1)

            def second_layer(e):
                pe.wait_ge(Z["hid_ready"], FT * (e + 1))
                if e:
                    pe.wait_ge(Z["olo_ready"], e)
                pe.matmul(bank[:, 5, 0:D], onesrow[:, :], rows[0:1, D + e * D:D + (e + 1) * D], start=True, stop=False)
                for f in range(FT):
                    ins = pe.matmul(bank[:, 5, 0:D], hid[:, e % 2, f, :], fc2[:, e, f, :], start=False,
                                    stop=(f == FT - 1))
                ins.then_inc(Z["fc2_psum"], 1)

            gather(0)
            for e in range(E0):
                if e + 1 < E0:
                    gather(e + 1)
                first_layer(e)
                if e:
                    second_layer(e - 1)
            second_layer(E0 - 1)
            pe.wait_ge(Z["pickT_ready"], 2 * E0)
            pe.wait_ge(Z["olo_ready"], E0)
            for b in range(B):
                for i in range(TB):
                    t = b * TB + i
                    for e in range(E0):
                        pe.matmul(bank[:, b, i * P:(i + 1) * P], pickT[:, e, t * P:(t + 1) * P], ohi[:, e, :],
                                  start=(e == 0), stop=False)
                        ins = pe.matmul(bank[:, b, i * P:(i + 1) * P], pickT[:, e, t * P:(t + 1) * P], olo[:, e, :],
                                        start=False, stop=(e == E0 - 1))
                ins.then_inc(Z["scat_psum"], 1)

            pe.wait_ge(L["wout"], 16)
            pe.wait_ge(L["ctxa"], 16)
            pe.wait_ge(L["ctxb"], 16)
            pe.wait_ge(L["wr"], 16)
            for b in range(B):
                t0, cs = b * TB, slice(b * S, (b + 1) * S)
                pe.wait_ge(Z["y2_ready"], TB * (b + 1))
                for i in range(TB):
                    ins = turn(bank[:, 2, i * P:(i + 1) * P], xn[:, t0 + i, :])
                ins.then_inc(Z["y2T_psum"], 1)
                pe.wait_ge(Z["y2T_ready"], b + 1)
                if b:
                    pe.wait_ge(Z["x3_ready"], b)
                for i in range(TB):
                    d = bank[:, 3, i * SK:(i + 1) * SK] if i < 3 else bank[:, 4, 0:SK]
                    ins = pe.matmul(d, xnT[:, (t0 + i) * P:(t0 + i + 1) * P], ctx2[:, b, 0:SK], start=True, stop=True)
                ins.then_inc(Z["s1_psum"], 1)
                pe.wait_ge(Z["p1n_ready"], TB * (b + 1))
                for i in range(TB):
                    turn(bank[:, 5, i * P:(i + 1) * P], sm[:, t0 + i, 0:P])
                    ins = turn(bank[0:SK - P, 6, i * P:(i + 1) * P], sm[:, t0 + i, P:SK])
                ins.then_inc(Z["p1T_psum"], 1)
                pe.wait_ge(Z["p1T_ready"], 2 * (b + 1))
                pe.matmul(bank[:, 7, :], ctxa[:, b, :], pTa[:, :], start=True, stop=False)
                pe.matmul(bank[:, 7, :], ctxb[:, b, :], pTb[:, :], start=False, stop=True).then_inc(Z["co_psum"], 1)
                pe.wait_ge(Z["co_ready"], b + 1)
                for i in range(TB):
                    pe.matmul(bank[:, 3, i * P:(i + 1) * P], coT[:, i * P:(i + 1) * P], wout[:, 0, :],
                              start=True, stop=False)
                    ins = pe.matmul(bank[:, 3, i * P:(i + 1) * P], xnT[:, (t0 + i) * P:(t0 + i + 1) * P],
                                    wout[:, 1, :], start=False, stop=True)
                ins.then_inc(Z["o1_psum"], 1)
                pe.wait_ge(Z["y3_ready"], TB * (b + 1))
                for i in range(TB):
                    ins = turn(bank[:, 2, i * P:(i + 1) * P], y0[:, t0 + i, :])
                ins.then_inc(Z["y3T_psum"], 1)
                pe.wait_ge(Z["y3T_ready"], b + 1)
            for t in range(T):
                d = bank[:, 4, t * E1:(t + 1) * E1]
                pe.matmul(d, onesrow[:, :], br_row, start=True, stop=False)
                ins = pe.matmul(d, xnT[:, t * P:(t + 1) * P], wr[:, :], start=False, stop=True)
            ins.then_inc(Z["lr_psum"], 1)
            pe.wait_ge(Z["wsel_ready"], 1)
            for b in range(B):
                for i in range(TB):
                    ins = turn(bank[0:E1, 5 + b, i * P:(i + 1) * P], wsel[:, b * TB + i, :])
                ins.then_inc(Z["wT_psum"], 1)
            pe.wait_ge(Z["w3_ready"], 2)
            pe.wait_ge(Z["w3ones_ready"], 1)
            pe.wait_ge(Z["y3lo_ready"], 2)

            def gate_up(c, u):
                cs = slice(c * S, (c + 1) * S)
                for j in range(2):
                    w = slice(j * P, (j + 1) * P)
                    d = bank[:, 2 * j + c, :]
                    pe.matmul(d, whi[:, u, w], y3hi[:, cs], start=True, stop=False)
                    pe.matmul(d, whi[:, u, w], y3lo[:, cs], start=False, stop=False)
                    ins = pe.matmul(d, wlo[:, u, w], y3hi[:, cs], start=False, stop=True)
                    if j == 0:
                        ins.then_inc(Z["gate_psum"], 1)
                pe.matmul(bank[:, 4 + c, :], whi[0:3 * E1, u, 3 * P:GW], w3[:, cs], start=True, stop=True)\
                    .then_inc(Z["upw_psum"], 1)

            pe.wait_ge(L["bd"], 16)
            for b in range(B):
                pe.matmul(bank[:, 6 + b, :], bd[:, :], wT[:, b * S:(b + 1) * S], start=True, stop=False,
                          skip_group_check=True)

            def down(k, c, u, last=False):
                pe.wait_ge(Z["hhi_ready"], k + 1)
                w = slice(2 * P, 3 * P)
                d = bank[:, 6 + c, :]
                pe.matmul(d, whi[:, u, w], hhi[:, c, :], start=False, stop=False, skip_group_check=True)
                pe.matmul(d, wlo[:, u, w], hhi[:, c, :], start=False, stop=False, skip_group_check=True)
                pe.wait_ge(Z["hlo_ready"], k + 1)
                ins = pe.matmul(d, whi[:, u, w], hlo[:, c, :], start=False, stop=last, skip_group_check=True)
                ins.then_inc(Z["y_psum"] if last else Z["down_done"], 1)

            pe.wait_ge(Z["split_ready"], 1)
            gate_up(0, 0)
            gate_up(1, 0)
            pe.wait_ge(Z["wT_ready"], 2)
            down(0, 0, 0)
            with pe.Fori(1, PAIRS, 2) as q:
                for u in range(2):
                    for c in range(2):
                        k = q * 2 + (2 * u + c)
                        if c == 0:
                            pe.wait_ge(Z["split_ready"], q + (u + 1))
                        pe.wait_ge(Z["hh_ready"], k - 1)
                        gate_up(c, (u + 1) % 2)
                        down(k - 1, 1 - c, (u if c == 0 else u + 1) % 2)
            down(2 * PAIRS - 1, 1, 0, last=True)
            for b in range(B):
                pe.wait_ge(Z["yT_ready"], b + 1)
                for i in range(TB):
                    c = (b * TB + i) * P
                    ins = turn(bank[:, b, i * P:(i + 1) * P], yT[:, c:c + P])
                ins.then_inc(Z["outT_psum"], 1)


def constants():
    p = np.arange(P)
    c = {"ident": np.eye(P)}
    c["headmask"] = (p[:, None] % (HH * DH) // DH == np.arange(HH)).astype(np.float32)
    pair = P * np.arange(NBLK)[None, :, None] + p[:, None, None]
    c["vmask"] = (pair // SK == np.arange(HH)).astype(np.float32).reshape(P, NBLK * HH)
    c["tri"] = (p[:, None] < p[None, :]).astype(np.float32)
    c["group"] = (p[:, None] // 16 == p[None, :] // 16).astype(np.float32)
    c["iota"] = np.broadcast_to(p[None, :], (P, P))
    j = (p % 16).astype(np.float64)
    jf = np.zeros((P, len(SHIFTS)))
    for k in range(len(SHIFTS) - 1):
        jf[:, k] = j * 2.0 ** SHIFTS[k + 1] - 2.0 ** SHIFTS[k]
    c["jf"] = jf
    c["cand0"] = (np.minimum(p % 16, 4).astype(np.int64) << SHIFTS[0]).astype(np.int32).view(np.float32)[:, None]
    sel = np.zeros((PAIRS, P, P), np.float32)
    sel[0, 2 * E1, 0:I1] = 1
    for q in range(1, PAIRS):
        for h in range(2):
            e = 2 * (q - 1) + h
            sel[q, e, h * I1:(h + 1) * I1] = 1
            sel[q, E1 + e, h * I1:(h + 1) * I1] = 1
    return {k: np.ascontiguousarray(v, dtype=np.float32) for k, v in c.items()}, sel


def kernel(**inputs):
    import concourse.bacc as bacc
    from concourse.bass_utils import run_bass_kernel_spmd as run

    i = {k: np.asarray(v) for k, v in inputs.items()}
    consts, sel = constants()
    col = lambda v: v.reshape(-1, 1)
    ctx = i["ctx_1024"]
    ctxT = ctx.transpose(2, 0, 1)
    vectors = {"bq": col(i["L0_xattn_bq"]), "bk": col(i["L0_xattn_bk"]), "bv": col(i["L0_xattn_bv"]),
               "ln_w": col(i["L0_ffn_ln_w"]), "ln_b": col(i["L0_ffn_ln_b"]), "bd_s": col(i["L1_ffn_bd_s"]),
               "b1": i["L0_ffn_b1s"].reshape(E0, FT, P).transpose(2, 0, 1).reshape(P, E0 * FT)}
    parts = {**consts, **vectors}
    rec = np.zeros((PAIRS, P, REC), np.float32)
    rec[:, :, 3 * P:GW] = sel
    rec[0, :, 0:I1] = i["L1_ffn_Wg_s"]
    rec[0, :, P:P + I1] = i["L1_ffn_Wu_s"]
    rec[0, 0:I1, 2 * P:3 * P] = i["L1_ffn_Wd_s"]
    rec[0, 0:I1, GW] = i["L1_ffn_bg_s"]
    rec[0, 0:I1, GW + 1] = i["L1_ffn_bu_s"]
    n = PAIRS - 1
    rec[1:, :, 0:P] = i["L1_ffn_Wg"].reshape(n, 2, D, I1).transpose(0, 2, 1, 3).reshape(n, D, P)
    rec[1:, :, P:2 * P] = i["L1_ffn_Wu"].reshape(n, 2, D, I1).transpose(0, 2, 1, 3).reshape(n, D, P)
    rec[1:, :, 2 * P:3 * P] = i["L1_ffn_Wd"].reshape(n, P, D)
    rec[1:, :, GW] = i["L1_ffn_bg"].reshape(n, P)
    rec[1:, :, GW + 1] = i["L1_ffn_bu"].reshape(n, P)
    arrays = {
        "x": i["x"].reshape(T, P, D).transpose(1, 0, 2),
        "ctx2": np.concatenate([ctxT, ctxT], axis=2),
        "ctxk": ctx.transpose(1, 0, 2),
        "mask": i["mask_BxSxS2_bk0"].reshape(T, P, SK).transpose(1, 0, 2),
        "watt": np.stack([i["L0_xattn_W" + n].T for n in "qkvo"], axis=1),
        "pack": np.concatenate([parts[n] for n in PACK], axis=1),
        "rows": np.concatenate([i["L0_xattn_bo"], i["L0_ffn_b2s"].reshape(-1), i["L1_ffn_br"]])[None, :],
        "gate": i["L0_ffn_gate_w"].T,
        "fc1": i["L0_ffn_fc1s"].transpose(2, 0, 1),
        "fc2": i["L0_ffn_fc2s"].reshape(E0, D, FT, P).transpose(3, 0, 2, 1),
        "wout": i["L1_xattn_W_attn"].reshape(D, 2, D).transpose(2, 1, 0),
        "wr": i["L1_ffn_Wr"],
        "rec": rec,
        "bd": i["L1_ffn_bd"],
    }
    nc = bacc.Bacc("TRN2", target_bir_lowering=False, num_devices=1)
    arrays = {f"in_{k}": np.ascontiguousarray(v) for k, v in arrays.items()}
    args = [nc.dram_tensor(k, v.shape, mybir.dt.from_np(v.dtype), kind="ExternalInput").ap()
            for k, v in arrays.items()]
    out = nc.dram_tensor("out_0", (P, T, D), F32, kind="ExternalOutput").ap()
    build(nc, *args, out)
    r = run(nc, [arrays], core_ids=[0])
    return r.results[0]["out_0"].transpose(1, 0, 2).reshape(B, S, D)
```

```python
from contextlib import ExitStack

import numpy as np
import concourse.bass as bass
from concourse import mybir

P = 128
D = 128
B, S = 2, 512
T = B * S // P
TB = T // B
SK = 154
HEADS, DH = 16, 8
HH = HEADS // 2
FLAT = HH * SK
NBLK = -(-FLAT // P)
HW = HH * DH
COMBOS = 2 * B
E0, F0 = 8, 512
FT = F0 // P
CAP = B * S // E0
E1, I1, TOP = 32, 64, 8
PAIRS = E1 // 2 + 1
LOOPS = PAIRS // 3
GW = 3 * P + P
REC = GW + 2
EPS = 1e-5
VGROUPS = ((0, 4), (4, 8), (8, NBLK))
SHIFTS = [28, 24, 20, 16, 12, 8, 4, 0]
MASKED = -3.0e38
NOSLOT = 200.0

F32 = mybir.dt.float32
F32R = mybir.dt.float32r
BF16 = mybir.dt.bfloat16
I32 = mybir.dt.int32
U8 = mybir.dt.uint8
ALU = mybir.AluOpType
ACT = mybir.ActivationFunctionType
AX = mybir.AxisListType

PACK = {}
_at = 0
for _name, _width in (("ident", P), ("headmask", HH), ("vmask", NBLK * HH), ("tri", P), ("group", P),
                      ("iota", P), ("jf", len(SHIFTS)), ("cand0", 1), ("bo", D), ("bq", 2), ("bk", 2), ("bv", 1),
                      ("ln_w", 1), ("ln_b", 1), ("bd_s", 1), ("b1", E0 * FT)):
    PACK[_name] = (_at, _at + _width)
    _at += _width
NPACK = _at


def build(nc, x_d, ctx2_d, ctxk_d, mask_d, watt_d, ind_d, pack_d, rows_d, gate_d, fc1_d, fc2_d, wout_d, wr_d, rec_d,
          bd_d, out_d):
    with ExitStack() as ctx:
        def sb(name, shape, dt=F32):
            return ctx.enter_context(nc.sbuf_tensor(name, shape, dt))

        def sem(name):
            return ctx.enter_context(nc.semaphore(name))

        def lay(base, names, parts=P):
            out, at = [], 0
            for shape in names:
                n = int(np.prod(shape[1:]))
                v = base[0:shape[0], at:at + n]
                ax = "abcd"[:len(shape) - 1]
                if len(shape) > 2:
                    v = v.rearrange(f"p ({' '.join(ax)}) -> p {' '.join(ax)}",
                                    **{a: m for a, m in zip(ax, shape[1:])})
                out.append(v)
                at += n
            assert at <= base.shape[1], (at, base.shape)
            return out

        bank = ctx.enter_context(nc.psum_tensor("bank", [P, 8, 512], F32))
        flat = bank[:, :, :].rearrange("p b c -> p (b c)")

        x = sb("x", [P, T, D])
        ctx2 = sb("ctx2", [P, B, 2 * SK])
        ctxa = sb("ctxa", [P, B, D])
        ctxb = sb("ctxb", [SK - P, B, D])
        mask = sb("mask", [P, T, SK], U8)
        keep = sb("keep", [P, T, SK], U8)
        watt = sb("watt", [P, 6, D])
        pack = sb("pack", [P, NPACK])
        rows = sb("rows", [1, E0 * D + E1])
        gate = sb("gate", [P, E0])
        fc2 = sb("fc2", [P, E0, FT, D])
        wout = sb("wout", [P, 2, D])
        wr = sb("wr", [P, E1])
        bd = sb("bd", [E1, D])

        def const(name):
            return pack[:, PACK[name][0]:PACK[name][1]]

        ident = const("ident")
        br_row = rows[0:1, E0 * D:]
        b1 = const("b1").rearrange("p (e f) -> p e f", e=E0)

        arena_a = sb("arena_a", [P, E0 * T * P], F32R)
        qa, qb, ka, kb = lay(arena_a, ([P, 2, S], [P, 2, S], [P, 2, NBLK * P], [P, 2, NBLK * P]))
        pickT, = lay(arena_a, ([P, E0, T * P],))
        arena_b = sb("arena_b", [P, T * E0 * P], F32R)
        pick, = lay(arena_b, ([P, T, E0, P],))
        y3hi, y3lo, w3, whi, wlo, hhi, hlo = lay(arena_b, (
            [P, T * P], [P, T * P], [3 * E1, T * P], [P, 3, GW], [P, 3, 3 * P], [P, 2, 512], [P, 2, 512]))
        arena_c = sb("arena_c", [P, 8192])
        vraw, vaug, pT = lay(arena_c, ([P, NBLK, D], [P, B, 2, NBLK, P], [P, 3, S]))
        ind = pT[HW:HW + HH, :, :].rearrange("p a b -> p (a b)")[:, 0:NBLK * P]
        yg, ygT, hid, aff, ex, left, wsel, pTa, pTb, coT, wT, sm = lay(arena_c, (
            [P, E0, D + E0], [P, 2, P], [P, 2, FT, P], [P, T, E1], [P, T, E1], [P, T, E1], [P, T, E1],
            [P, TB * P], [SK - P, TB * P], [P, TB * P], [E1, T * P],
            [P, T, SK]))
        screp, = lay(arena_c, ([P, T, E0, P // E0],))
        arena_d = sb("arena_d", [P, E0 * F0])
        fc1, = lay(arena_d, ([P, E0, F0],))
        sil, gu, hh, yT = lay(arena_d, ([P, 2, 512], [P, 2, 512], [P, 2, 512], [P, T * P]))

        stats = sb("stats", [P, TB, 6])
        mv = sb("mv", [P, TB, 2])
        vareps = sb("vareps", [P, TB])
        rstd = sb("rstd", [P, TB])
        neghalf = sb("neghalf", [P, TB])
        onesrow = sb("onesrow", [1, P])
        onesb = sb("onesb", [P, P], BF16)
        trib = sb("trib", [P, P], BF16)
        groupb = sb("groupb", [P, P], BF16)

        xn = sb("xn", [P, T, D])
        xnT = sb("xnT", [P, T * P])
        kT = sb("kT", [P, 2, B, SK])
        arena_e = sb("arena_e", [P, 2 * E0 * D], F32R)
        khi, klo = lay(arena_e, ([P, 2, B, SK], [P, 2, B, SK]))
        ohi, olo = lay(arena_e, ([P, E0, D], [P, E0, D]))
        smax = sb("smax", [P, COMBOS * TB, HH])
        rsum = sb("rsum", [HW, S])
        att = sb("att", [P, S])
        attT = sb("attT", [P, S])
        x1 = sb("x1", [P, T, D])
        y0 = sb("y0", [P, T, D])
        res = sb("res", [P, T, D])
        x2, x3, out = x1, res, x

        lg = sb("lg", [P, T, E0])
        sc = sb("sc", [P, T, E0])
        small = sb("small", [P, 4, T])
        srep = xnT
        junk = att[:, :].bitcast(BF16)
        count = sb("count", [P, 1])
        okb = sb("okb", [P, 1], BF16)
        prefix = sb("prefix", [P, 1], I32)
        delta = sb("delta", [P, 2], I32)
        cand = sb("cand", [P, 1], I32)
        thr = sb("thr", [P, E0])
        gteq = sb("gteq", [P, 2, T, E0], BF16)
        room = sb("room", [P, E0])
        pre = sb("pre", [P, 2, T, E0])
        work = sb("work", [P, 3, T, E0])
        slot = sb("slot", [P, T, E0])
        GC = D + E0
        yhi = sb("yhi", [P, T, GC], F32R)
        ylo = sb("ylo", [P, T, GC], F32R)

        negmax = sb("negmax", [P, T])
        ssum = sb("ssum", [P, T])
        srec = sb("srec", [P, T])

        top8 = sb("top8", [P, T, TOP])
        wsum = sb("wsum", [P, 2, T])
        rec = sb("rec", [P, 3, REC])
        bias = sb("bias", [P, 3, 2])

        def f32(ap):
            return ap.bitcast(F32)

        L = {n: sem("ld_" + n) for n in ("x0", "x1", "ctx2", "watt", "pack", "rows", "gate", "fc1", "fc2", "ctxa",
                                          "ctxb", "mask", "wout", "wr", "bd", "ind")}
        names = """var_ready rstd_ready consts_ready xn_ready xnT_psum xnT_ready q_psum qhi_ready qlo_ready k_psum
        kT_ready khi_ready klo_ready ka_first kb_ind expanded v_psum vraw_ready vaug_ready rough_done max_done
        mT_psum mT_ready score_psum exp_done pv_done o_psum rsum_done att_ready attT_ready proj_psum xbo_ready
        pad_zero x1_ready y0_ready y0T_psum y0T_ready logit_psum lgsub_ready lgexp_ready sc_ready screp_ready srep_psum srep_ready
        count_ready ok_ready nok_psum delta_ready prefix_ready cand_ready thr_psum gteq_ready pre_psum slot_ready
        pick_ready yh_ready yhi_ready ylo_ready res_ready gath_psum yg_ready ygT_psum ygT_ready fc1_psum hid_ready
        fc2_psum ohi_ready olo_ready pickT_psum pickT_ready scat_psum x2_ready
        y2_ready y2T_psum y2T_ready s1_psum keep_ready sm_ready negmax_ready p1_ready p1n_ready p1T_psum p1T_ready
        co_psum co_ready o1_psum x3_ready y3_ready y3T_psum y3T_ready y3hi_ready y3lo_ready
        lr_psum aff0_ready ex_ready wsel_ready wT_psum wT_ready w3_ready w3ones_ready rec_ready0 rec_ready1 rec_ready2 split_ready
        bias_ready rec_asked split_begun gate_psum upw_psum sil_ready gu_ready hh_ready hhi_ready hlo_ready down_done y_psum yT_ready
        outT_psum out_ready stored dve_chain""".split()
        Z = {n: sem(n) for n in names}

        block = ctx.enter_context(nc.Block())

        @block.sync
        def _(sp):
            sp.dma_start(x[:, 0:TB], x_d[:, 0:TB]).then_inc(L["x0"], 16)
            sp.dma_start(watt[:, :, :], watt_d).then_inc(L["watt"], 16)
            sp.dma_start(x[:, TB:], x_d[:, TB:]).then_inc(L["x1"], 16)
            sp.dma_start(rows[:, :], rows_d).then_inc(L["rows"], 16)
            sp.dma_start(gate[:, :], gate_d).then_inc(L["gate"], 16)
            sp.dma_start(fc1[:, :, :], fc1_d).then_inc(L["fc1"], 16)
            sp.dma_start(fc2[:, :, :, :], fc2_d).then_inc(L["fc2"], 16)
            sp.dma_start(mask[:, :, :], mask_d).then_inc(L["mask"], 16)
            sp.dma_start(ctxa[:, :, :], ctxk_d[0:P]).then_inc(L["ctxa"], 16)
            sp.dma_start(ctxb[:, :, :], ctxk_d[P:SK]).then_inc(L["ctxb"], 16)
            sp.dma_start(wout[:, :, :], wout_d).then_inc(L["wout"], 16)
            sp.dma_start(wr[:, :], wr_d).then_inc(L["wr"], 16)
            sp.dma_start(bd[:, :], bd_d).then_inc(L["bd"], 16)
            for n in range(3):
                sp.dma_start(rec[:, n, :], rec_d[n]).then_inc(Z["rec_ready%d" % n], 16)
            with sp.Fori(1, LOOPS) as m:
                for u in range(3):
                    sp.wait_ge(Z["split_ready"], m * 3 + (u - 2))
                    sp.sem_inc(Z["rec_asked"], 1)
                    sp.dma_start(rec[:, u, :], rec_d[bass.ds(m * 3 + u, 1)].rearrange("o p c -> (o p) c"))\
                        .then_inc(Z["rec_ready%d" % u], 16)
            for n in range(3 * LOOPS, PAIRS):
                sp.wait_ge(Z["split_ready"], n - 2)
                sp.dma_start(rec[:, n % 3, :], rec_d[n]).then_inc(Z["rec_ready%d" % (n % 3)], 16)
            for b in range(B):
                sp.wait_ge(Z["out_ready"], b + 1)
                sp.dma_start(out_d[:, b * TB:(b + 1) * TB], out[:, b * TB:(b + 1) * TB]).then_inc(Z["stored"], 16)
            sp.wait_ge(Z["stored"], 16 * B)

        @block.gpsimd
        def _(pool):
            rstds = [0]

            def rsqrt():
                rstds[0] += 1
                pool.wait_ge(Z["var_ready"], rstds[0])
                pool.tensor_tensor(rstd[:, :], vareps[:, :], neghalf[:, :], ALU.pow).then_inc(Z["rstd_ready"], 1)

            pool.memset(neghalf[:, :], -0.5).then_inc(Z["consts_ready"], 1)
            pool.memset(onesrow[:, :], 1.0).then_inc(Z["consts_ready"], 1)
            pool.memset(onesb[:, :], 1.0).then_inc(Z["consts_ready"], 1)
            pool.memset(ka[:, :, FLAT:].bitcast(F32), 0.0).then_inc(Z["pad_zero"], 1)
            pool.memset(kb[:, :, FLAT:].bitcast(F32), 0.0).then_inc(Z["pad_zero"], 1)
            pool.wait_ge(Z["consts_ready"], 3)
            rsqrt()
            pool.wait_ge(Z["rstd_ready"], 1)
            pool.wait_ge(L["ind"], 16)
            pool.wait_ge(Z["pad_zero"], 2)
            for n in range(2):
                pool.tensor_copy(kb[HW:HW + HH, n, :], ind).then_inc(Z["kb_ind"], 1)
            pool.wait_ge(Z["kb_ind"], 2)

            expansions = [0]

            def expand(dst, src, c, rows):
                b, g = c // 2, c % 2
                expansions[0] += 1
                if expansions[0] > 1:
                    pool.wait_ge(Z["expanded"], expansions[0] - 1)
                pool.tensor_tensor(dst[0:rows, c % 2, 0:FLAT].rearrange("p (h k) -> p h k", h=HH),
                                   f32(src[0:rows, g, b, None, :]).broadcast_to([rows, HH, SK]),
                                   const("headmask")[0:rows, :, None].broadcast_to([rows, HH, SK]),
                                   ALU.mult).then_inc(Z["expanded"], 1)

            def values(b):
                pool.wait_ge(Z["vraw_ready"], 3 * (b + 1))
                for g in range(2):
                    v = vaug[:, b, g, :, :].rearrange("p i (a h d) -> p i a h d", a=2, h=HH)
                    pool.tensor_tensor(v[:, :, 0], vraw[:, :, g * HW:(g + 1) * HW].rearrange("p i (h d) -> p i h d", h=HH),
                                       vm[:, :, :, None].broadcast_to([P, NBLK, HH, DH]), ALU.mult)\
                        .then_inc(Z["vaug_ready"], 1)

            vm = const("vmask").rearrange("p (i h) -> p i h", i=NBLK)
            pool.wait_ge(Z["klo_ready"], 1)
            expand(kb, klo, 0, HW)
            pool.wait_ge(Z["expanded"], 1)
            for b in range(B):
                for g in range(2):
                    v = vaug[:, b, g, :, :].rearrange("p i (a h d) -> p i a h d", a=2, h=HH)
                    pool.tensor_copy(v[:, :, 1], vm[:, :, :, None].broadcast_to([P, NBLK, HH, DH]))\
                        .then_inc(Z["pad_zero"], 1)
                if b == 0:
                    values(0)
                    expand(ka, khi, 1, P)
                    expand(kb, klo, 1, HW)
                    rsqrt()
            for c in range(2, COMBOS):
                if c == 2:
                    pool.wait_ge(L["x0"], 16)
                    pool.wait_ge(L["x1"], 16)
                    pool.tensor_tensor(x1[:, :, :], x[:, :, :], const("bo")[:, None, :].broadcast_to([P, T, D]),
                                       ALU.add).then_inc(Z["xbo_ready"], 1)
                pool.wait_ge(Z["o_psum"], c - 1)
                expand(ka, khi, c, P)
                expand(kb, klo, c, HW)
                if c == 2:
                    values(1)
            pool.wait_ge(L["mask"], 16)
            rsqrt()
            rsqrt()
            rsqrt()
            rsqrt()
            pool.wait_ge(Z["y0_ready"], 2 * TB)
            pool.tensor_tensor(res[:, :, :], x1[:, :, :], y0[:, :, :], ALU.add).then_inc(Z["res_ready"], 1)
            pool.memset(sm[:, :, :], MASKED).then_inc(Z["pad_zero"], 1)
            for b in range(B):
                rsqrt()
                rsqrt()
            pool.wait_ge(Z["rstd_ready"], rstds[0])
            pool.memset(w3[2 * E1:3 * E1, :].bitcast(F32), 1.0).then_inc(Z["w3ones_ready"], 1)
            pool.wait_ge(Z["w3ones_ready"], 1)
            def split(u):
                pool.tensor_copy(whi[:, u, :], rec[:, u, 0:GW])\
                    .then_inc(Z["bias_ready"], 1)
                pool.tensor_copy(bias[:, u, :], rec[:, u, GW:REC]).then_inc(Z["bias_ready"], 1)
            def split_lo(u):
                pool.tensor_tensor(wlo[:, u, :], rec[:, u, 0:3 * P], f32(whi[:, u, 0:3 * P]), ALU.subtract)\
                    .then_inc(Z["split_ready"], 1)
            for n in range(3):
                pool.wait_ge(Z["rec_ready%d" % n], 16)
                split(n)
                pool.wait_ge(Z["bias_ready"], 2 * (n + 1))
                split_lo(n)
            with pool.Fori(1, LOOPS) as m:
                for u in range(3):
                    pool.wait_ge(Z["rec_ready%d" % u], m * 16 + 16)
                    pool.wait_ge(Z["down_done"], m * 6 + (2 * u - 4))
                    pool.sem_inc(Z["split_begun"], 1)
                    split(u)
                    pool.wait_ge(Z["bias_ready"], m * 6 + (2 * u + 2))
                    split_lo(u)
            for n in range(3 * LOOPS, PAIRS):
                pool.wait_ge(Z["rec_ready%d" % (n % 3)], 16 * (n // 3 + 1))
                pool.wait_ge(Z["down_done"], 2 * n - 4)
                split(n % 3)
                pool.wait_ge(Z["bias_ready"], 2 * (n + 1))
                split_lo(n % 3)

        @block.vector
        def _(dve):
            chain = [0]

            def link(ins):
                chain[0] += 1
                ins.then_inc(Z["dve_chain"], 1)
                dve.wait_ge(Z["dve_chain"], chain[0])

            norms = [0]

            def norm(src, dst, t0, done):
                norms[0] += 1
                for i in range(TB):
                    ins = dve.bn_stats(stats[:, i, :], src[:, t0 + i, :])
                link(ins)
                for i in range(TB):
                    ins = dve.bn_aggr(mv[:, i, :], stats[:, i, :])
                link(ins)
                dve.tensor_scalar_add(vareps[:, :], mv[:, :, 1], EPS).then_inc(Z["var_ready"], 1)
                dve.wait_ge(Z["rstd_ready"], norms[0])
                for i in range(TB):
                    dve.tensor_scalar(dst[:, t0 + i, 0:D], src[:, t0 + i, :], mv[:, i, 0:1], rstd[:, i:i + 1],
                                      ALU.subtract, ALU.mult).then_inc(Z[done], 1)

            dve.wait_ge(L["x0"], 16)
            norm(x, xn, 0, "xn_ready")
            dve.wait_ge(L["pack"], 16)
            dve.wait_ge(Z["kT_ready"], 2)
            dve.tensor_copy(khi[:, :, :, :], kT[:, :, :, :]).then_inc(Z["khi_ready"], 1)
            dve.wait_ge(Z["khi_ready"], 1)
            dve.tensor_tensor(klo[:, :, :, :], kT[:, :, :, :], f32(khi[:, :, :, :]), ALU.subtract)\
                .then_inc(Z["klo_ready"], 1)
            dve.tensor_tensor(ka[:, 0, 0:FLAT].rearrange("p (h k) -> p h k", h=HH),
                              f32(khi[:, 0, 0, None, :]).broadcast_to([P, HH, SK]),
                              const("headmask")[:, :, None].broadcast_to([P, HH, SK]), ALU.mult)\
                .then_inc(Z["ka_first"], 1)

            def q_lo(c):
                dve.wait_ge(Z["qhi_ready"], 2 * c + 2)
                dve.scalar_tensor_tensor(qa[HW:P, c % 2, :], bank[HW:P, 6, :], const("bq")[HW:P, c % 2:c % 2 + 1],
                                         f32(qa[HW:P, c % 2, :]), ALU.add, ALU.subtract)\
                    .then_inc(Z["qlo_ready"], 1)

            def maxima(c, i):
                n = c * TB + i
                dve.wait_ge(Z["rough_done"], n + 1)
                dve.tensor_reduce(smax[:, n, :], flat[:, 0:FLAT].rearrange("p (h k) -> p h k", h=HH), AX.X, ALU.max)\
                    .then_inc(Z["max_done"], 1)

            def normalise(c):
                g = c % 2
                dve.wait_ge(Z["o_psum"], c + 1)
                dve.reciprocal(rsum[:, :], bank[HW:P, 5, :]).then_inc(Z["rsum_done"], 1)
                dve.wait_ge(Z["rsum_done"], c + 1)
                if c >= 2:
                    dve.wait_ge(Z["attT_ready"], 1)
                dve.tensor_tensor(att[g * HW:(g + 1) * HW, :], bank[0:HW, 5, :], rsum[:, :], ALU.mult)\
                    .then_inc(Z["att_ready"], 1)

            def residual(b):
                dve.wait_ge(Z["proj_psum"], b + 1)
                dve.wait_ge(Z["xbo_ready"], 1)
                v = x1[:, b * TB:(b + 1) * TB, :].rearrange("p t d -> p (t d)")
                dve.tensor_tensor(v, bank[:, 7, :], v, ALU.add).then_inc(Z["x1_ready"], 1)

            q_lo(0)
            for i in range(TB):
                maxima(0, i)
            dve.wait_ge(L["x1"], 16)
            norm(x, xn, TB, "xn_ready")
            dve.tensor_copy(trib[:, :], const("tri")).then_inc(Z["consts_ready"], 1)
            dve.tensor_copy(groupb[:, :], const("group")).then_inc(Z["consts_ready"], 1)
            for c in range(COMBOS):
                if c:
                    normalise(c - 1)
                if c + 1 < COMBOS:
                    q_lo(c + 1)
                    for i in range(TB):
                        if c == 2 and i == 1:
                            residual(0)
                        maxima(c + 1, i)
                if c == 3:
                    dve.wait_ge(Z["x1_ready"], 1)
                    norm(x1, y0, 0, "y0_ready")
                    dve.wait_ge(Z["y0_ready"], TB)
                    norm(y0, xn, 0, "yh_ready")
                    dve.wait_ge(L["mask"], 16)
                    dve.tensor_scalar(keep[:, :, :], mask[:, :, :], 0.0, None, ALU.is_equal)\
                        .then_inc(Z["keep_ready"], 1)
            normalise(COMBOS - 1)
            residual(1)
            dve.wait_ge(Z["x1_ready"], 2)
            norm(x1, y0, TB, "y0_ready")
            dve.wait_ge(Z["y0_ready"], T)
            dve.wait_ge(Z["logit_psum"], 1)
            gl = bank[:, 6, 0:T * E0].rearrange("p (t e) -> p t e", t=T)
            link(dve.tensor_reduce(small[:, 0, :], gl, AX.X, ALU.max))
            dve.tensor_tensor(lg[:, :, :], gl, small[:, 0, :, None].broadcast_to([P, T, E0]), ALU.subtract)\
                .then_inc(Z["lgsub_ready"], 1)
            norm(y0, xn, TB, "yh_ready")
            dve.wait_ge(Z["lgexp_ready"], 1)
            link(dve.tensor_reduce(small[:, 1, :], lg[:, :, :], AX.X, ALU.add))
            link(dve.reciprocal(small[:, 2, :], small[:, 1, :]))
            dve.tensor_tensor(sc[:, :, :], lg[:, :, :], small[:, 2, :, None].broadcast_to([P, T, E0]), ALU.mult)\
                .then_inc(Z["sc_ready"], 1)
            dve.wait_ge(Z["sc_ready"], 1)
            dve.tensor_copy(screp[:, :, :, :], sc[:, :, :, None].broadcast_to([P, T, E0, P // E0]))\
                .then_inc(Z["screp_ready"], 1)
            dve.memset(prefix[:, :], 0).then_inc(Z["prefix_ready"], 1)
            dve.wait_ge(Z["prefix_ready"], 1)
            dve.wait_ge(Z["srep_ready"], 1)
            for k, shift in enumerate(SHIFTS):
                c = const("cand0") if k == 0 else cand[:, :].bitcast(F32)
                if k:
                    dve.wait_ge(Z["cand_ready"], k)
                dve.tensor_scalar(junk[:, :], srep[:, :], c, 0.0, ALU.is_ge, ALU.add, accum_out=count[:, :])\
                    .then_inc(Z["count_ready"], 1)
                dve.wait_ge(Z["count_ready"], k + 1)
                dve.tensor_scalar(okb[:, :], count[:, :], CAP - 0.5, None, ALU.is_ge).then_inc(Z["ok_ready"], 1)
                dve.wait_ge(Z["nok_psum"], k + 1)
                nok = bank[:, 7, 0:1]
                if k + 1 < len(SHIFTS):
                    dve.tensor_scalar(delta[:, 0:1], nok, float(1 << shift), const("jf")[:, k:k + 1], ALU.mult, ALU.add)\
                        .then_inc(Z["delta_ready"], 1)
                else:
                    dve.tensor_scalar(delta[:, 0:1], nok, -1.0, None, ALU.add).then_inc(Z["delta_ready"], 1)
                dve.tensor_scalar(delta[:, 1:2], nok, -1.0, float(1 << shift), ALU.add, ALU.mult)\
                    .then_inc(Z["delta_ready"], 1)
                dve.wait_ge(Z["delta_ready"], 2 * k + 2)
                if k + 1 < len(SHIFTS):
                    dve.tensor_tensor(cand[:, :], prefix[:, :], delta[:, 0:1], ALU.bitwise_or)\
                        .then_inc(Z["cand_ready"], 1)
                dve.tensor_tensor(prefix[:, :], prefix[:, :], delta[:, 1:2], ALU.bitwise_or)\
                    .then_inc(Z["prefix_ready"], 1)
                dve.wait_ge(Z["prefix_ready"], k + 2)
            dve.wait_ge(Z["thr_psum"], 1)
            link(dve.tensor_copy(thr[:, :], bank[:, 6, 0:P].rearrange("p (e j) -> p e j", e=E0)[:, :, 0]))
            tb = thr[:, None, :].broadcast_to([P, T, E0])
            dve.tensor_tensor(gteq[:, 0], sc[:, :, :], tb, ALU.is_gt).then_inc(Z["gteq_ready"], 1)
            dve.tensor_tensor(gteq[:, 1], sc[:, :, :], tb, ALU.is_equal).then_inc(Z["gteq_ready"], 1)
            dve.wait_ge(Z["pre_psum"], 1)
            dve.tensor_copy(pre[:, :, :, :].rearrange("p k t e -> p (k t e)"), bank[:, 6, 0:2 * T * E0])
            link(dve.tensor_scalar(room[:, :], bank[:, 7, 0:E0], -1.0, float(CAP), ALU.mult, ALU.add))
            rb = room[:, None, :].broadcast_to([P, T, E0])
            link(dve.tensor_tensor(work[:, 0], pre[:, 1], rb, ALU.is_lt))
            link(dve.tensor_tensor(work[:, 1], work[:, 0], gteq[:, 1], ALU.mult))
            link(dve.tensor_tensor(work[:, 0], work[:, 1], gteq[:, 0], ALU.add))
            link(dve.tensor_tensor(work[:, 2], pre[:, 1], rb, ALU.min))
            link(dve.tensor_tensor(work[:, 1], work[:, 2], pre[:, 0], ALU.add))
            link(dve.scalar_tensor_tensor(work[:, 2], work[:, 1], -NOSLOT, work[:, 0], ALU.add, ALU.mult))
            dve.tensor_scalar_add(slot[:, :, :], work[:, 2], NOSLOT).then_inc(Z["slot_ready"], 1)
            dve.wait_ge(Z["slot_ready"], 1)
            dve.wait_ge(Z["yhi_ready"], 2)
            dve.tensor_tensor(ylo[:, :, 0:D], xn[:, :, :], f32(yhi[:, :, 0:D]), ALU.subtract)\
                .then_inc(Z["ylo_ready"], 1)
            dve.tensor_tensor(ylo[:, :, D:GC], sc[:, :, :], f32(yhi[:, :, D:GC]), ALU.subtract)\
                .then_inc(Z["ylo_ready"], 1)
            def picks(e):
                for t in range(T):
                    dve.tensor_scalar(pick[:, t, e, :], const("iota"), slot[:, t, e:e + 1], None, ALU.is_equal)\
                        .then_inc(Z["pick_ready"], 1)

            def low_out(e):
                dve.wait_ge(Z["ohi_ready"], e + 1)
                dve.scalar_tensor_tensor(olo[:, e, :], bank[:, 5, 0:D], yg[:, e, D + e:D + e + 1], f32(ohi[:, e, :]),
                                         ALU.mult, ALU.subtract).then_inc(Z["olo_ready"], 1)

            def keep_picks(e):
                dve.wait_ge(Z["pickT_psum"], 2 * e + 2)
                dve.tensor_copy(pickT[:, e, S:], bank[:, 7, :]).then_inc(Z["pickT_ready"], 1)

            picks(0)
            picks(1)
            keep_picks(0)
            for e in range(E0):
                if e + 2 < E0:
                    picks(e + 2)
                if e + 1 < E0:
                    keep_picks(e + 1)
                if e:
                    low_out(e - 1)
            low_out(E0 - 1)
            for b in range(B):
                dve.wait_ge(Z["res_ready"], 1)
                dve.wait_ge(Z["scat_psum"], b + 1)
                t0 = b * TB
                dve.tensor_tensor(x2[:, t0:t0 + TB, :].rearrange("p t d -> p (t d)"), bank[:, b, :],
                                  res[:, t0:t0 + TB, :].rearrange("p t d -> p (t d)"), ALU.add)\
                    .then_inc(Z["x2_ready"], 1)
                dve.wait_ge(Z["x2_ready"], b + 1)
                norm(x2, xn, t0, "y2_ready")
                dve.wait_ge(Z["s1_psum"], b + 1)
                dve.wait_ge(Z["keep_ready"], 1)
                dve.wait_ge(Z["pad_zero"], 2)
                dve.copy_predicated(sm[:, t0:t0 + 3, :], keep[:, t0:t0 + 3, :],
                                    bank[:, 3, 0:3 * SK].rearrange("p (t k) -> p t k", t=3))
                link(dve.copy_predicated(sm[:, t0 + 3, :], keep[:, t0 + 3, :], bank[:, 4, 0:SK]))
                dve.tensor_reduce(negmax[:, t0:t0 + TB], sm[:, t0:t0 + TB, :], AX.X, ALU.max, negate=True)\
                    .then_inc(Z["negmax_ready"], 1)
                dve.wait_ge(Z["p1_ready"], TB * (b + 1))
                link(dve.scalar_tensor_tensor(srec[:, t0:t0 + TB], negmax[:, t0:t0 + TB], -MASKED,
                                              ssum[:, t0:t0 + TB], ALU.is_lt, ALU.mult))
                link(dve.reciprocal(srec[:, t0:t0 + TB], srec[:, t0:t0 + TB]))
                for t in range(t0, t0 + TB):
                    dve.tensor_scalar(sm[:, t, :], sm[:, t, :], srec[:, t:t + 1], None, ALU.mult)\
                        .then_inc(Z["p1n_ready"], 1)
                dve.wait_ge(Z["o1_psum"], b + 1)
                dve.tensor_tensor(x3[:, t0:t0 + TB, :].rearrange("p t d -> p (t d)"), bank[:, 3, :],
                                  x2[:, t0:t0 + TB, :].rearrange("p t d -> p (t d)"), ALU.add)\
                    .then_inc(Z["x3_ready"], 1)
                dve.wait_ge(Z["x3_ready"], b + 1)
                norm(x3, y0, t0, "y3_ready")
                dve.wait_ge(Z["y3T_ready"], b + 1)
                cs = slice(b * S, (b + 1) * S)
                dve.tensor_copy(y3hi[:, cs], xnT[:, cs]).then_inc(Z["y3hi_ready"], 1)
                dve.wait_ge(Z["y3hi_ready"], b + 1)
                dve.tensor_tensor(y3lo[:, cs], xnT[:, cs], f32(y3hi[:, cs]), ALU.subtract).then_inc(Z["y3lo_ready"], 1)
            dve.wait_ge(Z["ex_ready"], 1)
            link(dve.tensor_scalar_add(ex[:, :, :], ex[:, :, :], 1.0))
            link(dve.reciprocal(aff[:, :, :], ex[:, :, :]))
            for t in range(T):
                ins = dve.max(top8[:, t, :], aff[:, t, :])
            link(ins)
            for t in range(T):
                ins = dve.match_replace(left[:, t, :], top8[:, t, :], aff[:, t, :], -1.0)
            link(ins)
            link(dve.scalar_tensor_tensor(wsel[:, :, :], left[:, :, :], 0.0, aff[:, :, :], ALU.is_lt, ALU.mult))
            link(dve.tensor_reduce(wsum[:, 0, :], wsel[:, :, :], AX.X, ALU.add))
            link(dve.tensor_scalar_add(wsum[:, 0, :], wsum[:, 0, :], 1e-9))
            link(dve.reciprocal(wsum[:, 1, :], wsum[:, 0, :]))
            dve.tensor_tensor(wsel[:, :, :], wsel[:, :, :], wsum[:, 1, :, None].broadcast_to([P, T, E1]), ALU.mult)\
                .then_inc(Z["wsel_ready"], 1)
            dve.wait_ge(Z["wT_ready"], 2)
            dve.tensor_copy(w3[0:E1, :], wT[:, :]).then_inc(Z["w3_ready"], 1)
            dve.wait_ge(Z["w3_ready"], 1)
            dve.tensor_tensor(w3[E1:2 * E1, :], wT[:, :], f32(w3[0:E1, :]), ALU.subtract).then_inc(Z["w3_ready"], 1)
            def hidden(k, c, u, first=False):
                dve.wait_ge(Z["sil_ready"], k + 1)
                dve.wait_ge(Z["upw_psum"], k + 1)
                dve.scalar_tensor_tensor(gu[:, c, :], bank[:, 2 + c, :], bias[:, u, 1:2], sil[:, c, :],
                                         ALU.add, ALU.mult).then_inc(Z["gu_ready"], 1)
                if not first:
                    low_hidden(k - 1, 1 - c)
                dve.wait_ge(Z["gu_ready"], k + 1)
                dve.tensor_tensor(hh[:, c, :], gu[:, c, :], bank[:, 4 + c, :], ALU.mult).then_inc(Z["hh_ready"], 1)

            def low_hidden(k, c):
                dve.wait_ge(Z["hhi_ready"], k + 1)
                dve.tensor_tensor(hlo[:, c, :], hh[:, c, :], f32(hhi[:, c, :]), ALU.subtract)\
                    .then_inc(Z["hlo_ready"], 1)

            hidden(0, 0, 0, first=True)
            hidden(1, 1, 0)
            with dve.Fori(0, LOOPS) as m:
                for u in range(3):
                    for c in range(2):
                        hidden(m * 6 + (2 * u + 2 + c), c, (u + 1) % 3)
            hidden(2 * PAIRS - 2, 0, (PAIRS - 1) % 3)
            hidden(2 * PAIRS - 1, 1, (PAIRS - 1) % 3)
            low_hidden(2 * PAIRS - 1, 1)
            for b in range(B):
                dve.wait_ge(Z["outT_psum"], b + 1)
                dve.tensor_tensor(out[:, b * TB:(b + 1) * TB, :].rearrange("p t d -> p (t d)"), bank[:, b, :],
                                  x3[:, b * TB:(b + 1) * TB, :].rearrange("p t d -> p (t d)"), ALU.add)\
                    .then_inc(Z["out_ready"], 1)

        @block.scalar
        def _(act):
            act.dma_start(pack[:, :], pack_d).then_inc(L["pack"], 16)
            act.dma_start(ctx2[:, :, :], ctx2_d).then_inc(L["ctx2"], 16)
            act.dma_start(ind, ind_d).then_inc(L["ind"], 16)
            act.wait_ge(L["pack"], 16)
            for g in range(2):
                act.wait_ge(Z["k_psum"], g + 1)
                act.activation(kT[:, g, :, :].rearrange("p b k -> p (b k)"), bank[:, 3 + g, 0:B * SK], ACT.Identity,
                               bias=const("bk")[:, g:g + 1]).then_inc(Z["kT_ready"], 1)

            def turned(b):
                act.wait_ge(Z["xnT_psum"], b + 1)
                act.copy(xnT[:, b * S:(b + 1) * S], bank[:, 6, :]).then_inc(Z["xnT_ready"], 1)

            def queries(c):
                act.wait_ge(Z["q_psum"], c + 1)
                bq = const("bq")[:, c % 2:c % 2 + 1]
                act.activation(qa[:, c % 2, :], bank[:, 6, :], ACT.Identity, bias=bq).then_inc(Z["qhi_ready"], 1)
                act.activation(qb[0:HW, c % 2, :], bank[0:HW, 6, :], ACT.Identity, bias=bq[0:HW])\
                    .then_inc(Z["qhi_ready"], 1)

            def values(b, r):
                if b and r == 0:
                    act.wait_ge(Z["vaug_ready"], 2 * b)
                i0, i1 = VGROUPS[r]
                act.wait_ge(Z["v_psum"], 3 * b + r + 1)
                act.copy(vraw[:, i0:i1, :].rearrange("p i d -> p (i d)"), bank[:, 6, 0:(i1 - i0) * P])\
                    .then_inc(Z["vraw_ready"], 1)

            def minus_max(c):
                act.wait_ge(Z["mT_psum"], c + 1)
                act.mul(qb[HW:HW + HH, c % 2, :], bank[0:HH, 7, :], -1.0).then_inc(Z["mT_ready"], 1)

            def with_bias(b):
                act.wait_ge(Z["att_ready"], 2 * (b + 1))
                act.activation(attT[:, :], att[:, :], ACT.Identity, bias=const("bv")).then_inc(Z["attT_ready"], 1)

            turned(0)
            queries(0)
            for r in range(3):
                values(0, r)
            minus_max(0)
            for c in range(COMBOS):
                for i in range(NBLK):
                    n = c * NBLK + i
                    act.wait_ge(Z["score_psum"], n + 1)
                    if n >= 3:
                        act.wait_ge(*((Z["o_psum"], (n - 2) // NBLK) if (n - 2) % NBLK == 0 else
                                      (Z["pv_done"], n - 2 - (n - 3) // NBLK)))
                    elif n == 0:
                        act.wait_ge(Z["kb_ind"], 2)
                    act.activation(pT[:, n % 3, :], bank[:, 3 + n % 2, :], ACT.Exp, scale=float(DH) ** -0.5)\
                        .then_inc(Z["exp_done"], 1)
                    if c + 1 < COMBOS and i == 0:
                        queries(c + 1)
                    if c == 0 and i == 4:
                        turned(1)
                    if c == 1 and i in (2, 4, 6):
                        values(1, i // 2 - 1)
                    if c == 2 and i == 1:
                        with_bias(0)
                    if c + 1 < COMBOS and i == 8:
                        minus_max(c + 1)
            with_bias(1)

            for b in range(B):
                act.wait_ge(Z["y0T_psum"], b + 1)
                act.copy(xnT[:, b * S:(b + 1) * S], bank[:, b, :]).then_inc(Z["y0T_ready"], 1)
            act.wait_ge(Z["lgsub_ready"], 1)
            act.activation(lg[:, :, :], lg[:, :, :], ACT.Exp).then_inc(Z["lgexp_ready"], 1)
            act.wait_ge(Z["srep_psum"], 1)
            act.copy(srep[:, :], flat[:, 2 * 512:4 * 512]).then_inc(Z["srep_ready"], 1)
            act.wait_ge(Z["yh_ready"], T)
            act.copy(yhi[:, :, 0:D], xn[:, :, :]).then_inc(Z["yhi_ready"], 1)
            act.wait_ge(Z["sc_ready"], 1)
            act.copy(yhi[:, :, D:GC], sc[:, :, :]).then_inc(Z["yhi_ready"], 1)

            def gathered(e):
                act.wait_ge(Z["gath_psum"], e + 1)
                act.copy(yg[:, e, :], bank[:, e % 2, 0:GC]).then_inc(Z["yg_ready"], 1)
                act.wait_ge(Z["pickT_psum"], 2 * e + 1)
                act.copy(pickT[:, e, 0:S], bank[:, 6, :]).then_inc(Z["pickT_ready"], 1)

            def high_out(e):
                act.wait_ge(Z["fc2_psum"], e + 1)
                act.activation(ohi[:, e, :], bank[:, 5, 0:D], ACT.Copy, scale=yg[:, e, D + e:D + e + 1])\
                    .then_inc(Z["ohi_ready"], 1)

            gathered(0)
            for e in range(E0):
                if e + 1 < E0:
                    gathered(e + 1)
                act.wait_ge(Z["ygT_psum"], e + 1)
                act.activation(ygT[:, e % 2, :], bank[:, 2, 0:P], ACT.Identity, bias=const("ln_b"),
                               scale=const("ln_w")).then_inc(Z["ygT_ready"], 1)
                act.wait_ge(Z["fc1_psum"], e + 1)
                for f in range(FT):
                    act.activation(hid[:, e % 2, f, :], bank[:, 3 + e % 2, f * P:(f + 1) * P], ACT.Gelu_apprx_tanh,
                                   bias=b1[:, e, f:f + 1]).then_inc(Z["hid_ready"], 1)
                if e:
                    high_out(e - 1)
            high_out(E0 - 1)

            for b in range(B):
                t0, cs = b * TB, slice(b * S, (b + 1) * S)
                act.wait_ge(Z["y2T_psum"], b + 1)
                act.copy(xnT[:, cs], bank[:, 2, :]).then_inc(Z["y2T_ready"], 1)
                act.wait_ge(Z["negmax_ready"], b + 1)
                for t in range(t0, t0 + TB):
                    act.activation(sm[:, t, :], sm[:, t, :], ACT.Exp, bias=negmax[:, t:t + 1],
                                   accum_out=ssum[:, t:t + 1]).then_inc(Z["p1_ready"], 1)
                act.wait_ge(Z["p1T_psum"], b + 1)
                act.copy(pTa[:, :], bank[:, 5, :]).then_inc(Z["p1T_ready"], 1)
                act.copy(pTb[:, :], bank[0:SK - P, 6, :]).then_inc(Z["p1T_ready"], 1)
                act.wait_ge(Z["co_psum"], b + 1)
                act.copy(coT[:, :], bank[:, 7, :]).then_inc(Z["co_ready"], 1)
                act.wait_ge(Z["y3T_psum"], b + 1)
                act.copy(xnT[:, cs], bank[:, 2, :]).then_inc(Z["y3T_ready"], 1)
            act.wait_ge(Z["lr_psum"], 1)
            act.activation(ex[:, :, :].rearrange("p t e -> p (t e)"), bank[:, 4, 0:T * E1], ACT.Exp, scale=-1.0)\
                .then_inc(Z["ex_ready"], 1)
            for b in range(B):
                act.wait_ge(Z["wT_psum"], b + 1)
                act.copy(wT[:, b * S:(b + 1) * S], bank[0:E1, 5 + b, :]).then_inc(Z["wT_ready"], 1)

            def silu(k, c, u):
                act.wait_ge(Z["gate_psum"], k + 1)
                act.activation(sil[:, c, :], bank[:, c, :], ACT.Silu, bias=bias[:, u, 0:1]).then_inc(Z["sil_ready"], 1)

            def high_hidden(k, c, free=True):
                act.wait_ge(Z["hh_ready"], k + 1)
                if free:
                    act.wait_ge(Z["down_done"], k - 1)
                act.copy(hhi[:, c, :], hh[:, c, :]).then_inc(Z["hhi_ready"], 1)

            def act_step(k, c, u, free=True):
                act.wait_ge(Z["hh_ready"], k - 1)
                silu(k, c, u)
                high_hidden(k - 1, 1 - c, free)

            silu(0, 0, 0)
            silu(1, 1, 0)
            high_hidden(0, 0, free=False)
            act_step(2, 0, 1, free=False)
            with act.Fori(0, LOOPS) as m:
                for u in range(3):
                    for c in range(2):
                        act_step(m * 6 + (2 * u + 3 + c), 1 - c, (u + 1 + c) % 3)
            act_step(2 * PAIRS - 1, 1, (PAIRS - 1) % 3)
            high_hidden(2 * PAIRS - 1, 1)
            for b in range(B):
                if b == 0:
                    act.wait_ge(Z["down_done"], 2 * PAIRS - 1)
                else:
                    act.wait_ge(Z["y_psum"], 1)
                act.activation(yT[:, b * S:(b + 1) * S], bank[:, 6 + b, :], ACT.Identity, bias=const("bd_s"))\
                    .then_inc(Z["yT_ready"], 1)

        @block.tensor
        def _(pe):
            def turn(dst, src, n=P):
                return pe.transpose(dst, src, ident[0:n, 0:n])

            free6 = [None]

            def take6(sem_, count):
                if free6[0]:
                    pe.wait_ge(*free6[0])
                free6[0] = (sem_, count)

            pe.wait_ge(L["ctx2"], 16)
            pe.wait_ge(L["watt"], 16)
            for g in range(2):
                pe.matmul(bank[:, 3 + g, 0:B * SK], watt[:, 2 + g, :], ctx2[:, :, 0:SK], start=True, stop=True)\
                    .then_inc(Z["k_psum"], 1)
            pe.wait_ge(L["pack"], 16)

            def turned(b):
                take6(Z["xnT_ready"], b + 1)
                pe.wait_ge(Z["xn_ready"], TB * (b + 1))
                for i in range(TB):
                    ins = turn(bank[:, 6, i * P:(i + 1) * P], xn[:, b * TB + i, :])
                ins.then_inc(Z["xnT_psum"], 1)

            def queries(c):
                b, g = c // 2, c % 2
                take6(Z["qlo_ready"], c + 1)
                pe.wait_ge(Z["xnT_ready"], b + 1)
                pe.matmul(bank[:, 6, :], watt[:, g, :], xnT[:, b * S:(b + 1) * S], start=True, stop=True)\
                    .then_inc(Z["q_psum"], 1)

            def values(b, r):
                take6(Z["vraw_ready"], 3 * b + r + 1)
                i0, i1 = VGROUPS[r]
                for i in range(i0, i1):
                    o = (P * i) % SK
                    ins = pe.matmul(bank[:, 6, (i - i0) * D:(i - i0 + 1) * D], ctx2[:, b, o:o + P], watt[:, 4, :],
                                    start=True, stop=True)
                ins.then_inc(Z["v_psum"], 1)

            chunks = ((0, 512), (512, 1024), (1024, FLAT))

            def rough(c, i):
                n = c * TB + i
                if n:
                    pe.wait_ge(Z["max_done"], n)
                if i == 0:
                    pe.wait_ge(Z["qlo_ready"], c + 1)
                    if c:
                        pe.wait_ge(Z["expanded"], 2 * c)
                    else:
                        pe.wait_ge(Z["ka_first"], 1)
                for c0, c1 in chunks:
                    ins = pe.matmul(flat[:, c0:c1], qa[:, c % 2, i * P:(i + 1) * P], ka[:, c % 2, c0:c1],
                                    start=True, stop=True)
                ins.then_inc(Z["rough_done"], 1)

            def maxima(c):
                pe.wait_ge(Z["max_done"], TB * (c + 1))
                if c:
                    pe.wait_ge(Z["mT_ready"], c)
                if c == 3:
                    pe.wait_ge(Z["x1_ready"], 1)
                for i in range(TB):
                    ins = turn(bank[0:HH, 7, i * P:(i + 1) * P], smax[:, c * TB + i, :])
                ins.then_inc(Z["mT_psum"], 1)

            def scores(c, i):
                n = c * NBLK + i
                if n >= 2:
                    pe.wait_ge(Z["exp_done"], n - 1)
                if i == 0:
                    pe.wait_ge(Z["qhi_ready"], 2 * c + 2)
                    pe.wait_ge(Z["mT_ready"], c + 1)
                    pe.wait_ge(Z["expanded"], 2 * c + 1)
                    if c == 0:
                        pe.wait_ge(Z["kb_ind"], 2)
                        pe.wait_ge(Z["pad_zero"], 2)
                cols = slice(i * P, (i + 1) * P)
                pe.matmul(bank[:, 3 + n % 2, :], ka[:, c % 2, cols], qa[:, c % 2, :], start=True, stop=False)
                pe.matmul(bank[:, 3 + n % 2, :], kb[0:HW + HH, c % 2, cols], qb[0:HW + HH, c % 2, :],
                          start=False, stop=True).then_inc(Z["score_psum"], 1)

            def attend(c, i):
                b, g, n = c // 2, c % 2, c * NBLK + i
                if i == 0:
                    pe.wait_ge(Z["vaug_ready"], 2 * (b + 1))
                    pe.wait_ge(Z["pad_zero"], 2 + 2 * (b + 1))
                    if c:
                        pe.wait_ge(Z["att_ready"], c)
                pe.wait_ge(Z["exp_done"], n + 1)
                ins = pe.matmul(bank[:, 5, :], vaug[:, b, g, i, :], pT[:, n % 3, :], start=(i == 0),
                                stop=(i == NBLK - 1))
                ins.then_inc(Z["o_psum"] if i == NBLK - 1 else Z["pv_done"], 1)

            def project(b):
                pe.wait_ge(Z["attT_ready"], b + 1)
                pe.wait_ge(Z["mT_ready"], 3 if b == 0 else 4)
                for i in range(TB):
                    ins = pe.matmul(bank[:, 7, i * P:(i + 1) * P], attT[:, i * P:(i + 1) * P], watt[:, 5, :],
                                    start=True, stop=True)
                ins.then_inc(Z["proj_psum"], 1)

            turned(0)
            queries(0)
            for r in range(3):
                values(0, r)
            for i in range(TB):
                rough(0, i)
            maxima(0)
            scores(0, 0)
            for c in range(COMBOS):
                for i in range(NBLK):
                    if c * NBLK + i + 1 < COMBOS * NBLK:
                        scores(c + (i + 1) // NBLK, (i + 1) % NBLK)
                    if c + 1 < COMBOS:
                        if i == 0:
                            queries(c + 1)
                        if i in (1, 3, 5, 7):
                            rough(c + 1, i // 2)
                        if i == 8:
                            maxima(c + 1)
                    if c == 0 and i == 4:
                        turned(1)
                    if c == 1 and i in (2, 4, 6):
                        values(1, i // 2 - 1)
                    if c == 2 and i == 2:
                        project(0)
                    attend(c, i)
            project(1)

            for b in range(B):
                pe.wait_ge(Z["y0_ready"], TB * (b + 1))
                for i in range(TB):
                    ins = turn(bank[:, b, i * P:(i + 1) * P], y0[:, b * TB + i, :])
                ins.then_inc(Z["y0T_psum"], 1)
            pe.wait_ge(L["gate"], 16)
            pe.wait_ge(Z["y0T_ready"], 2)
            for t in range(T):
                ins = pe.matmul(bank[:, 6, t * E0:(t + 1) * E0], xnT[:, t * P:(t + 1) * P], gate[:, :],
                                start=True, stop=True)
            ins.then_inc(Z["logit_psum"], 1)
            pe.wait_ge(Z["screp_ready"], 1)
            for t in range(T):
                ins = turn(flat[:, 2 * 512 + t * P:2 * 512 + (t + 1) * P],
                           screp[:, t].rearrange("p e j -> p (e j)"))
            ins.then_inc(Z["srep_psum"], 1)
            pe.wait_ge(Z["consts_ready"], 5)
            pe.wait_ge(Z["x1_ready"], 2)
            for k in range(len(SHIFTS)):
                pe.wait_ge(Z["ok_ready"], k + 1)
                if k:
                    pe.wait_ge(Z["delta_ready"], 2 * k)
                pe.matmul(bank[:, 7, 0:1], groupb[:, :], okb[:, :], start=True, stop=True).then_inc(Z["nok_psum"], 1)
            pe.wait_ge(Z["prefix_ready"], len(SHIFTS) + 1)
            turn(bank[:, 6, 0:P], prefix[:, :].bitcast(F32).broadcast_to([P, P])).then_inc(Z["thr_psum"], 1)
            pe.wait_ge(Z["gteq_ready"], 2)
            pv = bank[:, 6, 0:2 * T * E0].rearrange("p (k t e) -> p k t e", k=2, t=T)
            pe.matmul(bank[:, 6, 0:2 * T * E0], trib[:, :], gteq[:, :, :, :].rearrange("p k t e -> p (k t e)"),
                      start=True, stop=False)
            for t in range(T - 1):
                n = T - 1 - t
                for k in range(2):
                    pe.matmul(pv[:, k, t + 1:, :], onesb[:, :], gteq[:, k, t, None, :].broadcast_to([P, n, E0]),
                              start=False, stop=(t == T - 2 and k == 1))
            for t in range(T):
                ins = pe.matmul(bank[:, 7, 0:E0], onesb[:, :], gteq[:, 0, t, :], start=(t == 0), stop=(t == T - 1))
            ins.then_inc(Z["pre_psum"], 1)

            pe.wait_ge(L["fc1"], 16)
            pe.wait_ge(L["fc2"], 16)
            pe.wait_ge(L["rows"], 16)
            pe.wait_ge(Z["slot_ready"], 1)
            pe.wait_ge(Z["ylo_ready"], 2)

            def gather(e):
                pe.wait_ge(Z["pick_ready"], T * (e + 1))
                if e >= 2:
                    pe.wait_ge(Z["yg_ready"], e - 1)
                for t in range(T):
                    pe.matmul(bank[:, e % 2, 0:GC], pick[:, t, e, :], yhi[:, t, :], start=(t == 0), stop=False)
                    ins = pe.matmul(bank[:, e % 2, 0:GC], pick[:, t, e, :], ylo[:, t, :], start=False,
                                    stop=(t == T - 1))
                ins.then_inc(Z["gath_psum"], 1)
                for b in range(B):
                    if e:
                        pe.wait_ge(Z["pickT_ready"], 2 * e)
                    for i in range(TB):
                        ins = turn(bank[:, 6 + b, i * P:(i + 1) * P], f32(pick[:, b * TB + i, e, :]))
                    ins.then_inc(Z["pickT_psum"], 1)

            def first_layer(e):
                pe.wait_ge(Z["yg_ready"], e + 1)
                if e:
                    pe.wait_ge(Z["ygT_ready"], e)
                turn(bank[:, 2, 0:P], yg[:, e, 0:D]).then_inc(Z["ygT_psum"], 1)
                pe.wait_ge(Z["ygT_ready"], e + 1)
                if e >= 2:
                    pe.wait_ge(Z["hid_ready"], FT * (e - 1))
                for f in range(FT):
                    ins = pe.matmul(bank[:, 3 + e % 2, f * P:(f + 1) * P], fc1[:, e, f * P:(f + 1) * P],
                                    ygT[:, e % 2, :], start=True, stop=True)
                ins.then_inc(Z["fc1_psum"], 1)

            def second_layer(e):
                pe.wait_ge(Z["hid_ready"], FT * (e + 1))
                if e:
                    pe.wait_ge(Z["olo_ready"], e)
                pe.matmul(bank[:, 5, 0:D], onesrow[:, :], rows[0:1, e * D:(e + 1) * D], start=True, stop=False)
                for f in range(FT):
                    ins = pe.matmul(bank[:, 5, 0:D], hid[:, e % 2, f, :], fc2[:, e, f, :], start=False,
                                    stop=(f == FT - 1))
                ins.then_inc(Z["fc2_psum"], 1)

            gather(0)
            for e in range(E0):
                if e + 1 < E0:
                    gather(e + 1)
                first_layer(e)
                if e:
                    second_layer(e - 1)
            second_layer(E0 - 1)
            pe.wait_ge(Z["pickT_ready"], 2 * E0)
            pe.wait_ge(Z["olo_ready"], E0)
            for b in range(B):
                for i in range(TB):
                    t = b * TB + i
                    for e in range(E0):
                        pe.matmul(bank[:, b, i * P:(i + 1) * P], pickT[:, e, t * P:(t + 1) * P], ohi[:, e, :],
                                  start=(e == 0), stop=False)
                        ins = pe.matmul(bank[:, b, i * P:(i + 1) * P], pickT[:, e, t * P:(t + 1) * P], olo[:, e, :],
                                        start=False, stop=(e == E0 - 1))
                ins.then_inc(Z["scat_psum"], 1)

            pe.wait_ge(L["wout"], 16)
            pe.wait_ge(L["ctxa"], 16)
            pe.wait_ge(L["ctxb"], 16)
            pe.wait_ge(L["wr"], 16)
            for b in range(B):
                t0, cs = b * TB, slice(b * S, (b + 1) * S)
                pe.wait_ge(Z["y2_ready"], TB * (b + 1))
                for i in range(TB):
                    ins = turn(bank[:, 2, i * P:(i + 1) * P], xn[:, t0 + i, :])
                ins.then_inc(Z["y2T_psum"], 1)
                pe.wait_ge(Z["y2T_ready"], b + 1)
                if b:
                    pe.wait_ge(Z["x3_ready"], b)
                for i in range(TB):
                    d = bank[:, 3, i * SK:(i + 1) * SK] if i < 3 else bank[:, 4, 0:SK]
                    ins = pe.matmul(d, xnT[:, (t0 + i) * P:(t0 + i + 1) * P], ctx2[:, b, 0:SK], start=True, stop=True)
                ins.then_inc(Z["s1_psum"], 1)
                pe.wait_ge(Z["p1n_ready"], TB * (b + 1))
                for i in range(TB):
                    turn(bank[:, 5, i * P:(i + 1) * P], sm[:, t0 + i, 0:P])
                    ins = turn(bank[0:SK - P, 6, i * P:(i + 1) * P], sm[:, t0 + i, P:SK])
                ins.then_inc(Z["p1T_psum"], 1)
                pe.wait_ge(Z["p1T_ready"], 2 * (b + 1))
                pe.matmul(bank[:, 7, :], ctxa[:, b, :], pTa[:, :], start=True, stop=False)
                pe.matmul(bank[:, 7, :], ctxb[:, b, :], pTb[:, :], start=False, stop=True).then_inc(Z["co_psum"], 1)
                pe.wait_ge(Z["co_ready"], b + 1)
                for i in range(TB):
                    pe.matmul(bank[:, 3, i * P:(i + 1) * P], coT[:, i * P:(i + 1) * P], wout[:, 0, :],
                              start=True, stop=False)
                    ins = pe.matmul(bank[:, 3, i * P:(i + 1) * P], xnT[:, (t0 + i) * P:(t0 + i + 1) * P],
                                    wout[:, 1, :], start=False, stop=True)
                ins.then_inc(Z["o1_psum"], 1)
                pe.wait_ge(Z["y3_ready"], TB * (b + 1))
                for i in range(TB):
                    ins = turn(bank[:, 2, i * P:(i + 1) * P], y0[:, t0 + i, :])
                ins.then_inc(Z["y3T_psum"], 1)
                pe.wait_ge(Z["y3T_ready"], b + 1)
            for t in range(T):
                d = bank[:, 4, t * E1:(t + 1) * E1]
                pe.matmul(d, onesrow[:, :], br_row, start=True, stop=False)
                ins = pe.matmul(d, xnT[:, t * P:(t + 1) * P], wr[:, :], start=False, stop=True)
            ins.then_inc(Z["lr_psum"], 1)
            pe.wait_ge(Z["wsel_ready"], 1)
            for b in range(B):
                for i in range(TB):
                    ins = turn(bank[0:E1, 5 + b, i * P:(i + 1) * P], wsel[:, b * TB + i, :])
                ins.then_inc(Z["wT_psum"], 1)
            pe.wait_ge(Z["w3_ready"], 2)
            pe.wait_ge(Z["w3ones_ready"], 1)
            pe.wait_ge(Z["y3lo_ready"], 2)

            def gate_up(c, u):
                cs = slice(c * S, (c + 1) * S)
                for j in range(2):
                    w = slice(j * P, (j + 1) * P)
                    d = bank[:, 2 * j + c, :]
                    pe.matmul(d, whi[:, u, w], y3hi[:, cs], start=True, stop=False)
                    pe.matmul(d, whi[:, u, w], y3lo[:, cs], start=False, stop=False)
                    ins = pe.matmul(d, wlo[:, u, w], y3hi[:, cs], start=False, stop=True)
                    if j == 0:
                        ins.then_inc(Z["gate_psum"], 1)
                pe.matmul(bank[:, 4 + c, :], whi[0:3 * E1, u, 3 * P:GW], w3[:, cs], start=True, stop=True)\
                    .then_inc(Z["upw_psum"], 1)

            pe.wait_ge(L["bd"], 16)
            for b in range(B):
                pe.matmul(bank[:, 6 + b, :], bd[:, :], wT[:, b * S:(b + 1) * S], start=True, stop=False,
                          skip_group_check=True)

            def down(k, c, u, last=False):
                pe.wait_ge(Z["hhi_ready"], k + 1)
                w = slice(2 * P, 3 * P)
                d = bank[:, 6 + c, :]
                pe.matmul(d, whi[:, u, w], hhi[:, c, :], start=False, stop=False, skip_group_check=True)
                pe.matmul(d, wlo[:, u, w], hhi[:, c, :], start=False, stop=False, skip_group_check=True)
                pe.wait_ge(Z["hlo_ready"], k + 1)
                ins = pe.matmul(d, whi[:, u, w], hlo[:, c, :], start=False, stop=last, skip_group_check=True)
                ins.then_inc(Z["y_psum"] if last else Z["down_done"], 1)

            pe.wait_ge(Z["split_ready"], 1)
            gate_up(0, 0)
            gate_up(1, 0)
            with pe.Fori(0, LOOPS) as m:
                for u in range(3):
                    for c in range(2):
                        k = m * 6 + (2 * u + 2 + c)
                        if c == 0:
                            pe.wait_ge(Z["split_ready"], m * 3 + (u + 2))
                        pe.wait_ge(Z["hh_ready"], k - 1)
                        gate_up(c, (u + 1) % 3)
                        down(k - 2, c, u)
            u = (PAIRS - 1) % 3
            pe.wait_ge(Z["split_ready"], PAIRS)
            for c in range(2):
                pe.wait_ge(Z["hh_ready"], 2 * PAIRS - 3 + c)
                gate_up(c, u)
                down(2 * PAIRS - 4 + c, c, (u + 2) % 3)
            down(2 * PAIRS - 2, 0, u)
            down(2 * PAIRS - 1, 1, u, last=True)
            for b in range(B):
                pe.wait_ge(Z["yT_ready"], b + 1)
                for i in range(TB):
                    c = (b * TB + i) * P
                    ins = turn(bank[:, b, i * P:(i + 1) * P], yT[:, c:c + P])
                ins.then_inc(Z["outT_psum"], 1)


def constants():
    p = np.arange(P)
    c = {"ident": np.eye(P)}
    c["headmask"] = (p[:, None] % (HH * DH) // DH == np.arange(HH)).astype(np.float32)
    pair = P * np.arange(NBLK)[None, :, None] + p[:, None, None]
    c["vmask"] = (pair // SK == np.arange(HH)).astype(np.float32).reshape(P, NBLK * HH)
    c["tri"] = (p[:, None] < p[None, :]).astype(np.float32)
    c["group"] = (p[:, None] // 16 == p[None, :] // 16).astype(np.float32)
    c["iota"] = np.broadcast_to(p[None, :], (P, P))
    j = (p % 16).astype(np.float64)
    jf = np.zeros((P, len(SHIFTS)))
    for k in range(len(SHIFTS) - 1):
        jf[:, k] = j * 2.0 ** SHIFTS[k + 1] - 2.0 ** SHIFTS[k]
    c["jf"] = jf
    c["cand0"] = (np.minimum(p % 16, 4).astype(np.int64) << SHIFTS[0]).astype(np.int32).view(np.float32)[:, None]
    sel = np.zeros((PAIRS, P, P), np.float32)
    sel[0, 2 * E1, 0:I1] = 1
    for q in range(1, PAIRS):
        for h in range(2):
            e = 2 * (q - 1) + h
            sel[q, e, h * I1:(h + 1) * I1] = 1
            sel[q, E1 + e, h * I1:(h + 1) * I1] = 1
    return {k: np.ascontiguousarray(v, dtype=np.float32) for k, v in c.items()}, sel


def kernel(**inputs):
    import concourse.bacc as bacc
    from concourse.bass_utils import run_bass_kernel_spmd as run

    i = {k: np.asarray(v) for k, v in inputs.items()}
    consts, sel = constants()
    col = lambda v: v.reshape(-1, 1)
    ctx = i["ctx_1024"]
    ctxT = ctx.transpose(2, 0, 1)
    twice = lambda v, g: np.concatenate([v[g * HW:(g + 1) * HW]] * 2)
    ind = (np.arange(NBLK * P)[None, :] // SK == np.arange(HH)[:, None]).astype(np.float32)
    vectors = {"bq": np.stack([twice(i["L0_xattn_bq"], g) for g in range(2)], axis=1),
               "bk": np.stack([twice(i["L0_xattn_bk"], g) for g in range(2)], axis=1),
               "bo": np.broadcast_to(i["L0_xattn_bo"], (P, D)), "bv": col(i["L0_xattn_bv"]),
               "ln_w": col(i["L0_ffn_ln_w"]), "ln_b": col(i["L0_ffn_ln_b"]), "bd_s": col(i["L1_ffn_bd_s"]),
               "b1": i["L0_ffn_b1s"].reshape(E0, FT, P).transpose(2, 0, 1).reshape(P, E0 * FT)}
    parts = {**consts, **vectors}
    rec = np.zeros((PAIRS, P, REC), np.float32)
    rec[:, :, 3 * P:GW] = sel
    rec[0, :, 0:I1] = i["L1_ffn_Wg_s"]
    rec[0, :, P:P + I1] = i["L1_ffn_Wu_s"]
    rec[0, 0:I1, 2 * P:3 * P] = i["L1_ffn_Wd_s"]
    rec[0, 0:I1, GW] = i["L1_ffn_bg_s"]
    rec[0, 0:I1, GW + 1] = i["L1_ffn_bu_s"]
    n = PAIRS - 1
    rec[1:, :, 0:P] = i["L1_ffn_Wg"].reshape(n, 2, D, I1).transpose(0, 2, 1, 3).reshape(n, D, P)
    rec[1:, :, P:2 * P] = i["L1_ffn_Wu"].reshape(n, 2, D, I1).transpose(0, 2, 1, 3).reshape(n, D, P)
    rec[1:, :, 2 * P:3 * P] = i["L1_ffn_Wd"].reshape(n, P, D)
    rec[1:, :, GW] = i["L1_ffn_bg"].reshape(n, P)
    rec[1:, :, GW + 1] = i["L1_ffn_bu"].reshape(n, P)
    arrays = {
        "x": i["x"].reshape(T, P, D).transpose(1, 0, 2),
        "ctx2": np.concatenate([ctxT, ctxT], axis=2),
        "ctxk": ctx.transpose(1, 0, 2),
        "mask": i["mask_BxSxS2_bk0"].reshape(T, P, SK).transpose(1, 0, 2),
        "watt": np.stack([twice(i["L0_xattn_W" + n], g).T for n in "qk" for g in range(2)]
                         + [i["L0_xattn_Wv"].T, i["L0_xattn_Wo"].T], axis=1),
        "ind": ind,
        "pack": np.concatenate([parts[n] for n in PACK], axis=1),
        "rows": np.concatenate([i["L0_ffn_b2s"].reshape(-1), i["L1_ffn_br"]])[None, :],
        "gate": i["L0_ffn_gate_w"].T,
        "fc1": i["L0_ffn_fc1s"].transpose(2, 0, 1),
        "fc2": i["L0_ffn_fc2s"].reshape(E0, D, FT, P).transpose(3, 0, 2, 1),
        "wout": i["L1_xattn_W_attn"].reshape(D, 2, D).transpose(2, 1, 0),
        "wr": i["L1_ffn_Wr"],
        "rec": rec,
        "bd": i["L1_ffn_bd"],
    }
    nc = bacc.Bacc("TRN2", target_bir_lowering=False, num_devices=1)
    arrays = {f"in_{k}": np.ascontiguousarray(v) for k, v in arrays.items()}
    args = [nc.dram_tensor(k, v.shape, mybir.dt.from_np(v.dtype), kind="ExternalInput").ap()
            for k, v in arrays.items()]
    out = nc.dram_tensor("out_0", (P, T, D), F32, kind="ExternalOutput").ap()
    build(nc, *args, out)
    r = run(nc, [arrays], core_ids=[0])
    return r.results[0]["out_0"].transpose(1, 0, 2).reshape(B, S, D)
```

```python
from contextlib import ExitStack

import numpy as np
import concourse.bass as bass
from concourse import mybir

P = 128
D = 128
B, S = 2, 512
T = B * S // P
TB = T // B
SK = 154
HEADS, DH = 16, 8
HH = HEADS // 2
FLAT = HH * SK
NBLK = -(-FLAT // P)
HW = HH * DH
COMBOS = 2 * B
E0, F0 = 8, 512
FT = F0 // P
CAP = B * S // E0
E1, I1, TOP = 32, 64, 8
PAIRS = E1 // 2 + 1
LOOPS = PAIRS // 3
GW = 3 * P + P
REC = GW + 2
EPS = 1e-5
ROUGH_AT = (1, 3, 6, 7)
SECOND_PICKS = {0: (0, 2), 1: (2, 5), 2: (5, T)}
VGROUPS = ((0, 4), (4, 8), (8, NBLK))
SHIFTS = [28, 24, 20, 16, 12, 8, 4, 0]
EXACT = 5
MASKED = -3.0e38
NOSLOT = 200.0

F32 = mybir.dt.float32
F32R = mybir.dt.float32r
BF16 = mybir.dt.bfloat16
I32 = mybir.dt.int32
U8 = mybir.dt.uint8
ALU = mybir.AluOpType
ACT = mybir.ActivationFunctionType
AX = mybir.AxisListType

PACK = {}
_at = 0
for _name, _width in (("ident", P), ("headmask", HH), ("vmask", NBLK * HH), ("tri", P), ("group", P),
                      ("iota", P), ("jf", len(SHIFTS)), ("jg", EXACT + 1), ("cand0", 1), ("bo", D), ("bq", 2), ("bk", 2), ("bv", 1),
                      ("ln_w", 1), ("ln_b", 1), ("bd_s", 1), ("b1", E0 * FT), ("esel", E0), ("row", 1)):
    PACK[_name] = (_at, _at + _width)
    _at += _width
NPACK = _at


def build(nc, x_d, ctx2_d, mask_d, watt_d, ind_d, pack_d, rows_d, gate_d, fc1_d, fc2_d, wout_d, wr_d, rec_d,
          bd_d, out_d):
    with ExitStack() as ctx:
        def sb(name, shape, dt=F32):
            return ctx.enter_context(nc.sbuf_tensor(name, shape, dt))

        def sem(name):
            return ctx.enter_context(nc.semaphore(name))

        def lay(base, names, parts=P):
            out, at = [], 0
            for shape in names:
                n = int(np.prod(shape[1:]))
                v = base[0:shape[0], at:at + n]
                ax = "abcd"[:len(shape) - 1]
                if len(shape) > 2:
                    v = v.rearrange(f"p ({' '.join(ax)}) -> p {' '.join(ax)}",
                                    **{a: m for a, m in zip(ax, shape[1:])})
                out.append(v)
                at += n
            assert at <= base.shape[1], (at, base.shape)
            return out

        bank = ctx.enter_context(nc.psum_tensor("bank", [P, 8, 512], F32))
        flat = bank[:, :, :].rearrange("p b c -> p (b c)")

        x = sb("x", [P, T, D])
        ctx2 = sb("ctx2", [P, B, 2 * SK])
        cwa = sb("cwa", [P, B, D])
        cwb = sb("cwb", [SK - P, B, D])
        mask = sb("mask", [P, T, SK], U8)
        keep = sb("keep", [P, T, SK], U8)
        watt = sb("watt", [P, 6, D])
        pack = sb("pack", [P, NPACK])
        rows = sb("rows", [1, E0 * D + E1])
        gate = sb("gate", [P, E0])
        fc2 = sb("fc2", [P, E0, FT, D])
        wout = sb("wout", [P, 2, D])
        wr = sb("wr", [P, E1])
        bd = sb("bd", [2 * E1, D])

        def const(name):
            return pack[:, PACK[name][0]:PACK[name][1]]

        ident = const("ident")
        br_row = rows[0:1, E0 * D:]
        b1 = const("b1").rearrange("p (e f) -> p e f", e=E0)

        arena_a = sb("arena_a", [P, E0 * T * P], F32R)
        qa, qb, ka, kb = lay(arena_a, ([P, 2, S], [P, 2, S], [P, 2, NBLK * P], [P, 2, NBLK * P]))
        pickT, = lay(arena_a, ([P, E0, T * P],))
        arena_b = sb("arena_b", [P, T * E0 * P], F32R)
        pick, = lay(arena_b, ([P, T, E0, P],))
        y3hi, y3lo, w3, whi, wlo, hhi, hlo, bdhi, bdlo = lay(arena_b, (
            [P, T * P], [P, T * P], [3 * E1, T * P], [P, 3, GW], [P, 3, 3 * P], [P, 2, 512], [P, 2, 512],
            [2 * E1, D], [E1, D]))
        arena_c = sb("arena_c", [P, 8192])
        vraw, vaug, pT = lay(arena_c, ([P, NBLK, D], [P, B, 2, NBLK, P], [P, 3, S]))
        ind = pT[HW:HW + HH, :, :].rearrange("p a b -> p (a b)")[:, 0:NBLK * P]
        ygT, hid, aff, left, wsel, wrow, slotT, sm = lay(arena_c, (
            [P, E0 * P], [P, 2, FT, P], [P, T, E1], [P, T, E1], [P, T, E1],
            [2 * E0, E0 * P], [E0, T * P // 2], [P, T, SK]))
        slotT = slotT.bitcast(BF16)
        screp, = lay(arena_c, ([P, T, E0, P // E0],))
        arena_d = sb("arena_d", [P, E0 * F0])
        fc1, = lay(arena_d, ([P, E0, F0],))
        sil, gu, hh, yT = lay(arena_d, ([P, 2, 512], [P, 2, 512], [P, 2, 512], [P, T * P]))

        pTa, pTb = lay(arena_d, ([P, B, TB * P], [SK - P, B, TB * P]))

        stats = sb("stats", [P, 2, TB, 6])
        mv = sb("mv", [P, 2, TB, 2])
        negmean = sb("negmean", [P, 2, TB])
        shift = sb("shift", [P, 2, TB])
        vareps = sb("vareps", [P, 2, TB])
        rstd = sb("rstd", [P, 2, TB])
        neghalf = sb("neghalf", [P, TB])
        warm = sb("warm", [P, 1])
        onesrow = sb("onesrow", [1, P])
        onesb = sb("onesb", [P, P], BF16)
        trib = sb("trib", [P, P], BF16)
        groupb = sb("groupb", [P, P], BF16)

        xn = sb("xn", [P, T, D])
        xnT = sb("xnT", [P, T * P])
        kT = sb("kT", [P, 2, B, SK])
        arena_e = sb("arena_e", [P, 2 * E0 * D], F32R)
        khi, klo = lay(arena_e, ([P, 2, B, SK], [P, 2, B, SK]))
        ohi, olo = lay(arena_e, ([P, E0, D], [P, E0, D]))
        smax = sb("smax", [P, COMBOS * TB, HH])
        osb = sb("osb", [P, S])
        att = sb("att", [P, S])
        attT = sb("attT", [P, S])
        x1 = sb("x1", [P, T, D])
        y0 = sb("y0", [P, T, D])
        res = sb("res", [P, T, D])
        x2, x3, out = x1, res, x

        gsum = sb("gsum", [P, E0])
        lg = sb("lg", [P, T, E0])
        sc = sb("sc", [P, T, E0])
        small = sb("small", [P, 4, T])
        srep = xnT
        junk = att[:, :].bitcast(BF16)
        count = sb("count", [P, 1])
        okb = sb("okb", [P, 1], BF16)
        prefix = sb("prefix", [P, 1], I32)
        delta = sb("delta", [P, 2], I32)
        base = sb("base", [P, 1])
        cand = sb("cand", [P, 1], I32)
        thr = sb("thr", [P, E0])
        gteq = sb("gteq", [P, 2, T, E0], BF16)
        room = sb("room", [P, E0])
        pre = sb("pre", [P, 2, T, E0])
        work = sb("work", [P, 3, T, E0])
        slot = sb("slot", [P, T, E0])
        yhi = sb("yhi", [P, T, D], F32R)
        ylo = sb("ylo", [P, T, D], F32R)
        schl = sb("schl", [P, T, 2 * E0], F32R)
        wslot = sb("wslot", [P, E0])
        esel = osb[0:E0, :].bitcast(BF16)

        negmax = sb("negmax", [P, T])
        ssum = sb("ssum", [P, T])
        srec = sb("srec", [P, T])
        unmasked = sb("unmasked", [P, T])

        top8 = sb("top8", [P, T, TOP])
        wsum = sb("wsum", [P, 2, T])
        rec = sb("rec", [P, 3, REC])
        bias = sb("bias", [P, 3, 2])

        def f32(ap):
            return ap.bitcast(F32)

        L = {n: sem("ld_" + n) for n in ("x0", "x1", "ctx2", "watt", "pack", "rows", "gate", "fc1", "fc2", "mask", "wout", "wr", "bd", "ind")}
        names = """var_ready rstd_ready consts_ready xn_ready xnT_psum xnT_ready q_psum qhi_ready qlo_ready k_psum
        kT_ready khi_ready klo_ready ka_first kb_ind expanded v_psum vraw_ready vaug_ready rough_done max_done
        mT_psum mT_ready score_psum exp_done pv_done o_psum osb_ready att_ready attT_ready proj_psum xbo_ready
        pad_zero ones_ready sm_filled x1_ready y0_ready x1T_psum x1T_ready logit_psum lgsub_ready lgexp_ready sc_ready screp_ready srep_psum srep_ready
        count_ready ok_ready nok_psum delta_ready prefix_ready cand_ready thr_psum gteq_ready pre_psum slot_ready
        gsum_psum gsum_ready pick_ready yh1_ready yh_ready yhi_ready ylo_ready res_ready gath_psum ygT_ready wrow_psum wrow_ready w_psum w_ready
        esel_ready slotT_psum slotT_ready slotb_psum fc1_psum hid_ready schi_ready sclo_ready
        fc2_psum ohi_ready olo_ready pickT_ready scat_psum scT_ready back_psum x2_ready
        shift_ready y2a_ready y3a_ready y2_ready y2T_psum y2T_ready s1_psum keep_ready negmax_ready p1_ready srec_ready p1T_psum p1T_ready
        cw_psum cw_ready r1_psum r1_ready o1_psum x3_ready y3_ready y3T_psum y3T_ready y3hi_ready y3lo_ready
        lr_psum aff_ready wsel_ready wT_psum whi_ready w3_ready w3ones_ready bdhi_ready bdlo_ready rec_ready0 rec_ready1 rec_ready2 split_ready
        bias_ready rec_asked split_begun gate_psum upw_psum sil_ready gu_ready hh_ready hhi_ready hlo_ready down_done y_psum yT_ready
        warm_done outT_psum out_ready stored dve_chain""".split()
        Z = {n: sem(n) for n in names}

        block = ctx.enter_context(nc.Block())

        def indicators(copy, b, g):
            v = vaug[:, b, g, :, :].rearrange("p i (a h d) -> p i a h d", a=2, h=HH)
            mask_ = const("vmask").rearrange("p (i h) -> p i h", i=NBLK)
            copy(v[:, :, 1 - g], mask_[:, :, :, None].broadcast_to([P, NBLK, HH, DH])).then_inc(Z["ones_ready"], 1)

        @block.sync
        def _(sp):
            sp.dma_start(x[:, 0:TB], x_d[:, 0:TB]).then_inc(L["x0"], 16)
            sp.dma_start(watt[:, :, :], watt_d).then_inc(L["watt"], 16)
            sp.dma_start(x[:, TB:], x_d[:, TB:]).then_inc(L["x1"], 16)
            sp.dma_start(rows[:, :], rows_d).then_inc(L["rows"], 16)
            sp.dma_start(gate[:, :], gate_d).then_inc(L["gate"], 16)
            sp.dma_start(fc1[:, :, :], fc1_d).then_inc(L["fc1"], 16)
            sp.dma_start(fc2[:, :, :, :], fc2_d).then_inc(L["fc2"], 16)
            sp.dma_start(mask[:, :, :], mask_d).then_inc(L["mask"], 16)
            sp.dma_start(wout[:, :, :], wout_d).then_inc(L["wout"], 16)
            sp.dma_start(wr[:, :], wr_d).then_inc(L["wr"], 16)
            sp.dma_start(bd[:, :], bd_d).then_inc(L["bd"], 16)
            for n in range(3):
                sp.dma_start(rec[:, n, :], rec_d[n]).then_inc(Z["rec_ready%d" % n], 16)
            with sp.Fori(1, LOOPS) as m:
                for u in range(3):
                    sp.wait_ge(Z["split_ready"], m * 3 + (u - 2))
                    sp.sem_inc(Z["rec_asked"], 1)
                    sp.dma_start(rec[:, u, :], rec_d[bass.ds(m * 3 + u, 1)].rearrange("o p c -> (o p) c"))\
                        .then_inc(Z["rec_ready%d" % u], 16)
            for n in range(3 * LOOPS, PAIRS):
                sp.wait_ge(Z["split_ready"], n - 2)
                sp.dma_start(rec[:, n % 3, :], rec_d[n]).then_inc(Z["rec_ready%d" % (n % 3)], 16)
            for b in range(B):
                sp.wait_ge(Z["out_ready"], b + 1)
                sp.dma_start(out_d[:, b * TB:(b + 1) * TB], out[:, b * TB:(b + 1) * TB]).then_inc(Z["stored"], 16)
            sp.wait_ge(Z["stored"], 16 * B)

        @block.gpsimd
        def _(pool):
            rstds = [0]

            def rsqrt(shifts=False):
                rstds[0] += 1
                pool.wait_ge(Z["var_ready"], rstds[0])
                h = (rstds[0] - 1) % 2
                pool.tensor_tensor(rstd[:, h], vareps[:, h], neghalf[:, :], ALU.pow).then_inc(Z["rstd_ready"], 1)
                if shifts:
                    pool.wait_ge(Z["rstd_ready"], rstds[0])
                    pool.tensor_tensor(shift[:, h], negmean[:, h], rstd[:, h], ALU.mult).then_inc(Z["shift_ready"], 1)

            pool.memset(neghalf[:, :], -0.5).then_inc(Z["consts_ready"], 1)
            pool.memset(onesrow[:, :], 1.0).then_inc(Z["consts_ready"], 1)
            pool.memset(onesb[:, :], 1.0).then_inc(Z["consts_ready"], 1)
            pool.memset(ka[:, :, FLAT:].bitcast(F32), 0.0).then_inc(Z["pad_zero"], 1)
            pool.memset(kb[:, :, FLAT:].bitcast(F32), 0.0).then_inc(Z["pad_zero"], 1)
            pool.wait_ge(Z["consts_ready"], 3)
            rsqrt()
            pool.wait_ge(Z["rstd_ready"], 1)
            pool.wait_ge(Z["pad_zero"], 2)
            expansions = [0]

            def expand(dst, src, c, rows):
                b, g = c // 2, c % 2
                expansions[0] += 1
                if expansions[0] > 1:
                    pool.wait_ge(Z["expanded"], expansions[0] - 1)
                pool.tensor_tensor(dst[0:rows, c % 2, 0:FLAT].rearrange("p (h k) -> p h k", h=HH),
                                   f32(src[0:rows, g, b, None, :]).broadcast_to([rows, HH, SK]),
                                   const("headmask")[0:rows, :, None].broadcast_to([rows, HH, SK]),
                                   ALU.mult).then_inc(Z["expanded"], 1)

            def values(b):
                pool.wait_ge(Z["vraw_ready"], 3 * (b + 1))
                for g in range(2):
                    v = vaug[:, b, g, :, :].rearrange("p i (a h d) -> p i a h d", a=2, h=HH)
                    pool.tensor_tensor(v[:, :, g], vraw[:, :, g * HW:(g + 1) * HW].rearrange("p i (h d) -> p i h d", h=HH),
                                       vm[:, :, :, None].broadcast_to([P, NBLK, HH, DH]), ALU.mult)\
                        .then_inc(Z["vaug_ready"], 1)

            vm = const("vmask").rearrange("p (i h) -> p i h", i=NBLK)
            pool.wait_ge(Z["klo_ready"], 1)
            expand(kb, klo, 0, HW)
            expand(ka, khi, 1, P)
            expand(kb, klo, 1, HW)
            pool.wait_ge(Z["expanded"], 3)
            values(0)
            rsqrt()
            for g in range(2):
                indicators(pool.tensor_copy, 1, g)
            for c in range(2, COMBOS):
                if c == 2:
                    pool.wait_ge(L["x0"], 16)
                    pool.wait_ge(L["x1"], 16)
                    pool.tensor_tensor(x1[:, :, :], x[:, :, :], const("bo")[:, None, :].broadcast_to([P, T, D]),
                                       ALU.add).then_inc(Z["xbo_ready"], 1)
                pool.wait_ge(Z["score_psum"], (c - 1) * NBLK)
                expand(ka, khi, c, P)
                expand(kb, klo, c, HW)
                if c == 2:
                    values(1)
            pool.wait_ge(L["mask"], 16)
            rsqrt()
            rsqrt()
            rsqrt()
            rsqrt(shifts=True)
            pool.wait_ge(Z["y0_ready"], 2 * TB)
            pool.tensor_tensor(res[:, :, :], x1[:, :, :], y0[:, :, :], ALU.add).then_inc(Z["res_ready"], 1)
            pool.memset(sm[:, :, :], MASKED).then_inc(Z["sm_filled"], 1)
            pool.wait_ge(Z["yhi_ready"], 1)
            pool.tensor_tensor(ylo[:, :, :], xn[:, :, :], f32(yhi[:, :, :]), ALU.subtract).then_inc(Z["ylo_ready"], 1)
            pool.wait_ge(Z["schi_ready"], 1)
            pool.tensor_tensor(schl[:, :, E0:], sc[:, :, :], f32(schl[:, :, 0:E0]), ALU.subtract)\
                .then_inc(Z["sclo_ready"], 1)
            pool.wait_ge(Z["gath_psum"], 2)
            pool.wait_ge(Z["wrow_psum"], 2)
            pool.wait_ge(Z["ylo_ready"], 1)
            pool.memset(w3[2 * E1:3 * E1, :].bitcast(F32), 1.0).then_inc(Z["w3ones_ready"], 1)
            pool.wait_ge(Z["w3ones_ready"], 1)
            pool.wait_ge(L["bd"], 16)
            pool.tensor_copy(bdhi[:, :], bd[:, :]).then_inc(Z["bdhi_ready"], 1)
            pool.wait_ge(Z["bdhi_ready"], 1)
            pool.tensor_tensor(bdlo[:, :], bd[0:E1, :], f32(bdhi[0:E1, :]), ALU.subtract).then_inc(Z["bdlo_ready"], 1)
            pool.wait_ge(Z["bdlo_ready"], 1)

            def split(u):
                pool.tensor_copy(whi[:, u, :], rec[:, u, 0:GW])\
                    .then_inc(Z["bias_ready"], 1)
                pool.tensor_copy(bias[:, u, :], rec[:, u, GW:REC]).then_inc(Z["bias_ready"], 1)

            def split_lo(u):
                pool.tensor_tensor(wlo[:, u, :], rec[:, u, 0:3 * P], f32(whi[:, u, 0:3 * P]), ALU.subtract)\
                    .then_inc(Z["split_ready"], 1)

            for n in range(3):
                pool.wait_ge(Z["rec_ready%d" % n], 16)
                split(n)
                pool.wait_ge(Z["bias_ready"], 2 * (n + 1))
                split_lo(n)
            for _ in ("x2", "x3"):
                rsqrt(shifts=True)
                rsqrt()
            with pool.Fori(1, LOOPS) as m:
                for u in range(3):
                    pool.wait_ge(Z["rec_ready%d" % u], m * 16 + 16)
                    pool.wait_ge(Z["down_done"], m * 6 + (2 * u - 4))
                    pool.sem_inc(Z["split_begun"], 1)
                    split(u)
                    pool.wait_ge(Z["bias_ready"], m * 6 + (2 * u + 2))
                    split_lo(u)
            for n in range(3 * LOOPS, PAIRS):
                pool.wait_ge(Z["rec_ready%d" % (n % 3)], 16 * (n // 3 + 1))
                pool.wait_ge(Z["down_done"], 2 * n - 4)
                split(n % 3)
                pool.wait_ge(Z["bias_ready"], 2 * (n + 1))
                split_lo(n % 3)

        @block.vector
        def _(dve):
            chain = [0]

            def link(ins):
                chain[0] += 1
                ins.then_inc(Z["dve_chain"], 1)
                dve.wait_ge(Z["dve_chain"], chain[0])

            norms = [0]

            def measure(src, t0):
                h = norms[0] % 2
                norms[0] += 1
                for i in range(TB):
                    ins = dve.bn_stats(stats[:, h, i, :], src[:, t0 + i, :])
                link(ins)
                return aggregate(norms[0])

            def aggregate(n):
                h = (n - 1) % 2
                for i in range(TB):
                    ins = dve.bn_aggr(mv[:, h, i, :], stats[:, h, i, :])
                link(ins)
                dve.tensor_scalar(negmean[:, h], mv[:, h, :, 0], -1.0, None, ALU.mult)
                dve.tensor_scalar_add(vareps[:, h], mv[:, h, :, 1], EPS).then_inc(Z["var_ready"], 1)
                return n

            def center(n, src, dst, t0, done):
                h = (n - 1) % 2
                dve.wait_ge(Z["rstd_ready"], n)
                for i in range(TB):
                    dve.tensor_scalar(dst[:, t0 + i, :], src[:, t0 + i, :], mv[:, h, i, 0:1], rstd[:, h, i:i + 1],
                                      ALU.subtract, ALU.mult).then_inc(Z[done], 1)

            def norm(src, dst, t0, done):
                center(measure(src, t0), src, dst, t0, done)

            dve.wait_ge(L["x0"], 16)
            norm(x, xn, 0, "xn_ready")
            dve.wait_ge(L["pack"], 16)
            dve.wait_ge(Z["kT_ready"], 2)
            dve.tensor_copy(khi[:, :, :, :], kT[:, :, :, :]).then_inc(Z["khi_ready"], 1)
            dve.wait_ge(Z["khi_ready"], 1)
            dve.tensor_tensor(klo[:, :, :, :], kT[:, :, :, :], f32(khi[:, :, :, :]), ALU.subtract)\
                .then_inc(Z["klo_ready"], 1)
            dve.tensor_tensor(ka[:, 0, 0:FLAT].rearrange("p (h k) -> p h k", h=HH),
                              f32(khi[:, 0, 0, None, :]).broadcast_to([P, HH, SK]),
                              const("headmask")[:, :, None].broadcast_to([P, HH, SK]), ALU.mult)\
                .then_inc(Z["ka_first"], 1)

            def q_lo(c):
                dve.wait_ge(Z["qhi_ready"], 2 * c + 2)
                dve.scalar_tensor_tensor(qa[HW:P, c % 2, :], bank[HW:P, 6, :], const("bq")[HW:P, c % 2:c % 2 + 1],
                                         f32(qa[HW:P, c % 2, :]), ALU.add, ALU.subtract)\
                    .then_inc(Z["qlo_ready"], 1)

            def maxima(c, i):
                n = c * TB + i
                c0 = 3 * 512 * (i % 2) if c == 0 else 0
                dve.wait_ge(Z["rough_done"], n + 1)
                dve.tensor_reduce(smax[:, n, :], flat[:, c0:c0 + FLAT].rearrange("p (h k) -> p h k", h=HH), AX.X, ALU.max)\
                    .then_inc(Z["max_done"], 1)

            def normalise(c, c0=0, c1=S):
                g = c % 2
                own, other = slice(g * HW, (g + 1) * HW), slice((1 - g) * HW, (2 - g) * HW)
                dve.wait_ge(Z["osb_ready"], c + 1)
                if c >= 2:
                    dve.wait_ge(Z["attT_ready"], 1)
                link(dve.reciprocal(att[own, c0:c1], osb[other, c0:c1]))
                dve.tensor_tensor(att[own, c0:c1], osb[own, c0:c1], att[own, c0:c1], ALU.mult)\
                    .then_inc(Z["att_ready"], 1)

            def residual(b, c0=0, c1=S):
                dve.wait_ge(Z["proj_psum"], b + 1 + (c0 > 0))
                dve.wait_ge(Z["xbo_ready"], 1)
                v = x1[:, b * TB:(b + 1) * TB, :].rearrange("p t d -> p (t d)")[:, c0:c1]
                dve.tensor_tensor(v, bank[:, 4 if c0 else 7, c0:c1], v, ALU.add).then_inc(Z["x1_ready"], 1)

            q_lo(0)
            for i in range(TB):
                maxima(0, i)
            dve.tensor_copy(trib[:, :], const("tri")).then_inc(Z["consts_ready"], 1)
            dve.tensor_copy(groupb[:, :], const("group")).then_inc(Z["consts_ready"], 1)

            def logit_bank(b):
                return bank[:, (2, 6)[b], 0:TB * E0].rearrange("p (t e) -> p t e", t=TB)

            def gate_shift(b, n):
                ts, h = slice(b * TB, (b + 1) * TB), (n - 1) % 2
                link(dve.tensor_tensor(lg[:, ts], mv[:, h, :, 0, None].broadcast_to([P, TB, E0]),
                                       gsum[:, None, :].broadcast_to([P, TB, E0]), ALU.mult))
                dve.wait_ge(Z["logit_psum"], b + 1)
                link(dve.tensor_tensor(lg[:, ts], logit_bank(b), lg[:, ts], ALU.add))
                dve.wait_ge(Z["rstd_ready"], n)
                link(dve.tensor_tensor(lg[:, ts], lg[:, ts], rstd[:, h, :, None].broadcast_to([P, TB, E0]), ALU.mult))
                link(dve.tensor_reduce(small[:, 0, ts], lg[:, ts], AX.X, ALU.max))
                dve.tensor_tensor(lg[:, ts], lg[:, ts], small[:, 0, ts, None].broadcast_to([P, TB, E0]), ALU.subtract)\
                    .then_inc(Z["lgsub_ready"], 1)

            def gate_scores(b):
                ts = slice(b * TB, (b + 1) * TB)
                dve.wait_ge(Z["lgexp_ready"], b + 1)
                link(dve.tensor_reduce(small[:, 1, ts], lg[:, ts], AX.X, ALU.add))
                link(dve.reciprocal(small[:, 2, ts], small[:, 1, ts]))
                dve.tensor_tensor(sc[:, ts], lg[:, ts], small[:, 2, ts, None].broadcast_to([P, TB, E0]), ALU.mult)\
                    .then_inc(Z["sc_ready"], 1)
                dve.wait_ge(Z["sc_ready"], b + 1)
                dve.tensor_copy(screp[:, ts], sc[:, ts, :, None].broadcast_to([P, TB, E0, P // E0]))\
                    .then_inc(Z["screp_ready"], 1)

            q_lo(1)
            for c in range(COMBOS):
                if c + 1 < COMBOS:
                    for i in range(TB):
                        if c and i == 1:
                            normalise(c - 1)
                        maxima(c + 1, i)
                        if c == 0 and i == 1:
                            dve.wait_ge(L["x1"], 16)
                            norm(x, xn, TB, "xn_ready")
                    if c + 2 < COMBOS:
                        q_lo(c + 2)
                    if c == 2:
                        residual(0)
            normalise(2)
            dve.wait_ge(Z["x1_ready"], 1)
            n = measure(x1, 0)
            center(n, x1, y0, 0, "y0_ready")
            dve.wait_ge(Z["gsum_ready"], 1)
            gate_shift(0, n)
            dve.wait_ge(Z["y0_ready"], TB)
            norm(y0, xn, 0, "yh_ready")
            dve.wait_ge(L["mask"], 16)
            dve.tensor_scalar(keep[:, :, :], mask[:, :, :], 0.0, None, ALU.is_equal).then_inc(Z["keep_ready"], 1)
            gate_scores(0)
            dve.wait_ge(Z["osb_ready"], COMBOS + 1)
            link(dve.reciprocal(osb[:, 0:S // 2], osb[:, 0:S // 2]))
            for a, rows in enumerate((slice(0, HW), slice(HW, P))):
                cs = slice(a * S // 2, (a + 1) * S // 2)
                dve.tensor_tensor(att[HW:P, cs], bank[HW:P, 5, cs], osb[rows, 0:S // 2], ALU.mult)\
                    .then_inc(Z["att_ready"], 1)
            norms[0] += 1
            n = norms[0]
            for a in range(2):
                residual(1, a * S // 2, (a + 1) * S // 2)
                dve.wait_ge(Z["x1_ready"], 2 + a)
                for i in (2 * a, 2 * a + 1):
                    ins = dve.bn_stats(stats[:, (n - 1) % 2, i, :], x1[:, TB + i, :])
            link(ins)
            aggregate(n)
            gate_shift(1, n)
            gate_scores(1)
            center(n, x1, y0, TB, "y0_ready")
            dve.wait_ge(Z["y0_ready"], T)
            measure(y0, TB)
            dve.wait_ge(Z["srep_ready"], 2)
            for k, shift in enumerate(SHIFTS):
                dve.tensor_scalar(junk[:, :], srep[:, :], const("cand0") if k == 0 else cand[:, :].bitcast(F32),
                                  0.0, ALU.is_ge, ALU.add, accum_out=count[:, :]).then_inc(Z["count_ready"], 1)
                dve.wait_ge(Z["count_ready"], k + 1)
                dve.tensor_scalar(okb[:, :], count[:, :], CAP - 0.5, None, ALU.is_ge).then_inc(Z["ok_ready"], 1)
                jg = const("jg")[:, k:k + 1] if k <= EXACT else None
                if 1 <= k < EXACT:
                    link(dve.tensor_scalar(base[:, :], cand[:, :], jg, None, ALU.add))
                elif k == EXACT:
                    dve.tensor_scalar(prefix[:, :], cand[:, :], jg, None, ALU.add).then_inc(Z["prefix_ready"], 1)
                dve.wait_ge(Z["nok_psum"], k + 1)
                nok = bank[:, 7, 0:1]
                if k < EXACT:
                    dve.tensor_scalar(cand[:, :], nok, float(1 << shift), base[:, :] if k else const("jf")[:, 0:1],
                                      ALU.mult, ALU.add).then_inc(Z["cand_ready"], 1)
                    dve.wait_ge(Z["cand_ready"], k + 1)
                    continue
                last = k + 1 == len(SHIFTS)
                if not last:
                    dve.tensor_scalar(delta[:, 0:1], nok, float(1 << shift), const("jf")[:, k:k + 1], ALU.mult, ALU.add)\
                        .then_inc(Z["delta_ready"], 1)
                dve.tensor_scalar(delta[:, 1:2], nok, -1.0, float(1 << shift), ALU.add, ALU.mult)\
                    .then_inc(Z["delta_ready"], 1)
                dve.wait_ge(Z["delta_ready"], 2 * (k - EXACT) + (1 if last else 2))
                dve.wait_ge(Z["prefix_ready"], k - EXACT + 1)
                if not last:
                    dve.tensor_tensor(cand[:, :], prefix[:, :], delta[:, 0:1], ALU.bitwise_or)\
                        .then_inc(Z["cand_ready"], 1)
                dve.tensor_tensor(prefix[:, :], prefix[:, :], delta[:, 1:2], ALU.bitwise_or)\
                    .then_inc(Z["prefix_ready"], 1)
                if not last:
                    dve.wait_ge(Z["cand_ready"], k + 1)
            dve.wait_ge(Z["thr_psum"], 1)
            link(dve.tensor_copy(thr[:, :], bank[:, 6, 0:P].rearrange("p (e j) -> p e j", e=E0)[:, :, 0]))
            tb = thr[:, None, :].broadcast_to([P, T, E0])
            dve.tensor_tensor(gteq[:, 0], sc[:, :, :], tb, ALU.is_gt).then_inc(Z["gteq_ready"], 1)
            dve.tensor_tensor(gteq[:, 1], sc[:, :, :], tb, ALU.is_equal).then_inc(Z["gteq_ready"], 1)
            dve.wait_ge(Z["pre_psum"], 1)
            dve.tensor_copy(pre[:, :, :, :].rearrange("p k t e -> p (k t e)"), bank[:, 6, 0:2 * T * E0])
            link(dve.tensor_scalar(room[:, :], bank[:, 7, 0:E0], -1.0, float(CAP), ALU.mult, ALU.add))
            rb = room[:, None, :].broadcast_to([P, T, E0])
            link(dve.tensor_tensor(work[:, 0], pre[:, 1], rb, ALU.is_lt))
            link(dve.tensor_tensor(work[:, 1], work[:, 0], gteq[:, 1], ALU.mult))
            link(dve.tensor_tensor(work[:, 0], work[:, 1], gteq[:, 0], ALU.add))
            link(dve.tensor_tensor(work[:, 2], pre[:, 1], rb, ALU.min))
            link(dve.tensor_tensor(work[:, 1], work[:, 2], pre[:, 0], ALU.add))
            link(dve.scalar_tensor_tensor(work[:, 2], work[:, 1], -NOSLOT, work[:, 0], ALU.add, ALU.mult))
            dve.tensor_scalar_add(slot[:, :, :], work[:, 2], NOSLOT).then_inc(Z["slot_ready"], 1)
            dve.wait_ge(Z["slot_ready"], 1)

            def picks(g, t):
                n = E0 // 2
                for e in range(g * n, (g + 1) * n):
                    ins = dve.tensor_scalar(pick[:, t, e, :], const("iota"), slot[:, t, e:e + 1], None, ALU.is_equal)
                ins.then_inc(Z["pick_ready"], 1)

            def picks_turned(e):
                for b in range(B):
                    if b and e >= 2:
                        low_out(e - 2)
                    dve.wait_ge(Z["slotb_psum"], 2 * e + b + 1)
                    dve.tensor_scalar(pickT[:, e, b * S:(b + 1) * S], bank[:, 5, :], const("row"), None, ALU.is_equal)\
                        .then_inc(Z["pickT_ready"], 1)

            def slot_scores(g):
                dve.wait_ge(Z["w_psum"], g + 1)
                n = E0 // 2
                dve.tensor_copy(wslot[:, g * n:(g + 1) * n], bank[:, 1, 0:n]).then_inc(Z["w_ready"], 1)

            def low_out(e):
                dve.wait_ge(Z["ohi_ready"], e + 1)
                dve.scalar_tensor_tensor(olo[:, e, :], bank[:, 4, 0:D], wslot[:, e:e + 1], f32(ohi[:, e, :]),
                                         ALU.mult, ALU.subtract).then_inc(Z["olo_ready"], 1)

            for t in range(T):
                picks(0, t)
            for e in range(E0):
                picks_turned(e)
                if e in (1, E0 // 2):
                    slot_scores(2 * e // E0)
                for t in range(*SECOND_PICKS.get(e, (0, 0))):
                    picks(1, t)
            low_out(E0 - 2)
            low_out(E0 - 1)
            half = lambda v, b: v[:, b * TB:(b + 1) * TB, :].rearrange("p t d -> p (t d)")
            dve.wait_ge(Z["res_ready"], 1)
            n = []
            for b in range(B):
                dve.wait_ge(Z["back_psum"], b + 1)
                dve.tensor_tensor(half(x2, b), bank[:, b, :], half(res, b), ALU.add).then_inc(Z["x2_ready"], 1)
                dve.wait_ge(Z["x2_ready"], b + 1)
                n.append(measure(x2, b * TB))
            center(n[1], x2, xn, TB, "y2_ready")
            dve.wait_ge(Z["keep_ready"], 1)
            dve.wait_ge(Z["sm_filled"], 1)
            for b in range(B):
                t0 = b * TB
                dve.wait_ge(Z["s1_psum"], b + 1)
                dve.copy_predicated(sm[:, t0:t0 + 3, :], keep[:, t0:t0 + 3, :],
                                    bank[:, 2 + 2 * b, 0:3 * SK].rearrange("p (t k) -> p t k", t=3))
                link(dve.copy_predicated(sm[:, t0 + 3, :], keep[:, t0 + 3, :], bank[:, 3 + 2 * b, 0:SK]))
                dve.tensor_reduce(negmax[:, t0:t0 + TB], sm[:, t0:t0 + TB, :], AX.X, ALU.max, negate=True)\
                    .then_inc(Z["negmax_ready"], 1)
            for b in range(B):
                dve.wait_ge(Z["r1_psum"], b + 1)
                dve.tensor_tensor(half(x2, b), bank[:, 6 + b, :], half(x2, b), ALU.add).then_inc(Z["r1_ready"], 1)
            for b in range(B):
                ts = slice(b * TB, (b + 1) * TB)
                dve.wait_ge(Z["p1_ready"], TB * (b + 1))
                link(dve.tensor_scalar(unmasked[:, ts], negmax[:, ts], -MASKED, None, ALU.is_lt))
                link(dve.tensor_tensor(srec[:, ts], unmasked[:, ts], ssum[:, ts], ALU.mult))
                link(dve.reciprocal(srec[:, ts], srec[:, ts]))
                dve.tensor_tensor(srec[:, ts], srec[:, ts], unmasked[:, ts], ALU.mult).then_inc(Z["srec_ready"], 1)
            n = []
            for b in range(B):
                dve.wait_ge(Z["o1_psum"], b + 1)
                dve.wait_ge(Z["srec_ready"], b + 1)
                dve.wait_ge(Z["r1_ready"], b + 1)
                for i in range(TB):
                    t = b * TB + i
                    ins = dve.scalar_tensor_tensor(x3[:, t, :], bank[:, 2 + 2 * b, i * P:(i + 1) * P], srec[:, t:t + 1],
                                                   x2[:, t, :], ALU.mult, ALU.add)
                ins.then_inc(Z["x3_ready"], 1)
                dve.wait_ge(Z["x3_ready"], b + 1)
                n.append(measure(x3, b * TB))
            center(n[1], x3, y0, TB, "y3_ready")
            for b in range(B):
                cs = slice(b * S, (b + 1) * S)
                dve.wait_ge(Z["y3hi_ready"], b + 1)
                dve.tensor_tensor(y3lo[:, cs], bank[:, b, :], f32(y3hi[:, cs]), ALU.subtract).then_inc(Z["y3lo_ready"], 1)

            def low_weights(b):
                cs = slice(b * S, (b + 1) * S)
                dve.wait_ge(Z["whi_ready"], b + 1)
                dve.tensor_tensor(w3[E1:2 * E1, cs], bank[0:E1, 6 + b, :], f32(w3[0:E1, cs]), ALU.subtract)\
                    .then_inc(Z["w3_ready"], 1)

            for b in range(B):
                ts = slice(b * TB, (b + 1) * TB)
                dve.wait_ge(Z["aff_ready"], b + 1)
                for t in range(b * TB, (b + 1) * TB):
                    ins = dve.max(top8[:, t, :], aff[:, t, :])
                link(ins)
                for t in range(b * TB, (b + 1) * TB):
                    ins = dve.match_replace(left[:, t, :], top8[:, t, :], aff[:, t, :], -1.0)
                link(ins)
                link(dve.scalar_tensor_tensor(wsel[:, ts], left[:, ts], 0.0, aff[:, ts], ALU.is_lt, ALU.mult))
                link(dve.tensor_reduce(wsum[:, 0, ts], wsel[:, ts], AX.X, ALU.add))
                link(dve.tensor_scalar_add(wsum[:, 0, ts], wsum[:, 0, ts], 1e-9))
                link(dve.reciprocal(wsum[:, 1, ts], wsum[:, 0, ts]))
                dve.tensor_tensor(wsel[:, ts], wsel[:, ts], wsum[:, 1, ts, None].broadcast_to([P, TB, E1]), ALU.mult)\
                    .then_inc(Z["wsel_ready"], 1)
                if b:
                    low_weights(0)
            low_weights(1)
            def hidden(k, c, u, first=False):
                dve.wait_ge(Z["sil_ready"], k + 1)
                dve.wait_ge(Z["upw_psum"], k + 1)
                dve.scalar_tensor_tensor(gu[:, c, :], bank[:, 2 + c, :], bias[:, u, 1:2], sil[:, c, :],
                                         ALU.add, ALU.mult).then_inc(Z["gu_ready"], 1)
                if not first:
                    low_hidden(k - 1, 1 - c)
                dve.wait_ge(Z["gu_ready"], k + 1)
                dve.tensor_tensor(hh[:, c, :], gu[:, c, :], bank[:, 4 + c, :], ALU.mult).then_inc(Z["hh_ready"], 1)

            def low_hidden(k, c):
                dve.wait_ge(Z["hhi_ready"], k + 1)
                dve.tensor_tensor(hlo[:, c, :], hh[:, c, :], f32(hhi[:, c, :]), ALU.subtract)\
                    .then_inc(Z["hlo_ready"], 1)

            hidden(0, 0, 0, first=True)
            hidden(1, 1, 0)
            with dve.Fori(0, LOOPS) as m:
                for u in range(3):
                    for c in range(2):
                        hidden(m * 6 + (2 * u + 2 + c), c, (u + 1) % 3)
            hidden(2 * PAIRS - 2, 0, (PAIRS - 1) % 3)
            hidden(2 * PAIRS - 1, 1, (PAIRS - 1) % 3)
            low_hidden(2 * PAIRS - 1, 1)
            for b in range(B):
                dve.wait_ge(Z["outT_psum"], b + 1)
                dve.tensor_tensor(out[:, b * TB:(b + 1) * TB, :].rearrange("p t d -> p (t d)"), bank[:, b, :],
                                  x3[:, b * TB:(b + 1) * TB, :].rearrange("p t d -> p (t d)"), ALU.add)\
                    .then_inc(Z["out_ready"], 1)

        @block.scalar
        def _(act):
            act.dma_start(pack[:, :], pack_d).then_inc(L["pack"], 16)
            act.dma_start(ctx2[:, :, :], ctx2_d).then_inc(L["ctx2"], 16)
            act.dma_start(ind, ind_d).then_inc(L["ind"], 16)
            act.wait_ge(Z["consts_ready"], 1)
            act.activation(warm[:, :], neghalf[:, 0:1], ACT.Exp).then_inc(Z["warm_done"], 1)
            act.wait_ge(L["pack"], 16)
            for g in range(2):
                act.wait_ge(Z["k_psum"], g + 1)
                act.activation(kT[:, g, :, :].rearrange("p b k -> p (b k)"), bank[:, 3 + g, 0:B * SK], ACT.Identity,
                               bias=const("bk")[:, g:g + 1]).then_inc(Z["kT_ready"], 1)

            def turned(b):
                act.wait_ge(Z["xnT_psum"], b + 1)
                act.copy(xnT[:, b * S:(b + 1) * S], bank[:, 6, :]).then_inc(Z["xnT_ready"], 1)

            def queries(c):
                act.wait_ge(Z["q_psum"], c + 1)
                bq = const("bq")[:, c % 2:c % 2 + 1]
                act.activation(qa[:, c % 2, :], bank[:, 6, :], ACT.Identity, bias=bq).then_inc(Z["qhi_ready"], 1)
                act.activation(qb[0:HW, c % 2, :], bank[0:HW, 6, :], ACT.Identity, bias=bq[0:HW])\
                    .then_inc(Z["qhi_ready"], 1)

            def values(b, r):
                if b and r == 0:
                    act.wait_ge(Z["vaug_ready"], 2 * b)
                i0, i1 = VGROUPS[r]
                act.wait_ge(Z["v_psum"], 3 * b + r + 1)
                act.copy(vraw[:, i0:i1, :].rearrange("p i d -> p (i d)"), bank[:, 6, 0:(i1 - i0) * P])\
                    .then_inc(Z["vraw_ready"], 1)

            def minus_max(c):
                act.wait_ge(Z["mT_psum"], c + 1)
                act.mul(qb[HW:HW + HH, c % 2, :], bank[0:HH, 7, :], -1.0).then_inc(Z["mT_ready"], 1)

            def with_bias(b, c0=0, c1=S):
                act.wait_ge(Z["att_ready"], 2 * (b + 1) + (c0 > 0))
                act.activation(attT[:, c0:c1], att[:, c0:c1], ACT.Identity, bias=const("bv"))\
                    .then_inc(Z["attT_ready"], 1)

            def outputs(c):
                act.wait_ge(Z["o_psum"], c + 1)
                if c:
                    act.wait_ge(Z["att_ready"], c)
                act.copy(osb[:, :], bank[:, 5, :]).then_inc(Z["osb_ready"], 1)

            def center(src, dst, t0, h, times, done):
                act.wait_ge(Z["shift_ready"], times)
                for i in range(TB):
                    act.activation(dst[:, t0 + i, :], src[:, t0 + i, :], ACT.Identity, bias=shift[:, h, i:i + 1],
                                   scale=rstd[:, h, i:i + 1]).then_inc(Z[done], 1)

            def gate_input(b):
                act.wait_ge(Z["x1T_psum"], b + 1)
                act.copy(xnT[:, b * S:(b + 1) * S], bank[:, b, :]).then_inc(Z["x1T_ready"], 1)

            def gate_exp(b):
                act.wait_ge(Z["lgsub_ready"], b + 1)
                v = lg[:, b * TB:(b + 1) * TB, :]
                act.activation(v, v, ACT.Exp).then_inc(Z["lgexp_ready"], 1)

            def gate_rows(b):
                act.wait_ge(Z["srep_psum"], b + 1)
                act.copy(srep[:, b * S:(b + 1) * S], bank[:, 3 + b, :]).then_inc(Z["srep_ready"], 1)

            turned(0)
            queries(0)
            act.wait_ge(L["ind"], 16)
            act.wait_ge(Z["pad_zero"], 2)
            for n in range(2):
                act.copy(kb[HW:HW + HH, n, :], ind).then_inc(Z["kb_ind"], 1)
            for g in range(2):
                indicators(act.copy, 0, g)
            for r in range(3):
                values(0, r)
            act.wait_ge(Z["gsum_psum"], 1)
            act.mul(gsum[:, :], bank[:, 7, 0:E0], 2.0).then_inc(Z["gsum_ready"], 1)
            minus_max(0)
            for c in range(COMBOS):
                for i in range(NBLK):
                    n = c * NBLK + i
                    act.wait_ge(Z["score_psum"], n + 1)
                    if n >= 3:
                        act.wait_ge(*((Z["o_psum"], (n - 2) // NBLK) if (n - 2) % NBLK == 0 else
                                      (Z["pv_done"], n - 2 - (n - 3) // NBLK)))
                    elif n == 0:
                        act.wait_ge(Z["kb_ind"], 2)
                    act.activation(pT[:, n % 3, :], bank[:, 3 + n % 2, :], ACT.Exp, scale=float(DH) ** -0.5)\
                        .then_inc(Z["exp_done"], 1)
                    if c and i == 0:
                        outputs(c - 1)
                    if n == 0:
                        queries(1)
                    if c and c + 1 < COMBOS and i == 0:
                        queries(c + 1)
                    if c == 3 and i == 3:
                        gate_input(0)
                    if c == 0 and i == 8:
                        turned(1)
                    if c == 1 and i in (2, 4, 6):
                        values(1, i // 2 - 1)
                    if c == 2 and i == 5:
                        with_bias(0)
                    if c + 1 < COMBOS and i == 8:
                        minus_max(c + 1)
            gate_exp(0)
            act.wait_ge(Z["o_psum"], COMBOS)
            act.wait_ge(Z["att_ready"], COMBOS - 1)
            for a, rows in enumerate((slice(0, HW), slice(HW, P))):
                act.copy(osb[rows, 0:S // 2], bank[0:HW, 5, a * S // 2:(a + 1) * S // 2]).then_inc(Z["osb_ready"], 1)
            gate_rows(0)
            for c0, c1 in ((0, S // 2), (S // 2, S)):
                with_bias(1, c0, c1)
            gate_input(1)
            gate_exp(1)
            gate_rows(1)
            act.wait_ge(Z["cw_psum"], 1)
            act.copy(cwa[:, :, :].rearrange("p b d -> p (b d)"), bank[:, 0, 0:B * D])
            act.copy(cwb[:, :, :].rearrange("p b d -> p (b d)"), bank[0:SK - P, 0, B * D:2 * B * D])\
                .then_inc(Z["cw_ready"], 1)
            center(y0, xn, TB, 1, 1, "yh1_ready")
            act.wait_ge(Z["yh_ready"], TB)
            act.wait_ge(Z["yh1_ready"], TB)
            act.copy(yhi[:, :, :], xn[:, :, :]).then_inc(Z["yhi_ready"], 1)
            act.wait_ge(Z["sc_ready"], 2)
            act.copy(schl[:, :, 0:E0], sc[:, :, :]).then_inc(Z["schi_ready"], 1)
            act.copy(esel[:, :].rearrange("p (e j) -> p e j", e=E0), ident[0:E0, 0:E0, None].broadcast_to([E0, E0, P]))\
                .then_inc(Z["esel_ready"], 1)
            act.wait_ge(Z["warm_done"], 1)
            act.activation(warm[:, :], neghalf[:, 0:1], ACT.Gelu_apprx_tanh).then_inc(Z["warm_done"], 1)
            for b in range(B):
                act.wait_ge(Z["slotT_psum"], b + 1)
                act.copy(slotT[:, b * S:(b + 1) * S], bank[0:E0, 6 + b, :]).then_inc(Z["slotT_ready"], 1)

            def gathered(g):
                cs = slice(g * S, (g + 1) * S)
                act.wait_ge(Z["gath_psum"], g + 1)
                act.activation(ygT[:, cs], bank[:, 0, :], ACT.Identity, bias=const("ln_b"), scale=const("ln_w"))\
                    .then_inc(Z["ygT_ready"], 1)

            def gathered_scores(g):
                cs = slice(g * S, (g + 1) * S)
                act.wait_ge(Z["wrow_psum"], g + 1)
                act.copy(wrow[:, cs], bank[0:2 * E0, 1, :]).then_inc(Z["wrow_ready"], 1)

            def high_out(e):
                act.wait_ge(Z["fc2_psum"], e + 1)
                act.wait_ge(Z["w_ready"], 1 + 2 * e // E0)
                act.activation(ohi[:, e, :], bank[:, 4, 0:D], ACT.Copy, scale=wslot[:, e:e + 1])\
                    .then_inc(Z["ohi_ready"], 1)

            gathered(0)
            for e in range(E0):
                if e >= 2:
                    high_out(e - 2)
                act.wait_ge(Z["fc1_psum"], e + 1)
                for f in range(FT):
                    act.activation(hid[:, e % 2, f, :], bank[:, 2 + e % 2, f * P:(f + 1) * P], ACT.Gelu_apprx_tanh,
                                   bias=b1[:, e, f:f + 1]).then_inc(Z["hid_ready"], 1)
                if e == 0:
                    gathered_scores(0)
                if e == 3:
                    gathered(1)
                    gathered_scores(1)
            high_out(E0 - 2)
            high_out(E0 - 1)
            for b in range(B):
                act.wait_ge(Z["scat_psum"], b + 1)
                act.copy(xnT[:, b * S:(b + 1) * S], bank[:, 6 + b, :]).then_inc(Z["scT_ready"], 1)

            center(x2, xn, 0, 0, 2, "y2a_ready")
            for b in range(B):
                act.wait_ge(Z["y2T_psum"], b + 1)
                act.copy(xnT[:, b * S:(b + 1) * S], bank[:, 6 + b, :]).then_inc(Z["y2T_ready"], 1)
            for b in range(B):
                act.wait_ge(Z["negmax_ready"], b + 1)
                for t in range(b * TB, (b + 1) * TB):
                    act.activation(sm[:, t, :], sm[:, t, :], ACT.Exp, bias=negmax[:, t:t + 1],
                                   accum_out=ssum[:, t:t + 1]).then_inc(Z["p1_ready"], 1)
            for b in range(B):
                act.wait_ge(Z["p1T_psum"], b + 1)
                act.copy(pTa[:, b, :], bank[:, b, :]).then_inc(Z["p1T_ready"], 1)
                act.copy(pTb[:, b, :], bank[0:SK - P, 3 + 2 * b, :]).then_inc(Z["p1T_ready"], 1)
            act.wait_ge(Z["warm_done"], 2)
            act.activation(warm[:, :], neghalf[:, 0:1], ACT.Sigmoid).then_inc(Z["warm_done"], 1)
            center(x3, y0, 0, 0, 3, "y3a_ready")
            for b in range(B):
                act.wait_ge(Z["y3T_psum"], b + 1)
                act.copy(xnT[:, b * S:(b + 1) * S], bank[:, b, :]).then_inc(Z["y3T_ready"], 1)
                act.copy(y3hi[:, b * S:(b + 1) * S], bank[:, b, :]).then_inc(Z["y3hi_ready"], 1)
            for b in range(B):
                act.wait_ge(Z["lr_psum"], b + 1)
                act.activation(aff[:, b * TB:(b + 1) * TB, :].rearrange("p t e -> p (t e)"),
                               bank[:, 3 + 2 * b, 0:TB * E1], ACT.Sigmoid).then_inc(Z["aff_ready"], 1)
            def silu(k, c, u):
                act.wait_ge(Z["gate_psum"], k + 1)
                act.activation(sil[:, c, :], bank[:, c, :], ACT.Silu, bias=bias[:, u, 0:1]).then_inc(Z["sil_ready"], 1)

            def high_hidden(k, c, free=True):
                act.wait_ge(Z["hh_ready"], k + 1)
                if free:
                    act.wait_ge(Z["down_done"], k - 1)
                act.copy(hhi[:, c, :], hh[:, c, :]).then_inc(Z["hhi_ready"], 1)

            def act_step(k, c, u, free=True):
                act.wait_ge(Z["hh_ready"], k - 1)
                silu(k, c, u)
                high_hidden(k - 1, 1 - c, free)

            silu(0, 0, 0)
            for b in range(B):
                act.wait_ge(Z["wT_psum"], b + 1)
                act.copy(w3[0:E1, b * S:(b + 1) * S], bank[0:E1, 6 + b, :]).then_inc(Z["whi_ready"], 1)
            silu(1, 1, 0)
            high_hidden(0, 0, free=False)
            act_step(2, 0, 1, free=False)
            with act.Fori(0, LOOPS) as m:
                for u in range(3):
                    for c in range(2):
                        act_step(m * 6 + (2 * u + 3 + c), 1 - c, (u + 1 + c) % 3)
            act_step(2 * PAIRS - 1, 1, (PAIRS - 1) % 3)
            high_hidden(2 * PAIRS - 1, 1)
            for b in range(B):
                if b == 0:
                    act.wait_ge(Z["down_done"], 2 * PAIRS - 1)
                else:
                    act.wait_ge(Z["y_psum"], 1)
                act.activation(yT[:, b * S:(b + 1) * S], bank[:, 6 + b, :], ACT.Identity, bias=const("bd_s"))\
                    .then_inc(Z["yT_ready"], 1)

        @block.tensor
        def _(pe):
            def turn(dst, src, n=P):
                return pe.transpose(dst, src, ident[0:n, 0:n])

            free6 = [None]

            def take6(sem_, count):
                if free6[0]:
                    pe.wait_ge(*free6[0])
                free6[0] = (sem_, count)

            pe.wait_ge(L["ctx2"], 16)
            pe.wait_ge(L["watt"], 16)
            for g in range(2):
                pe.matmul(bank[:, 3 + g, 0:B * SK], watt[:, 2 + g, :], ctx2[:, :, 0:SK], start=True, stop=True)\
                    .then_inc(Z["k_psum"], 1)
            pe.wait_ge(L["pack"], 16)

            def turned(b):
                take6(Z["xnT_ready"], b + 1)
                pe.wait_ge(Z["xn_ready"], TB * (b + 1))
                for i in range(TB):
                    ins = turn(bank[:, 6, i * P:(i + 1) * P], xn[:, b * TB + i, :])
                ins.then_inc(Z["xnT_psum"], 1)

            def queries(c):
                b, g = c // 2, c % 2
                take6(Z["qlo_ready"], c + 1)
                pe.wait_ge(Z["xnT_ready"], b + 1)
                pe.matmul(bank[:, 6, :], watt[:, g, :], xnT[:, b * S:(b + 1) * S], start=True, stop=True)\
                    .then_inc(Z["q_psum"], 1)

            def values(b, r):
                take6(Z["vraw_ready"], 3 * b + r + 1)
                i0, i1 = VGROUPS[r]
                for i in range(i0, i1):
                    o = (P * i) % SK
                    ins = pe.matmul(bank[:, 6, (i - i0) * D:(i - i0 + 1) * D], ctx2[:, b, o:o + P], watt[:, 4, :],
                                    start=True, stop=True)
                ins.then_inc(Z["v_psum"], 1)

            chunks = ((0, 512), (512, 1024), (1024, FLAT))

            def rough(c, i):
                n = c * TB + i
                c0 = 0
                if c:
                    pe.wait_ge(Z["max_done"], n)
                else:
                    c0 = 3 * 512 * (i % 2)
                    if i >= 2:
                        pe.wait_ge(Z["max_done"], i - 1)
                if i == 0:
                    pe.wait_ge(Z["qlo_ready"], c + 1)
                    if c:
                        pe.wait_ge(Z["expanded"], 2 * c)
                    else:
                        pe.wait_ge(Z["ka_first"], 1)
                for k0, k1 in chunks:
                    ins = pe.matmul(flat[:, c0 + k0:c0 + k1], qa[:, c % 2, i * P:(i + 1) * P], ka[:, c % 2, k0:k1],
                                    start=True, stop=True)
                ins.then_inc(Z["rough_done"], 1)

            def maxima(c):
                if c == 0:
                    pe.wait_ge(Z["gsum_ready"], 1)
                pe.wait_ge(Z["max_done"], TB * (c + 1))
                if c:
                    pe.wait_ge(Z["mT_ready"], c)
                if c == 3:
                    pe.wait_ge(Z["x1_ready"], 1)
                for i in range(TB):
                    ins = turn(bank[0:HH, 7, i * P:(i + 1) * P], smax[:, c * TB + i, :])
                ins.then_inc(Z["mT_psum"], 1)

            def scores(c, i):
                n = c * NBLK + i
                if n >= 2:
                    pe.wait_ge(Z["exp_done"], n - 1)
                if i == 0:
                    pe.wait_ge(Z["qhi_ready"], 2 * c + 2)
                    pe.wait_ge(Z["mT_ready"], c + 1)
                    pe.wait_ge(Z["expanded"], 2 * c + 1)
                    if c == 0:
                        pe.wait_ge(Z["kb_ind"], 2)
                        pe.wait_ge(Z["pad_zero"], 2)
                cols = slice(i * P, (i + 1) * P)
                pe.matmul(bank[:, 3 + n % 2, :], ka[:, c % 2, cols], qa[:, c % 2, :], start=True, stop=False)
                pe.matmul(bank[:, 3 + n % 2, :], kb[0:HW + HH, c % 2, cols], qb[0:HW + HH, c % 2, :],
                          start=False, stop=True).then_inc(Z["score_psum"], 1)

            def attend(c, i):
                b, g, n = c // 2, c % 2, c * NBLK + i
                if i == 0:
                    pe.wait_ge(Z["vaug_ready"], 2 * (b + 1))
                    pe.wait_ge(Z["ones_ready"], 2 * (b + 1))
                    if c:
                        pe.wait_ge(Z["osb_ready"], c)
                pe.wait_ge(Z["exp_done"], n + 1)
                ins = pe.matmul(bank[:, 5, :], vaug[:, b, g, i, :], pT[:, n % 3, :], start=(i == 0),
                                stop=(i == NBLK - 1))
                ins.then_inc(Z["o_psum"] if i == NBLK - 1 else Z["pv_done"], 1)

            def project(b):
                pe.wait_ge(Z["mT_ready"], 3 + b)
                for i in range(TB):
                    half = b and i >= TB // 2
                    pe.wait_ge(Z["attT_ready"], b + 1 + half)
                    ins = pe.matmul(bank[:, 4 if half else 7, i * P:(i + 1) * P], attT[:, i * P:(i + 1) * P],
                                    watt[:, 5, :], start=True, stop=True)
                    if i == TB - 1 or (b and i == TB // 2 - 1):
                        ins.then_inc(Z["proj_psum"], 1)

            def gate_turn(b):
                for i in range(TB):
                    pe.wait_ge(Z["x1_ready"], 1 if b == 0 else 2 + 2 * i // TB)
                    ins = turn(bank[:, b, i * P:(i + 1) * P], x1[:, b * TB + i, :])
                ins.then_inc(Z["x1T_psum"], 1)

            def logits(b):
                pe.wait_ge(L["gate"], 16)
                pe.wait_ge(Z["x1T_ready"], b + 1)
                for i in range(TB):
                    t = b * TB + i
                    ins = pe.matmul(bank[:, (2, 6)[b], i * E0:(i + 1) * E0], xnT[:, t * P:(t + 1) * P], gate[:, :],
                                    start=True, stop=True)
                ins.then_inc(Z["logit_psum"], 1)

            def score_rows(b):
                pe.wait_ge(Z["screp_ready"], b + 1)
                for i in range(TB):
                    ins = turn(bank[:, 3 + b, i * P:(i + 1) * P], screp[:, b * TB + i].rearrange("p e j -> p (e j)"))
                ins.then_inc(Z["srep_psum"], 1)

            turned(0)
            queries(0)
            pe.wait_ge(Z["consts_ready"], 1)
            pe.wait_ge(L["gate"], 16)
            pe.matmul(bank[:, 7, 0:E0], neghalf[:, 0:1].broadcast_to([P, P]), gate[:, :], start=True, stop=True)\
                .then_inc(Z["gsum_psum"], 1)
            rough(0, 0)
            for r in range(3):
                rough(0, r + 1)
                values(0, r)
            maxima(0)
            scores(0, 0)
            queries(1)
            for c in range(COMBOS):
                for i in range(NBLK):
                    if c * NBLK + i + 1 < COMBOS * NBLK:
                        scores(c + (i + 1) // NBLK, (i + 1) % NBLK)
                    if c + 1 < COMBOS:
                        if i in ROUGH_AT:
                            rough(c + 1, ROUGH_AT.index(i))
                    if c == 0 and i == 8:
                        turned(1)
                    if c == 1 and i in (2, 4, 6):
                        values(1, i // 2 - 1)
                    if c == 2 and i == 7:
                        project(0)
                    if c == 3 and i == 2:
                        gate_turn(0)
                    if c == 3 and i == 4:
                        logits(0)
                    if c + 1 < COMBOS and i == 8:
                        maxima(c + 1)
                    if c + 2 < COMBOS and i == NBLK - 1:
                        queries(c + 2)
                    attend(c, i)
            score_rows(0)
            project(1)
            gate_turn(1)
            logits(1)
            score_rows(1)
            pe.wait_ge(L["wout"], 16)
            for b in range(B):
                pe.matmul(bank[:, 0, b * D:(b + 1) * D], ctx2[:, b, 0:P], wout[:, 0, :], start=True, stop=True)
                ins = pe.matmul(bank[0:SK - P, 0, (B + b) * D:(B + b + 1) * D], ctx2[:, b, P:SK], wout[:, 0, :],
                                start=True, stop=True)
            ins.then_inc(Z["cw_psum"], 1)
            pe.wait_ge(Z["consts_ready"], 5)
            pe.wait_ge(Z["x1_ready"], 3)
            for k in range(len(SHIFTS)):
                pe.wait_ge(Z["ok_ready"], k + 1)
                if 1 <= k <= EXACT:
                    pe.wait_ge(Z["cand_ready"], k)
                elif k:
                    pe.wait_ge(Z["delta_ready"], 2 * (k - EXACT))
                pe.matmul(bank[:, 7, 0:1], groupb[:, :], okb[:, :], start=True, stop=True).then_inc(Z["nok_psum"], 1)
            pe.wait_ge(Z["prefix_ready"], len(SHIFTS) - EXACT + 1)
            turn(bank[:, 6, 0:P], prefix[:, :].bitcast(F32).broadcast_to([P, P])).then_inc(Z["thr_psum"], 1)
            pe.wait_ge(Z["gteq_ready"], 2)
            pv = bank[:, 6, 0:2 * T * E0].rearrange("p (k t e) -> p k t e", k=2, t=T)
            pe.matmul(bank[:, 6, 0:2 * T * E0], trib[:, :], gteq[:, :, :, :].rearrange("p k t e -> p (k t e)"),
                      start=True, stop=False)
            for t in range(T - 1):
                n = T - 1 - t
                for k in range(2):
                    pe.matmul(pv[:, k, t + 1:, :], onesb[:, :], gteq[:, k, t, None, :].broadcast_to([P, n, E0]),
                              start=False, stop=(t == T - 2 and k == 1))
            for t in range(T):
                ins = pe.matmul(bank[:, 7, 0:E0], onesb[:, :], gteq[:, 0, t, :], start=(t == 0), stop=(t == T - 1))
            ins.then_inc(Z["pre_psum"], 1)

            pe.wait_ge(L["fc1"], 16)
            pe.wait_ge(L["fc2"], 16)
            pe.wait_ge(L["rows"], 16)
            pe.wait_ge(Z["slot_ready"], 1)
            for b in range(B):
                for i in range(TB):
                    ins = turn(bank[0:E0, 6 + b, i * P:(i + 1) * P], slot[:, b * TB + i, :])
                ins.then_inc(Z["slotT_psum"], 1)
            pe.wait_ge(Z["ylo_ready"], 1)
            pe.wait_ge(Z["sclo_ready"], 1)

            def gather(g, t0, t1):
                n = E0 // 2
                if g and t0 == 0 and t1:
                    pe.wait_ge(Z["ygT_ready"], g)
                for t in range(t0, t1):
                    pe.wait_ge(Z["pick_ready"], T * g + t + 1)
                    to = pick[:, t, g * n:(g + 1) * n, :].rearrange("p e s -> p (e s)")
                    pe.matmul(bank[:, 0, :], yhi[:, t, :], to, start=(t == 0), stop=False)
                    ins = pe.matmul(bank[:, 0, :], ylo[:, t, :], to, start=False, stop=(t == T - 1))
                    if t == T - 1:
                        ins.then_inc(Z["gath_psum"], 1)

            def gather_scores(g):
                n = E0 // 2
                if g:
                    pe.wait_ge(Z["w_ready"], g)
                for t in range(T):
                    ins = pe.matmul(bank[0:2 * E0, 1, :], schl[:, t, :],
                                    pick[:, t, g * n:(g + 1) * n, :].rearrange("p e s -> p (e s)"),
                                    start=(t == 0), stop=(t == T - 1))
                ins.then_inc(Z["wrow_psum"], 1)

            def slot_scores(g):
                n = E0 // 2
                pe.wait_ge(Z["wrow_ready"], g + 1)
                for j in range(n):
                    e = g * n + j
                    ins = pe.matmul(bank[:, 1, j:j + 1], wrow[:, e * P:(e + 1) * P],
                                    const("esel")[0:2 * E0, e:e + 1], start=True, stop=True)
                ins.then_inc(Z["w_psum"], 1)

            def slots_of(e, b):
                pe.wait_ge(Z["slotT_ready"], b + 1)
                pe.wait_ge(Z["esel_ready"], 1)
                if e or b:
                    pe.wait_ge(Z["pickT_ready"], 2 * e + b)
                pe.matmul(bank[:, 5, :], esel[:, e * P:(e + 1) * P], slotT[:, b * S:(b + 1) * S],
                          start=True, stop=True).then_inc(Z["slotb_psum"], 1)

            def first_layer(e):
                pe.wait_ge(Z["ygT_ready"], 1 + 2 * e // E0)
                if e >= 2:
                    pe.wait_ge(Z["hid_ready"], FT * (e - 1))
                for f in range(FT):
                    ins = pe.matmul(bank[:, 2 + e % 2, f * P:(f + 1) * P], fc1[:, e, f * P:(f + 1) * P],
                                    ygT[:, e * P:(e + 1) * P], start=True, stop=True)
                ins.then_inc(Z["fc1_psum"], 1)

            def second_layer(e):
                pe.wait_ge(Z["hid_ready"], FT * (e + 1))
                if e:
                    pe.wait_ge(Z["olo_ready"], e)
                pe.matmul(bank[:, 4, 0:D], onesrow[:, :], rows[0:1, e * D:(e + 1) * D], start=True, stop=False)
                for f in range(FT):
                    ins = pe.matmul(bank[:, 4, 0:D], hid[:, e % 2, f, :], fc2[:, e, f, :], start=False,
                                    stop=(f == FT - 1))
                ins.then_inc(Z["fc2_psum"], 1)

            def scatter(e):
                pe.wait_ge(Z["olo_ready"], e + 1)
                pe.wait_ge(Z["pickT_ready"], 2 * (e + 1))
                for b in range(B):
                    cs = slice(b * S, (b + 1) * S)
                    pe.matmul(bank[:, 6 + b, :], ohi[:, e, :], pickT[:, e, cs], start=(e == 0), stop=False)
                    ins = pe.matmul(bank[:, 6 + b, :], olo[:, e, :], pickT[:, e, cs], start=False, stop=(e == E0 - 1))
                    if e == E0 - 1:
                        ins.then_inc(Z["scat_psum"], 1)

            gather(0, 0, T)
            for e in range(E0 + 2):
                if e < E0:
                    slots_of(e, 0)
                    first_layer(e)
                    slots_of(e, 1)
                if e >= 2:
                    scatter(e - 2)
                if e == 0:
                    gather_scores(0)
                if e in (1, E0 // 2):
                    slot_scores(2 * e // E0)
                if 1 <= e <= E0:
                    second_layer(e - 1)
                gather(1, *SECOND_PICKS.get(e - 1, (0, 0)))
                if e == E0 // 2 - 1:
                    gather_scores(1)
            for b in range(B):
                pe.wait_ge(Z["scT_ready"], b + 1)
                for i in range(TB):
                    ins = turn(bank[:, b, i * P:(i + 1) * P], xnT[:, (b * TB + i) * P:(b * TB + i + 1) * P])
                ins.then_inc(Z["back_psum"], 1)

            pe.wait_ge(L["wr"], 16)
            tile = lambda b, i: slice((b * TB + i) * P, (b * TB + i + 1) * P)
            for b in range(B):
                for i in range(TB):
                    pe.wait_ge(Z["y2_ready" if b else "y2a_ready"], i + 1)
                    ins = turn(bank[:, 6 + b, i * P:(i + 1) * P], xn[:, b * TB + i, :])
                ins.then_inc(Z["y2T_psum"], 1)
            for b in range(B):
                pe.wait_ge(Z["y2T_ready"], b + 1)
                for i in range(TB):
                    d = bank[:, 2 + 2 * b, i * SK:(i + 1) * SK] if i < 3 else bank[:, 3 + 2 * b, 0:SK]
                    ins = pe.matmul(d, xnT[:, tile(b, i)], ctx2[:, b, 0:SK], start=True, stop=True)
                ins.then_inc(Z["s1_psum"], 1)
            for b in range(B):
                for i in range(TB):
                    ins = pe.matmul(bank[:, 6 + b, i * P:(i + 1) * P], xnT[:, tile(b, i)], wout[:, 1, :],
                                    start=True, stop=True)
                ins.then_inc(Z["r1_psum"], 1)
            for b in range(B):
                for i in range(TB):
                    pe.wait_ge(Z["p1_ready"], TB * b + i + 1)
                    turn(bank[:, b, i * P:(i + 1) * P], sm[:, b * TB + i, 0:P])
                    ins = turn(bank[0:SK - P, 3 + 2 * b, i * P:(i + 1) * P], sm[:, b * TB + i, P:SK])
                ins.then_inc(Z["p1T_psum"], 1)
            pe.wait_ge(Z["cw_ready"], 1)
            for b in range(B):
                pe.wait_ge(Z["p1T_ready"], 2 * (b + 1))
                for i in range(TB):
                    d = bank[:, 2 + 2 * b, i * P:(i + 1) * P]
                    pe.matmul(d, pTa[:, b, i * P:(i + 1) * P], cwa[:, b, :], start=True, stop=False)
                    ins = pe.matmul(d, pTb[:, b, i * P:(i + 1) * P], cwb[:, b, :], start=False, stop=True)
                ins.then_inc(Z["o1_psum"], 1)
            for b in range(B):
                for i in range(TB):
                    pe.wait_ge(Z["y3_ready" if b else "y3a_ready"], i + 1)
                    ins = turn(bank[:, b, i * P:(i + 1) * P], y0[:, b * TB + i, :])
                ins.then_inc(Z["y3T_psum"], 1)
            for b in range(B):
                d = bank[:, 3 + 2 * b, 0:TB * E1]
                pe.matmul(d, onesrow[:, :], br_row[:, None, :].broadcast_to([1, TB, E1]), start=True, stop=False)
                pe.wait_ge(Z["y3T_ready"], b + 1)
                for i in range(TB):
                    ins = pe.matmul(d[:, i * E1:(i + 1) * E1], xnT[:, tile(b, i)], wr[:, :], start=False, stop=(i == TB - 1))
                ins.then_inc(Z["lr_psum"], 1)
            def gate_and_up(c, u):
                cs = slice(c * S, (c + 1) * S)
                for j in range(2):
                    w = slice(j * P, (j + 1) * P)
                    d = bank[:, 2 * j + c, :]
                    pe.matmul(d, whi[:, u, w], y3hi[:, cs], start=True, stop=False)
                    pe.matmul(d, whi[:, u, w], y3lo[:, cs], start=False, stop=False)
                    ins = pe.matmul(d, wlo[:, u, w], y3hi[:, cs], start=False, stop=True)
                    if j == 0:
                        ins.then_inc(Z["gate_psum"], 1)

            def router_weights(c, u):
                pe.matmul(bank[:, 4 + c, :], whi[0:3 * E1, u, 3 * P:GW], w3[:, c * S:(c + 1) * S],
                          start=True, stop=True).then_inc(Z["upw_psum"], 1)

            pe.wait_ge(Z["split_ready"], 1)
            pe.wait_ge(Z["y3lo_ready"], 1)
            gate_and_up(0, 0)
            for b in range(B):
                pe.wait_ge(Z["wsel_ready"], b + 1)
                for i in range(TB):
                    ins = turn(bank[0:E1, 6 + b, i * P:(i + 1) * P], wsel[:, b * TB + i, :])
                ins.then_inc(Z["wT_psum"], 1)
            pe.wait_ge(Z["w3ones_ready"], 1)
            pe.wait_ge(Z["bdlo_ready"], 1)
            for b in range(B):
                cs = slice(b * S, (b + 1) * S)
                if b:
                    pe.wait_ge(Z["y3lo_ready"], 2)
                    gate_and_up(1, 0)
                pe.wait_ge(Z["w3_ready"], b + 1)
                router_weights(b, 0)
                pe.matmul(bank[:, 6 + b, :], bdhi[:, :], w3[0:2 * E1, cs], start=True, stop=False,
                          skip_group_check=True)
                pe.matmul(bank[:, 6 + b, :], bdlo[:, :], w3[0:E1, cs], start=False, stop=False,
                          skip_group_check=True)

            def down(k, c, u, last=False):
                pe.wait_ge(Z["hhi_ready"], k + 1)
                w = slice(2 * P, 3 * P)
                d = bank[:, 6 + c, :]
                pe.matmul(d, whi[:, u, w], hhi[:, c, :], start=False, stop=False, skip_group_check=True)
                pe.matmul(d, wlo[:, u, w], hhi[:, c, :], start=False, stop=False, skip_group_check=True)
                pe.wait_ge(Z["hlo_ready"], k + 1)
                ins = pe.matmul(d, whi[:, u, w], hlo[:, c, :], start=False, stop=last, skip_group_check=True)
                ins.then_inc(Z["y_psum"] if last else Z["down_done"], 1)

            with pe.Fori(0, LOOPS) as m:
                for u in range(3):
                    for c in range(2):
                        k = m * 6 + (2 * u + 2 + c)
                        if c == 0:
                            pe.wait_ge(Z["split_ready"], m * 3 + (u + 2))
                        pe.wait_ge(Z["hh_ready"], k - 1)
                        gate_and_up(c, (u + 1) % 3)
                        router_weights(c, (u + 1) % 3)
                        down(k - 2, c, u)
            u = (PAIRS - 1) % 3
            pe.wait_ge(Z["split_ready"], PAIRS)
            for c in range(2):
                pe.wait_ge(Z["hh_ready"], 2 * PAIRS - 3 + c)
                gate_and_up(c, u)
                router_weights(c, u)
                down(2 * PAIRS - 4 + c, c, (u + 2) % 3)
            down(2 * PAIRS - 2, 0, u)
            down(2 * PAIRS - 1, 1, u, last=True)
            for b in range(B):
                pe.wait_ge(Z["yT_ready"], b + 1)
                for i in range(TB):
                    c = (b * TB + i) * P
                    ins = turn(bank[:, b, i * P:(i + 1) * P], yT[:, c:c + P])
                ins.then_inc(Z["outT_psum"], 1)


def constants():
    p = np.arange(P)
    c = {"ident": np.eye(P)}
    c["headmask"] = (p[:, None] % (HH * DH) // DH == np.arange(HH)).astype(np.float32)
    pair = P * np.arange(NBLK)[None, :, None] + p[:, None, None]
    c["vmask"] = (pair // SK == np.arange(HH)).astype(np.float32).reshape(P, NBLK * HH)
    c["tri"] = (p[:, None] < p[None, :]).astype(np.float32)
    c["group"] = (p[:, None] // 16 == p[None, :] // 16).astype(np.float32)
    c["esel"] = (p[:, None] % E0 == np.arange(E0)).astype(np.float32)
    c["row"] = p[:, None]
    c["iota"] = np.broadcast_to(p[None, :], (P, P))
    j = (p % 16).astype(np.float64)
    jf = np.zeros((P, len(SHIFTS)))
    for k in range(len(SHIFTS) - 1):
        jf[:, k] = j * 2.0 ** SHIFTS[k + 1] - 2.0 ** SHIFTS[k]
    c["jf"] = jf
    jg = np.zeros((P, EXACT + 1))
    for k in range(1, EXACT + 1):
        jg[:, k] = -j * 2.0 ** SHIFTS[k] + (jf[:, k] if k < EXACT else 0)
    c["jg"] = jg
    c["cand0"] = (np.minimum(p % 16, 4).astype(np.int64) << SHIFTS[0]).astype(np.int32).view(np.float32)[:, None]
    sel = np.zeros((PAIRS, P, P), np.float32)
    sel[0, 2 * E1, 0:I1] = 1
    for q in range(1, PAIRS):
        for h in range(2):
            e = 2 * (q - 1) + h
            sel[q, e, h * I1:(h + 1) * I1] = 1
            sel[q, E1 + e, h * I1:(h + 1) * I1] = 1
    return {k: np.ascontiguousarray(v, dtype=np.float32) for k, v in c.items()}, sel


def kernel(**inputs):
    import concourse.bacc as bacc
    from concourse.bass_utils import run_bass_kernel_spmd as run

    i = {k: np.asarray(v) for k, v in inputs.items()}
    consts, sel = constants()
    col = lambda v: v.reshape(-1, 1)
    ctx = i["ctx_1024"]
    ctxT = ctx.transpose(2, 0, 1)
    twice = lambda v, g: np.concatenate([v[g * HW:(g + 1) * HW]] * 2)
    ind = (np.arange(NBLK * P)[None, :] // SK == np.arange(HH)[:, None]).astype(np.float32)
    vectors = {"bq": np.stack([twice(i["L0_xattn_bq"], g) for g in range(2)], axis=1),
               "bk": np.stack([twice(i["L0_xattn_bk"], g) for g in range(2)], axis=1),
               "bo": np.broadcast_to(i["L0_xattn_bo"], (P, D)), "bv": col(i["L0_xattn_bv"]),
               "ln_w": col(i["L0_ffn_ln_w"]), "ln_b": col(i["L0_ffn_ln_b"]), "bd_s": col(i["L1_ffn_bd_s"]),
               "b1": i["L0_ffn_b1s"].reshape(E0, FT, P).transpose(2, 0, 1).reshape(P, E0 * FT)}
    parts = {**consts, **vectors}
    rec = np.zeros((PAIRS, P, REC), np.float32)
    rec[:, :, 3 * P:GW] = sel
    rec[0, :, 0:I1] = i["L1_ffn_Wg_s"]
    rec[0, :, P:P + I1] = i["L1_ffn_Wu_s"]
    rec[0, 0:I1, 2 * P:3 * P] = i["L1_ffn_Wd_s"]
    rec[0, 0:I1, GW] = i["L1_ffn_bg_s"]
    rec[0, 0:I1, GW + 1] = i["L1_ffn_bu_s"]
    n = PAIRS - 1
    rec[1:, :, 0:P] = i["L1_ffn_Wg"].reshape(n, 2, D, I1).transpose(0, 2, 1, 3).reshape(n, D, P)
    rec[1:, :, P:2 * P] = i["L1_ffn_Wu"].reshape(n, 2, D, I1).transpose(0, 2, 1, 3).reshape(n, D, P)
    rec[1:, :, 2 * P:3 * P] = i["L1_ffn_Wd"].reshape(n, P, D)
    rec[1:, :, GW] = i["L1_ffn_bg"].reshape(n, P)
    rec[1:, :, GW + 1] = i["L1_ffn_bu"].reshape(n, P)
    arrays = {
        "x": i["x"].reshape(T, P, D).transpose(1, 0, 2),
        "ctx2": np.concatenate([ctxT, ctxT], axis=2),
        "mask": i["mask_BxSxS2_bk0"].reshape(T, P, SK).transpose(1, 0, 2),
        "watt": np.stack([twice(i["L0_xattn_W" + n], g).T for n in "qk" for g in range(2)]
                         + [i["L0_xattn_Wv"].T, i["L0_xattn_Wo"].T], axis=1),
        "ind": ind,
        "pack": np.concatenate([parts[n] for n in PACK], axis=1),
        "rows": np.concatenate([i["L0_ffn_b2s"].reshape(-1), i["L1_ffn_br"]])[None, :],
        "gate": i["L0_ffn_gate_w"].T,
        "fc1": i["L0_ffn_fc1s"].transpose(2, 0, 1),
        "fc2": i["L0_ffn_fc2s"].reshape(E0, D, FT, P).transpose(3, 0, 2, 1),
        "wout": i["L1_xattn_W_attn"].reshape(D, 2, D).transpose(2, 1, 0),
        "wr": i["L1_ffn_Wr"],
        "rec": rec,
        "bd": np.concatenate([i["L1_ffn_bd"]] * 2),
    }
    nc = bacc.Bacc("TRN2", target_bir_lowering=False, num_devices=1)
    arrays = {f"in_{k}": np.ascontiguousarray(v) for k, v in arrays.items()}
    args = [nc.dram_tensor(k, v.shape, mybir.dt.from_np(v.dtype), kind="ExternalInput").ap()
            for k, v in arrays.items()]
    out = nc.dram_tensor("out_0", (P, T, D), F32, kind="ExternalOutput").ap()
    build(nc, *args, out)
    r = run(nc, [arrays], core_ids=[0])
    return r.results[0]["out_0"].transpose(1, 0, 2).reshape(B, S, D)
```
